# Optimizing a Trainium2 kernel written in Bass

```python
import numpy as np
import jax
import jax.numpy as jnp

def _softmax(x, axis=-1):
    return jax.nn.softmax(x, axis=axis)

def _gelu(x):
    return jax.nn.gelu(x, approximate=True)

def _silu(x):
    return jax.nn.silu(x)

def _sigmoid(x):
    return jax.nn.sigmoid(x)

def _layernorm(x, axis=-1, eps=1e-05):
    m = jnp.mean(x, axis=axis, keepdims=True)
    v = jnp.var(x, axis=axis, keepdims=True)
    return (x - m) / jnp.sqrt(v + eps)

def _scatter_add(tgt, idx, src, axis=0):
    return tgt.at[idx].add(src)

def _segment_sum(src, seg, n):
    return jax.ops.segment_sum(src, seg, n)
kernel_name = 'mk_gnn_resnorm_d4_gnn_r32_c3b5d9'

def setup_inputs(seed: int=0):
    np.random.seed(seed)
    _w = jnp.asarray

    def _rec_inputs():
        import jax
        import jax.numpy as jnp
        _gk = jax.random.key(seed)
        x = -0.0002117 + 1 * jax.random.normal(jax.random.fold_in(_gk, 1), (50000, 256), jnp.float32)
        src = jax.random.randint(jax.random.fold_in(_gk, 2), (25000,), 0, 50000, jnp.int32)
        dst = jnp.minimum((50000 * jax.random.uniform(jax.random.fold_in(_gk, 3), (25000,)) ** 2.0).astype(jnp.int32), 49999)
        _o = jnp.argsort(dst, stable=True)
        src = src[_o]
        dst = dst[_o]
        edge_attr_64 = -9.77346e-05 + 0.999888 * jax.random.normal(jax.random.fold_in(_gk, 12), (25000, 64), jnp.float32)
        edge_weight = jax.random.uniform(jax.random.fold_in(_gk, 14), (25000,), jnp.float32, 0.0, 0.999999)
        return (x, src, dst, edge_attr_64, edge_weight)
    x, src, dst, edge_attr_64, edge_weight = _rec_inputs()

    def _L0_gnn_setup():
        import jax, jax.numpy as jnp
        import numpy as np
        N_NODES = 3125
        N_EDGES = 50000
        D = 256
        key = jax.random.key(seed)
        ks = jax.random.split(key, 8)
        h6_all = jax.random.normal(ks[0], (N_NODES, D), dtype=jnp.float32)
        edge_index = jax.random.randint(ks[1], (2, N_EDGES), 0, N_NODES, dtype=jnp.int64)
        edge_weight = jax.random.uniform(ks[2], (N_EDGES,), dtype=jnp.float32)
        s = 1.0 / np.sqrt(D)
        W = jax.random.normal(ks[3], (D, D), dtype=jnp.float32) * s
        b = jnp.zeros((D,), dtype=jnp.float32)
        W1 = jax.random.normal(ks[4], (D, D), dtype=jnp.float32) * s
        b1 = jnp.zeros((D,), dtype=jnp.float32)
        W2 = jax.random.normal(ks[5], (D, D), dtype=jnp.float32) * s
        b2 = jnp.zeros((D,), dtype=jnp.float32)
        return {'h6_all': h6_all, 'edge_index': edge_index, 'edge_weight': edge_weight, 'W': W, 'b': b, 'W1': W1, 'b1': b1, 'W2': W2, 'b2': b2}
    _L0_gnn_all = _L0_gnn_setup()
    _L0_gnn_in = {k: v for k, v in _L0_gnn_all.items() if k in ('W', 'b', 'W1', 'b1', 'W2', 'b2')}
    del _L0_gnn_all

    def _L1_gnn_setup():
        import jax, jax.numpy as jnp
        import numpy as np
        N_NODES = 50000
        N_EDGES = 25000
        IN_DIM = 256
        E_DIM = 64
        N_HEADS = 8
        OUT_DIM = 32
        NEG_SLOPE = 0.2
        key = jax.random.key(seed)
        ks = jax.random.split(key, 10)
        return {'feat': jax.random.normal(ks[0], (N_NODES, IN_DIM), dtype=jnp.float32), 'edge_attr': jax.random.normal(ks[1], (N_EDGES, E_DIM), dtype=jnp.float32), 'src': jax.random.randint(ks[2], (N_EDGES,), 0, N_NODES, dtype=jnp.int32), 'dst': jax.random.randint(ks[3], (N_EDGES,), 0, N_NODES, dtype=jnp.int32), 'W_fc': jax.random.normal(ks[4], (IN_DIM, N_HEADS * OUT_DIM), dtype=jnp.float32) * (1.0 / np.sqrt(IN_DIM)), 'W_e': jax.random.normal(ks[5], (E_DIM, N_HEADS * OUT_DIM), dtype=jnp.float32) * (1.0 / np.sqrt(E_DIM)), 'attn_h': jax.random.normal(ks[6], (N_HEADS, OUT_DIM), dtype=jnp.float32) * 0.1, 'attn_e': jax.random.normal(ks[7], (N_HEADS, OUT_DIM), dtype=jnp.float32) * 0.1, 'attn_t': jax.random.normal(ks[8], (N_HEADS, OUT_DIM), dtype=jnp.float32) * 0.1, 'bias': jnp.zeros((N_HEADS, OUT_DIM), dtype=jnp.float32)}
    _L1_gnn_all = _L1_gnn_setup()
    _L1_gnn_in = {k: v for k, v in _L1_gnn_all.items() if k in ('W_fc', 'W_e', 'attn_h', 'attn_e', 'attn_t', 'bias')}
    del _L1_gnn_all

    def _L2_gnn_setup():
        import jax, jax.numpy as jnp
        import numpy as np
        N, E = (50000, 25000)
        H, C_IN, C_HID, C_OUT = (4, 256, 64, 64)
        NEG_SLOPE = 0.2

        def leaky_relu(x, s=NEG_SLOPE):
            return jnp.where(x >= 0, x, s * x)

        def gat_conv(x, src, dst, W, att_src, att_dst, bias, n_nodes):
            Hh, Cc = (att_src.shape[1], att_src.shape[2])
            h = (x @ W).reshape(n_nodes, Hh, Cc)
            a_src = (h * att_src).sum(-1)
            a_dst = (h * att_dst).sum(-1)
            alpha = leaky_relu(a_src[src] + a_dst[dst])
            m = jax.ops.segment_max(alpha, dst, num_segments=n_nodes)
            e = jnp.exp(alpha - m[dst])
            denom = jax.ops.segment_sum(e, dst, num_segments=n_nodes)
            w = e / jnp.clip(denom, 1e-16)[dst]
            out = jax.ops.segment_sum(w[:, :, None] * h[src], dst, num_segments=n_nodes)
            return out.reshape(n_nodes, Hh * Cc) + bias
        key = jax.random.key(seed)
        ks = jax.random.split(key, 10)
        glorot = lambda k, shp: jax.random.normal(k, shp, jnp.float32) * np.sqrt(2.0 / (shp[0] + shp[-1]))
        return {'x': jax.random.normal(ks[0], (N, C_IN), jnp.float32), 'edge_index': jax.random.randint(ks[1], (2, E), 0, N, jnp.int32), 'W1': glorot(ks[2], (C_IN, H * C_HID)), 'att_src1': glorot(ks[3], (1, H, C_HID)), 'att_dst1': glorot(ks[4], (1, H, C_HID)), 'b1': jnp.zeros((H * C_HID,), jnp.float32), 'W2': glorot(ks[5], (H * C_HID, H * C_OUT)), 'att_src2': glorot(ks[6], (1, H, C_OUT)), 'att_dst2': glorot(ks[7], (1, H, C_OUT)), 'b2': jnp.zeros((H * C_OUT,), jnp.float32)}
    _L2_gnn_all = _L2_gnn_setup()
    _L2_gnn_in = {k: v for k, v in _L2_gnn_all.items() if k in ('W1', 'att_src1', 'att_dst1', 'b1', 'W2', 'att_src2', 'att_dst2', 'b2')}
    del _L2_gnn_all

    def _L3_gnn_setup():
        import jax, jax.numpy as jnp
        import numpy as np
        N_NODES = 18870
        N_EDGES = 37500
        DIM = 256
        EPS = 1e-05

        def _layer_norm(x, g, b):
            mu = jnp.mean(x, axis=-1, keepdims=True)
            var = jnp.mean(jnp.square(x - mu), axis=-1, keepdims=True)
            return (x - mu) * jax.lax.rsqrt(var + EPS) * g + b

        def _gcn_conv(x, edge_index, edge_weight, W, b):
            n = x.shape[0]
            row, col = (edge_index[0], edge_index[1])
            loop = jnp.arange(n, dtype=row.dtype)
            row = jnp.concatenate([row, loop])
            col = jnp.concatenate([col, loop])
            ew = jnp.concatenate([edge_weight, jnp.ones((n,), dtype=x.dtype)])
            deg = jax.ops.segment_sum(ew, col, num_segments=n)
            dis = jnp.where(deg > 0, jax.lax.rsqrt(jnp.where(deg > 0, deg, 1.0)), 0.0)
            norm = dis[row] * ew * dis[col]
            h = x @ W.T
            msg = h[row] * norm[:, None]
            out = jax.ops.segment_sum(msg, col, num_segments=n)
            return out + b

        def _block(x, edge_index, edge_weight, g, bln, W, b):
            h = _layer_norm(x, g, bln)
            h = _gcn_conv(h, edge_index, edge_weight, W, b)
            h = jax.nn.relu(h)
            return x + h
        key = jax.random.key(seed)
        ks = jax.random.split(key, 8)
        s = 0.05
        return {'x': jax.random.normal(ks[0], (N_NODES, DIM), dtype=jnp.float32), 'edge_index': jax.random.randint(ks[1], (2, N_EDGES), 0, N_NODES, dtype=jnp.int64) if jax.config.jax_enable_x64 else jax.random.randint(ks[1], (2, N_EDGES), 0, N_NODES).astype(jnp.int32), 'edge_weight': jax.random.uniform(ks[2], (N_EDGES,), dtype=jnp.float32), 'ln6_g': jnp.ones((DIM,), jnp.float32), 'ln6_b': jnp.zeros((DIM,), jnp.float32), 'W6': jax.random.normal(ks[3], (DIM, DIM), jnp.float32) * s, 'b6': jnp.zeros((DIM,), jnp.float32), 'ln7_g': jnp.ones((DIM,), jnp.float32), 'ln7_b': jnp.zeros((DIM,), jnp.float32), 'W7': jax.random.normal(ks[4], (DIM, DIM), jnp.float32) * s, 'b7': jnp.zeros((DIM,), jnp.float32), 'Wp': jax.random.normal(ks[5], (DIM, DIM), jnp.float32) * s, 'bp': jnp.zeros((DIM,), jnp.float32)}
    _L3_gnn_all = _L3_gnn_setup()
    _L3_gnn_in = {k: v for k, v in _L3_gnn_all.items() if k in ('ln6_g', 'ln6_b', 'W6', 'b6', 'ln7_g', 'ln7_b', 'W7', 'b7', 'Wp', 'bp')}
    del _L3_gnn_all
    return {'x': x, 'src': src, 'dst': dst, 'edge_attr_64': edge_attr_64, 'edge_weight': edge_weight, 'L0_gnn_W': _L0_gnn_in['W'], 'L0_gnn_b': _L0_gnn_in['b'], 'L0_gnn_W1': _L0_gnn_in['W1'], 'L0_gnn_b1': _L0_gnn_in['b1'], 'L0_gnn_W2': _L0_gnn_in['W2'], 'L0_gnn_b2': _L0_gnn_in['b2'], 'L1_gnn_W_fc': _L1_gnn_in['W_fc'], 'L1_gnn_W_e': _L1_gnn_in['W_e'], 'L1_gnn_attn_h': _L1_gnn_in['attn_h'], 'L1_gnn_attn_e': _L1_gnn_in['attn_e'], 'L1_gnn_attn_t': _L1_gnn_in['attn_t'], 'L1_gnn_bias': _L1_gnn_in['bias'], 'L2_gnn_W1': _L2_gnn_in['W1'], 'L2_gnn_att_src1': _L2_gnn_in['att_src1'], 'L2_gnn_att_dst1': _L2_gnn_in['att_dst1'], 'L2_gnn_b1': _L2_gnn_in['b1'], 'L2_gnn_W2': _L2_gnn_in['W2'], 'L2_gnn_att_src2': _L2_gnn_in['att_src2'], 'L2_gnn_att_dst2': _L2_gnn_in['att_dst2'], 'L2_gnn_b2': _L2_gnn_in['b2'], 'L3_gnn_ln6_g': _L3_gnn_in['ln6_g'], 'L3_gnn_ln6_b': _L3_gnn_in['ln6_b'], 'L3_gnn_W6': _L3_gnn_in['W6'], 'L3_gnn_b6': _L3_gnn_in['b6'], 'L3_gnn_ln7_g': _L3_gnn_in['ln7_g'], 'L3_gnn_ln7_b': _L3_gnn_in['ln7_b'], 'L3_gnn_W7': _L3_gnn_in['W7'], 'L3_gnn_b7': _L3_gnn_in['b7'], 'L3_gnn_Wp': _L3_gnn_in['Wp'], 'L3_gnn_bp': _L3_gnn_in['bp']}

def reference(x, src, dst, edge_attr_64, edge_weight, L0_gnn_W, L0_gnn_b, L0_gnn_W1, L0_gnn_b1, L0_gnn_W2, L0_gnn_b2, L1_gnn_W_fc, L1_gnn_W_e, L1_gnn_attn_h, L1_gnn_attn_e, L1_gnn_attn_t, L1_gnn_bias, L2_gnn_W1, L2_gnn_att_src1, L2_gnn_att_dst1, L2_gnn_b1, L2_gnn_W2, L2_gnn_att_src2, L2_gnn_att_dst2, L2_gnn_b2, L3_gnn_ln6_g, L3_gnn_ln6_b, L3_gnn_W6, L3_gnn_b6, L3_gnn_ln7_g, L3_gnn_ln7_b, L3_gnn_W7, L3_gnn_b7, L3_gnn_Wp, L3_gnn_bp):
    import jax
    import jax.numpy as jnp

    def _L0_gnn_ref(h6_all, edge_index, edge_weight, W, b, W1, b1, W2, b2):
        import jax, jax.numpy as jnp
        import numpy as np
        N_NODES = 3125
        N_EDGES = 50000
        D = 256
        'GCNConv(256->256, weighted, self-loops, symmetric norm) + 2-layer MLP head.'
        N = h6_all.shape[0]
        row, col = (edge_index[0], edge_index[1])
        sl = jnp.arange(N, dtype=edge_index.dtype)
        row_sl = jnp.concatenate([row, sl])
        col_sl = jnp.concatenate([col, sl])
        ew_sl = jnp.concatenate([edge_weight, jnp.ones((N,), dtype=edge_weight.dtype)])
        deg = jax.ops.segment_sum(ew_sl, row_sl, num_segments=N)
        dinv = jnp.where(deg > 0, jax.lax.rsqrt(deg), 0.0)
        norm = dinv[row_sl] * ew_sl * dinv[col_sl]
        xw = h6_all @ W
        msgs = xw[col_sl] * norm[:, None]
        h7 = jax.ops.segment_sum(msgs, row_sl, num_segments=N) + b
        h = jax.nn.relu(h7 @ W1 + b1)
        out = h @ W2 + b2
        return out

    def _L1_gnn_ref(feat, edge_attr, src, dst, W_fc, W_e, attn_h, attn_e, attn_t, bias):
        import jax, jax.numpy as jnp
        import numpy as np
        N_NODES = 50000
        N_EDGES = 25000
        IN_DIM = 256
        E_DIM = 64
        N_HEADS = 8
        OUT_DIM = 32
        NEG_SLOPE = 0.2
        N = feat.shape[0]
        H, D = attn_h.shape
        ft = (feat @ W_fc).reshape(N, H, D)
        eh = jnp.einsum('nhd,hd->nh', ft, attn_h)
        et = jnp.einsum('nhd,hd->nh', ft, attn_t)
        fe = (edge_attr @ W_e).reshape(-1, H, D)
        ee = jnp.einsum('ehd,hd->eh', fe, attn_e)
        e = jax.nn.leaky_relu(eh[src] + ee + et[dst], negative_slope=NEG_SLOPE)
        e_max = jax.ops.segment_max(e, dst, num_segments=N)
        e_max = jax.lax.stop_gradient(jnp.where(jnp.isfinite(e_max), e_max, 0.0))
        ex = jnp.exp(e - e_max[dst])
        denom = jax.ops.segment_sum(ex, dst, num_segments=N)
        a = ex / denom[dst]
        msg = ft[src] * a[:, :, None]
        rst = jax.ops.segment_sum(msg, dst, num_segments=N)
        rst = rst + bias[None, :, :]
        return rst.reshape(N, H * D)

    def _L2_gnn_ref(x, edge_index, W1, att_src1, att_dst1, b1, W2, att_src2, att_dst2, b2):
        import jax, jax.numpy as jnp
        import numpy as np
        N, E = (50000, 25000)
        H, C_IN, C_HID, C_OUT = (4, 256, 64, 64)
        NEG_SLOPE = 0.2

        def leaky_relu(x, s=NEG_SLOPE):
            return jnp.where(x >= 0, x, s * x)

        def gat_conv(x, src, dst, W, att_src, att_dst, bias, n_nodes):
            Hh, Cc = (att_src.shape[1], att_src.shape[2])
            h = (x @ W).reshape(n_nodes, Hh, Cc)
            a_src = (h * att_src).sum(-1)
            a_dst = (h * att_dst).sum(-1)
            alpha = leaky_relu(a_src[src] + a_dst[dst])
            m = jax.ops.segment_max(alpha, dst, num_segments=n_nodes)
            e = jnp.exp(alpha - m[dst])
            denom = jax.ops.segment_sum(e, dst, num_segments=n_nodes)
            w = e / jnp.clip(denom, 1e-16)[dst]
            out = jax.ops.segment_sum(w[:, :, None] * h[src], dst, num_segments=n_nodes)
            return out.reshape(n_nodes, Hh * Cc) + bias
        n = x.shape[0]
        loops = jnp.arange(n, dtype=edge_index.dtype)
        src = jnp.concatenate([edge_index[0], loops])
        dst = jnp.concatenate([edge_index[1], loops])
        h1 = gat_conv(x, src, dst, W1, att_src1, att_dst1, b1, n)
        h1 = jax.nn.relu(h1)
        out = gat_conv(h1, src, dst, W2, att_src2, att_dst2, b2, n)
        return out

    def _L3_gnn_ref(x, edge_index, edge_weight, ln6_g, ln6_b, W6, b6, ln7_g, ln7_b, W7, b7, Wp, bp):
        import jax, jax.numpy as jnp
        import numpy as np
        N_NODES = 18870
        N_EDGES = 37500
        DIM = 256
        EPS = 1e-05

        def _layer_norm(x, g, b):
            mu = jnp.mean(x, axis=-1, keepdims=True)
            var = jnp.mean(jnp.square(x - mu), axis=-1, keepdims=True)
            return (x - mu) * jax.lax.rsqrt(var + EPS) * g + b

        def _gcn_conv(x, edge_index, edge_weight, W, b):
            n = x.shape[0]
            row, col = (edge_index[0], edge_index[1])
            loop = jnp.arange(n, dtype=row.dtype)
            row = jnp.concatenate([row, loop])
            col = jnp.concatenate([col, loop])
            ew = jnp.concatenate([edge_weight, jnp.ones((n,), dtype=x.dtype)])
            deg = jax.ops.segment_sum(ew, col, num_segments=n)
            dis = jnp.where(deg > 0, jax.lax.rsqrt(jnp.where(deg > 0, deg, 1.0)), 0.0)
            norm = dis[row] * ew * dis[col]
            h = x @ W.T
            msg = h[row] * norm[:, None]
            out = jax.ops.segment_sum(msg, col, num_segments=n)
            return out + b

        def _block(x, edge_index, edge_weight, g, bln, W, b):
            h = _layer_norm(x, g, bln)
            h = _gcn_conv(h, edge_index, edge_weight, W, b)
            h = jax.nn.relu(h)
            return x + h
        x = _block(x, edge_index, edge_weight, ln6_g, ln6_b, W6, b6)
        x = _block(x, edge_index, edge_weight, ln7_g, ln7_b, W7, b7)
        return x @ Wp.T + bp
    edge_index = jnp.stack([src, dst])
    x = _layernorm(x + _L0_gnn_ref(x, edge_index, edge_weight, L0_gnn_W, L0_gnn_b, L0_gnn_W1, L0_gnn_b1, L0_gnn_W2, L0_gnn_b2), axis=-1)
    x = _layernorm(x + _L1_gnn_ref(x, edge_attr_64, src, dst, L1_gnn_W_fc, L1_gnn_W_e, L1_gnn_attn_h, L1_gnn_attn_e, L1_gnn_attn_t, L1_gnn_bias), axis=-1)
    x = _layernorm(x + _L2_gnn_ref(x, edge_index, L2_gnn_W1, L2_gnn_att_src1, L2_gnn_att_dst1, L2_gnn_b1, L2_gnn_W2, L2_gnn_att_src2, L2_gnn_att_dst2, L2_gnn_b2), axis=-1)
    x = _layernorm(x + _L3_gnn_ref(x, edge_index, edge_weight, L3_gnn_ln6_g, L3_gnn_ln6_b, L3_gnn_W6, L3_gnn_b6, L3_gnn_ln7_g, L3_gnn_ln7_b, L3_gnn_W7, L3_gnn_b7, L3_gnn_Wp, L3_gnn_bp), axis=-1)
    return x

_drawn_inputs = setup_inputs


def setup_inputs(seed=0):
    import zlib

    import numpy as np

    out = dict(_drawn_inputs(seed))
    spreads = {'L0_gnn_b': (0.0, 0.1),
     'L0_gnn_b1': (0.0, 0.1),
     'L0_gnn_b2': (0.0, 0.1),
     'L1_gnn_bias': (0.0, 0.1),
     'L2_gnn_b1': (0.0, 0.1),
     'L2_gnn_b2': (0.0, 0.1),
     'L3_gnn_ln6_g': (1.0, 0.2),
     'L3_gnn_ln6_b': (0.0, 0.1),
     'L3_gnn_b6': (0.0, 0.1),
     'L3_gnn_ln7_g': (1.0, 0.2),
     'L3_gnn_ln7_b': (0.0, 0.269),
     'L3_gnn_b7': (0.0, 0.1),
     'L3_gnn_bp': (0.0, 0.1)}
    factors = {'L1_gnn_attn_t': 5.823, 'L2_gnn_att_dst1': 3.155, 'L2_gnn_att_dst2': 6.736}
    for name, (base, spread) in spreads.items():
        noise = np.random.default_rng([zlib.crc32(name.encode()), seed]).standard_normal(out[name].shape)
        drawn = base * np.exp(spread * noise) if base else spread * noise
        out[name] = jnp.asarray(drawn.astype(out[name].dtype))
    for name, factor in factors.items():
        out[name] = (out[name] * factor).astype(out[name].dtype)
    return out
```

```python
from contextlib import ExitStack

import numpy as np

import concourse.bass as bass
from concourse import mybir

F32 = mybir.dt.float32
I32 = mybir.dt.int32
BF16 = mybir.dt.bfloat16
ALU = mybir.AluOpType
ACT = mybir.ActivationFunctionType
AX_X = mybir.AxisListType.X

P = 128
N_NODES, N_EDGES, D = 50000, 25000, 256
NT = 392
NP = P * NT
ET = 196
EP = P * ET
GN, GE = 4, 7
NG, EG = NT // GN, ET // GE
AUX = 8
RW = D + AUX
DEFAULT_ROW = EP
SPARE_ROWS = EP + P
SUM_ROWS = EP + 2 * P
SORT = 32768
SW = SORT // P
LOG = 15
KEY_SHIFT = 15
KEY_BIAS = 256
PAD_KEY = 65023
FAR = 1 << 20
BIG = 1e38
EPS = 1e-5
SLOPE = 0.2
DST, SRC = 0, 1


class Steps:

    def __init__(self, eng, sem, base=0):
        self.eng, self.sem, self.base, self.n = eng, sem, base, 0

    def mark(self, ins):
        ins.then_inc(self.sem, 1)
        self.n += 1

    def then(self, ins):
        self.mark(ins)
        self.ready()

    def ready(self):
        self.eng.wait_ge(self.sem, self.base + self.n)


def in_slots(eng, groups, steps, unroll=2):
    lags = [lag for _, lag in steps]
    first = -(-(max(lags) + 2) // unroll)
    rounds = (groups + min(lags)) // unroll - first

    def slot(k, u):
        for step, lag in steps:
            back, at = divmod(u - lag, unroll)
            if not isinstance(k, int) or 0 <= unroll * (k + back) + at < groups:
                step(k + back, at)

    for tau in range(unroll * first):
        slot(tau // unroll, tau % unroll)
    with eng.Fori(first, first + rounds) as k:
        for u in range(unroll):
            slot(k, u)
    for tau in range(unroll * (first + rounds), groups + max(lags)):
        slot(tau // unroll, tau % unroll)


def reused(turn):
    return not isinstance(turn, int) or turn >= 1


def build(nc, a, out):
    with ExitStack() as whole:
        def dram(name, shape, dt=F32):
            return nc.dram_tensor(name, shape, dt).ap()

        def keep(name, shape, dt=F32):
            return whole.enter_context(nc.sbuf_tensor(name, shape, dt))

        sorted_words = dram("sorted_words", (2, SORT + 2), I32)
        edge_fields = dram("edge_fields", (EP, 16), I32)
        edge_pair = dram("edge_pair", (EP, 4), I32)
        node_tab = [dram(f"node_tab_{o}", (NP, 2), I32) for o in ("d", "s")]
        scores = dram("scores", (NP, AUX))
        sums = dram("sums", (SUM_ROWS, RW))
        ft_edges = dram("ft_edges", (EP, D))
        x1, x2, x3, x4 = (dram(f"x{i}", (NP, D)) for i in (1, 2, 3, 4))
        h2a, h2b, h3a, h3b = (dram(n, (NP, D)) for n in ("h2a", "h2b", "h3a", "h3b"))

        ident = keep("ident", [P, P])
        before = keep("before", [P, P])
        ww1 = keep("ww1", [P, 2, D])
        w2 = keep("w2", [P, 2, D])
        wfc = keep("wfc", [P, 2, RW])
        v_t = keep("v_t", [P, 2, AUX])
        v_e = keep("v_e", [P, 2 * AUX])
        wa = keep("wa", [P, 2, RW])
        wb = keep("wb", [P, 2, RW])
        w6 = keep("w6", [P, 2, D])
        w7 = keep("w7", [P, 2, D])
        wp = keep("wp", [P, 2, D])
        mlp_bias = keep("mlp_bias", [P, 2])
        ones3 = keep("ones3", [3, P], BF16)
        bias3 = {n: keep(f"bias3_{n}", [3, RW], BF16) for n in ("b2", "fc", "a", "b", "c6", "c7", "bp")}
        b6_all = keep("b6_all", [P, D])
        b7_all = keep("b7_all", [P, D])
        eps = keep("eps", [P, 1])

        order = []
        for o in ("d", "s"):
            t = {n: keep(f"{n}_{o}", [P, ET]) for n in ("not_first", "restart", "not_last", "is_last", "weight")}
            t["gather_idx"] = keep(f"gather_idx_{o}", [P, ET], I32)
            t["own_idx"] = keep(f"own_idx_{o}", [P, ET], I32)
            t["edge_idx"] = keep(f"edge_idx_{o}", [P, ET], I32)
            t["scatter_idx"] = keep(f"scatter_idx_{o}", [P, ET], I32)
            t["part_rows"] = keep(f"part_rows_{o}", [AUX, 3, P])
            t["lead_idx"] = keep(f"lead_idx_{o}", [P, 1], I32)
            t["carry_mat"] = keep(f"carry_mat_{o}", [P, P])
            t["aux"] = keep(f"aux_{o}", [P, ET, AUX])
            t["node_rows"] = keep(f"node_rows_{o}", [P, NT, 2], I32)
            order.append(t)
        edge_term = keep("edge_term", [P, ET, AUX])

        def phase(name):
            st = ExitStack()
            st.sb = lambda n, shape, dt=F32: st.enter_context(nc.sbuf_tensor(f"{name}_{n}", shape, dt))
            st.ps = lambda n, shape, dt=F32: st.enter_context(nc.psum_tensor(f"{name}_{n}", shape, dt))
            sems = []

            def gather_sem(n):
                return whole.enter_context(nc.semaphore(f"{name}_{n}"))

            def sem(n):
                sems.append(st.enter_context(nc.semaphore(f"{name}_{n}")))
                return sems[-1]

            def clear():
                if sems:
                    with nc.Block() as block:
                        @block.sync
                        def _(sp):
                            for x in sems:
                                sp.sem_clear(x)

            def blocks():
                st.callback(clear)
                return st.enter_context(nc.Block())

            st.sem, st.gather_sem, st.block = sem, gather_sem, blocks
            return st

        def weights():
            with phase("weights") as ph:
                w0t, w1 = ph.sb("w0t", [P, 2, D]), ph.sb("w1", [P, 2, D])
                we = ph.sb("we", [P, D])
                rows = {n: ph.sb(f"row_{n}", [P, D]) for n in
                        ("attn_h", "attn_t", "attn_e", "as1", "ad1", "as2", "ad2")}
                prod = ph.sb("prod", [P, D])
                red = ph.sb("red", [P, AUX])
                b_col = ph.sb("b_col", [P, 2])
                b1_col = ph.sb("b1_col", [P, 2])
                g_col = ph.sb("g_col", [P, 2, 2])
                ln_col = ph.sb("ln_col", [P, 2, 2])
                ln_col3 = ph.sb("ln_col3", [P, 2, 2, 3])
                raw3 = {n: ph.sb(f"raw3_{n}", [3, D]) for n in ("b2", "fc", "a", "b", "bp")}
                w6t, w7t = ph.sb("w6t", [P, 2, D]), ph.sb("w7t", [P, 2, D])
                c67 = ph.sb("c67", [3, 2, D])
                part = ph.sb("part", [3, 3, D])
                part_b = ph.sb("part_b", [3, 2, D], BF16)
                ps_ww = ph.ps("ww", [P, 2, 512])
                ps_c = ph.ps("c", [P, 512])
                ps_r = ph.ps("r", [P, 2, 512])
                loaded = ph.sem("loaded")
                dve_steps = ph.sem("dve_steps")
                cols_ready = ph.sem("cols_ready")
                products = ph.sem("products")

                def chunks(w):
                    return w.rearrange("(k p) n -> p k n", p=P)

                def spread(v, parts):
                    return v.rearrange("(a n) -> a n", a=1).broadcast_to([parts, v.shape[0]])

                loads = [
                    (ident[:, :], a["ident"]), (before[:, :], a["before"]),
                    (w0t[:, :, :], chunks(a["L0_Wt"])), (w1[:, :, :], chunks(a["L0_W1"])),
                    (w2[:, :, :], chunks(a["L0_W2"])),
                    (wfc[:, :, 0:D], chunks(a["L1_W_fc"])),
                    (we[0:64, :], a["L1_W_e"]), (we[64:128, :], a["L1_W_e"]),
                    (wa[:, :, 0:D], chunks(a["L2_W1"])), (wb[:, :, 0:D], chunks(a["L2_W2"])),
                    (w6t[:, :, :], chunks(a["L3_W6t"])), (w7t[:, :, :], chunks(a["L3_W7t"])),
                    (wp[:, :, :], chunks(a["L3_Wpt"])),
                    (rows["attn_h"][:, :], spread(a["L1_attn_h"], P)), (rows["attn_t"][:, :], spread(a["L1_attn_t"], P)),
                    (rows["attn_e"][:, :], spread(a["L1_attn_e"], P)),
                    (rows["as1"][:, :], spread(a["L2_att_src1"], P)), (rows["ad1"][:, :], spread(a["L2_att_dst1"], P)),
                    (rows["as2"][:, :], spread(a["L2_att_src2"], P)), (rows["ad2"][:, :], spread(a["L2_att_dst2"], P)),
                    (b_col[:, :], a["L0_b"]),
                    (b1_col[:, :], a["L0_b1"]),
                    (g_col[:, 0, :], a["L3_ln6_g"]),
                    (g_col[:, 1, :], a["L3_ln7_g"]),
                    (ln_col[:, 0, :], a["L3_ln6_b"]),
                    (ln_col[:, 1, :], a["L3_ln7_b"]),
                    (raw3["b2"][:, :], spread(a["L0_b2"], 3)), (raw3["fc"][:, :], spread(a["L1_bias"], 3)),
                    (raw3["a"][:, :], spread(a["L2_b1"], 3)), (raw3["b"][:, :], spread(a["L2_b2"], 3)),
                    (raw3["bp"][:, :], spread(a["L3_bp"], 3)),
                    (b6_all[:, :], spread(a["L3_b6"], P)), (b7_all[:, :], spread(a["L3_b7"], P)),
                ]
                block = ph.block()

                @block.sync
                def _(sp):
                    for dst, src in loads:
                        sp.dma_start(dst, src).then_inc(loaded, 16)
                    sp.wait_ge(loaded, 16 * len(loads))

                @block.tensor
                def _(pe):
                    pe.wait_ge(loaded, 16 * len(loads))
                    for m in range(2):
                        for k in range(2):
                            last = nc.tensor.matmul(ps_ww[:, m, 0:D], w0t[:, k, m * P:(m + 1) * P], w1[:, k, :],
                                                    start=k == 0, stop=k == 1)
                    last.then_inc(products, 1)
                    for m in range(2):
                        for k in range(2):
                            last = nc.tensor.matmul(ps_c[:, m:m + 1], w1[:, k, m * P:(m + 1) * P], b_col[:, k:k + 1],
                                                    start=k == 0, stop=k == 1)
                    last.then_inc(products, 1)
                    pe.wait_ge(cols_ready, 1)
                    for l, w in enumerate((w6t, w7t)):
                        for k in range(2):
                            last = nc.tensor.matmul(ps_r[0:3, l, 0:D], ln_col3[:, l, k, :], w[:, k, :],
                                                    start=k == 0, stop=k == 1)
                    last.then_inc(products, 1)

                @block.vector
                def _(dve):
                    st = Steps(dve, dve_steps)
                    dve.wait_ge(loaded, 16 * len(loads))
                    for l in range(2):
                        for k in range(2):
                            last = nc.vector.tensor_copy(ln_col3[:, l, k, :], ln_col[:, l, k:k + 1].broadcast_to([P, 3]))
                            if (l, k) == (1, 1):
                                last.then_inc(cols_ready, 1)
                    st.then(nc.vector.memset(ones3[:, :], 1.0))
                    st.then(nc.vector.memset(eps[:, :], EPS))
                    st.then(nc.vector.memset(v_e[:, :], 0.0))

                    def attend(dst, w, row, heads, parts=slice(0, P)):
                        st.then(nc.vector.tensor_tensor(prod[parts, :], w, row[parts, :], ALU.mult))
                        st.then(nc.vector.tensor_reduce(dst, prod[parts, :].rearrange("p (h c) -> p h c", h=heads),
                                                        AX_X, ALU.add))

                    for k in range(2):
                        attend(wfc[:, k, D:RW], wfc[:, k, 0:D], rows["attn_h"], 8)
                        attend(v_t[:, k, :], wfc[:, k, 0:D], rows["attn_t"], 8)
                        for w, s, d in ((wa, "as1", "ad1"), (wb, "as2", "ad2")):
                            attend(w[:, k, D:D + 4], w[:, k, 0:D], rows[s], 4)
                            attend(w[:, k, D + 4:RW], w[:, k, 0:D], rows[d], 4)
                        for l, (dst, src) in enumerate(((w6, w6t), (w7, w7t))):
                            st.then(nc.vector.tensor_scalar(dst[:, k, :], src[:, k, :], g_col[:, l, k:k + 1], None, ALU.mult))
                    attend(v_e[0:64, 0:AUX], we[0:64, :], rows["attn_e"], 8, slice(0, 64))
                    attend(v_e[64:128, AUX:2 * AUX], we[64:128, :], rows["attn_e"], 8, slice(64, 128))
                    dve.wait_ge(products, 1)
                    st.then(nc.vector.tensor_copy(ww1[:, :, :], ps_ww[:, :, 0:D]))
                    dve.wait_ge(products, 2)
                    st.then(nc.vector.tensor_tensor(mlp_bias[:, :], ps_c[:, 0:2], b1_col[:, :], ALU.add))
                    dve.wait_ge(products, 3)
                    st.then(nc.vector.tensor_copy(c67[:, :, :], ps_r[0:3, :, 0:D]))

                    def in_three(name, src):
                        dst = bias3[name]
                        st.then(nc.vector.memset(dst[:, D:RW], 0.0))
                        st.then(nc.vector.tensor_copy(part_b[:, 0, :], src))
                        st.then(nc.vector.tensor_tensor(part[:, 0, :], src, part_b[:, 0, :], ALU.subtract))
                        st.then(nc.vector.tensor_copy(part_b[:, 1, :], part[:, 0, :]))
                        st.then(nc.vector.tensor_tensor(part[:, 1, :], part[:, 0, :], part_b[:, 1, :], ALU.subtract))
                        st.then(nc.vector.tensor_scalar(part[:, 2, :], part[:, 1, :], ident[0:3, 2:3], None, ALU.mult))
                        st.then(nc.vector.scalar_tensor_tensor(part[:, 0, :], part_b[:, 1, :], ident[0:3, 1:2],
                                                               part[:, 2, :], ALU.mult, ALU.add))
                        st.then(nc.vector.scalar_tensor_tensor(dst[:, 0:D], part_b[:, 0, :], ident[0:3, 0:1],
                                                               part[:, 0, :], ALU.mult, ALU.add))

                    for n in ("b2", "fc", "a", "b", "bp"):
                        in_three(n, raw3[n][:, :])
                    in_three("c6", c67[:, 0, :])
                    in_three("c7", c67[:, 1, :])

        def edge_table():
            with phase("fields") as ph:
                src_i, dst_i = ph.sb("src", [P, ET], I32), ph.sb("dst", [P, ET], I32)
                ew = ph.sb("ew", [P, ET])
                at = ph.sb("at", [P, 2, GE, P])
                fields, pair = ph.sb("fields", [P, ET, 16], I32), ph.sb("pair", [P, ET, 4], I32)
                ps = ph.ps("ps", [P, 2, 512])
                loaded, at_landed, at_used = ph.sem("loaded"), [ph.sem("at0"), ph.sem("at1")], ph.sem("at_used")
                terms, taken, cleared, filled, written = (ph.sem(n) for n in
                                                          ("terms", "taken", "cleared", "filled", "written"))
                attr = a["edge_attr_pairs"]
                groups = ET // 2 // GE
                block = ph.block()

                @block.sync
                def _(sp):
                    for dst, src in ((src_i, "src"), (dst_i, "dst"), (ew, "edge_weight")):
                        sp.dma_start(dst[:, :], a[src].rearrange("(p t) -> p t", p=P)).then_inc(loaded, 16)
                    with sp.Fori(0, groups // 2) as k:
                        for s in range(2):
                            sp.wait_ge(at_used, 2 * k + s + 1)
                            sp.dma_start(at[:, s, :, :], attr[:, bass.ds((2 * k + s) * GE, GE), :]).then_inc(at_landed[s], 16)
                    sp.wait_ge(filled, 4)
                    sp.wait_ge(taken, groups + 1)
                    sp.dma_start(edge_fields.rearrange("(p t) c -> p t c", p=P), fields[:, :, :]).then_inc(written, 16)
                    sp.dma_start(edge_pair.rearrange("(p t) c -> p t c", p=P), pair[:, :, :]).then_inc(written, 16)
                    sp.wait_ge(written, 32)

                @block.tensor
                def _(pe):
                    pe.sem_inc(at_used, 2)
                    with pe.Fori(0, groups // 2) as k:
                        for s in range(2):
                            pe.wait_ge(at_landed[s], 16 * (k + 1))
                            pe.wait_ge(taken, 2 * k + s)
                            for j in range(GE):
                                last = nc.tensor.matmul(ps[:, s, j * 16:j * 16 + 16], at[:, s, j, :], v_e[:, :],
                                                        start=True, stop=True)
                                if j == GE - 1:
                                    last.then_inc(terms, 1)
                            pe.wait_ge(terms, 2 * k + s + 1)
                            pe.sem_inc(at_used, 1)

                @block.vector
                def _(dve):
                    nc.vector.memset(fields[:, :, :], 0).then_inc(cleared, 1)
                    nc.vector.memset(pair[:, :, :], 0).then_inc(cleared, 1)
                    dve.wait_ge(cleared, 2)
                    dve.wait_ge(loaded, 48)
                    nc.vector.tensor_copy(fields[:, :, 8], src_i[:, :]).then_inc(filled, 1)
                    nc.vector.tensor_copy(fields[:, :, 9].bitcast(F32), ew[:, :]).then_inc(filled, 1)
                    nc.vector.tensor_copy(pair[:, :, 0], dst_i[:, :]).then_inc(filled, 1)
                    nc.vector.tensor_copy(pair[:, :, 1].bitcast(F32), ew[:, :]).then_inc(filled, 1)
                    dve.sem_inc(taken, 1)
                    with dve.Fori(0, groups // 2) as k:
                        for s in range(2):
                            dve.wait_ge(terms, 2 * k + s + 1)
                            nc.vector.tensor_copy(
                                fields[:, bass.ds((2 * k + s) * 2 * GE, 2 * GE), 0:AUX].bitcast(F32),
                                ps[:, s, 0:GE * 16].rearrange("p (t h) -> p t h", h=AUX)).then_inc(taken, 1)

        def sort():
            with phase("sort") as ph:
                keys = ph.sb("keys", [P, 2, SW], I32)
                edge_no = ph.sb("edge_no", [P, SW], I32)
                words = [ph.sb("words0", [P, 2 * SW]), ph.sb("words1", [P, 2 * SW])]
                signs = ph.sb("signs", [P, LOG, SW])
                fence = ph.sb("fence", [1, 1], I32)
                turned = ph.ps("turned", [P, 2 * SW])
                filled, numbered, loaded = ph.sem("filled"), ph.sem("numbered"), ph.sem("loaded")
                dve_steps, turn_ready, turn_done = ph.sem("dve_steps"), ph.sem("turn_ready"), ph.sem("turn_done")
                ready, stored = ph.sem("ready"), ph.sem("stored")
                last_part = N_EDGES - (P - 1) * ET
                turns = []

                plan = [("sign", 0)]
                for k in range(1, LOG + 1):
                    if k > 8:
                        plan.append(("turn",))
                        plan += [("cmp", 1 << (b - 8)) for b in range(k - 1, 7, -1)]
                        plan.append(("turn",))
                    plan += [("cmp", 1 << b) for b in range(min(k, 8) - 1, -1, -1)]
                    if k < LOG:
                        plan.append(("sign", k))
                cur = 0
                for step in plan:
                    if step[0] == "turn":
                        turns.append(cur)
                    cur ^= 1
                final = words[cur][:, :].bitcast(I32)

                block = ph.block()

                @block.gpsimd
                def _(pool):
                    nc.gpsimd.iota(edge_no[:, 0:ET], [[1, ET]], base=0, channel_multiplier=ET).then_inc(numbered, 1)
                    nc.gpsimd.iota(edge_no[:, ET:SW], [[1, SW - ET]], base=EP, channel_multiplier=SW - ET).then_inc(numbered, 1)

                @block.sync
                def _(sp):
                    sp.dma_start(signs[:, :, :], a["sort_signs"]).then_inc(loaded, 16)
                    sp.wait_ge(filled, 1)
                    for o, n in ((DST, "dst"), (SRC, "src")):
                        sp.dma_start(keys[0:P - 1, o, 0:ET],
                                     a[n][0:(P - 1) * ET].rearrange("(p t) -> p t", t=ET)).then_inc(loaded, 16)
                        sp.dma_start(keys[P - 1:P, o, 0:last_part],
                                     a[n][(P - 1) * ET:N_EDGES].rearrange("(p t) -> p t", p=1)).then_inc(loaded, 16)
                    sp.wait_ge(ready, 1)
                    for o in (DST, SRC):
                        sp.dma_start(sorted_words[o, 1:1 + SORT].rearrange("(p f) -> p f", p=P),
                                     final[:, o * SW:(o + 1) * SW]).then_inc(stored, 16)
                        sp.dma_start(sorted_words[o:o + 1, 0:1], fence[:, :]).then_inc(stored, 16)
                    sp.wait_ge(stored, 64)
                    for o in (DST, SRC):
                        sp.dma_start(sorted_words[o:o + 1, 1 + EP:2 + EP], fence[:, :]).then_inc(stored, 16)
                    sp.wait_ge(stored, 96)

                @block.tensor
                def _(pe):
                    for n, buf in enumerate(turns):
                        pe.wait_ge(turn_ready, n + 1)
                        for b in range(4):
                            last = nc.tensor.transpose(turned[:, b * P:(b + 1) * P], words[buf][:, b * P:(b + 1) * P], ident[:, :])
                        last.then_inc(turn_done, 1)

                @block.vector
                def _(dve):
                    st = Steps(dve, dve_steps)
                    nc.vector.memset(keys[:, :, :], PAD_KEY).then_inc(filled, 1)
                    st.then(nc.vector.memset(fence[:, :], -1))
                    dve.wait_ge(loaded, 16 * 5)
                    dve.wait_ge(numbered, 2)
                    st.then(nc.vector.tensor_scalar(keys[:, :, :], keys[:, :, :], float(KEY_BIAS), None, ALU.add))
                    st.then(nc.vector.tensor_scalar(keys[:, :, :], keys[:, :, :], KEY_SHIFT, None, ALU.logical_shift_left))
                    st.then(nc.vector.tensor_tensor(words[0][:, :].bitcast(I32).rearrange("p (o f) -> p o f", o=2), keys[:, :, :],
                                                    edge_no[:, None, :].broadcast_to([P, 2, SW]), ALU.bitwise_or))
                    cur, turn = 0, 0
                    for step in plan:
                        src, dst = words[cur], words[cur ^ 1]
                        if step[0] == "sign":
                            st.then(nc.vector.tensor_tensor(dst[:, :].rearrange("p (o f) -> p o f", o=2),
                                                            src[:, :].rearrange("p (o f) -> p o f", o=2),
                                                            signs[:, step[1]:step[1] + 1, :].broadcast_to([P, 2, SW]), ALU.mult))
                        elif step[0] == "turn":
                            dve.sem_inc(turn_ready, 1)
                            turn += 1
                            dve.wait_ge(turn_done, turn)
                            st.then(nc.vector.tensor_copy(dst[:, :], turned[:, :]))
                        else:
                            s4 = src[:, :].rearrange("p (m two d) -> p m two d", two=2, d=step[1])
                            d4 = dst[:, :].rearrange("p (m two d) -> p m two d", two=2, d=step[1])
                            st.mark(nc.vector.tensor_tensor(d4[:, :, 0, :], s4[:, :, 0, :], s4[:, :, 1, :], ALU.min))
                            st.then(nc.vector.tensor_tensor(d4[:, :, 1, :], s4[:, :, 0, :], s4[:, :, 1, :], ALU.max))
                        cur ^= 1
                    dve.sem_inc(ready, 1)

        def marks():
            with phase("marks") as ph:
                raw = ph.sb("raw", [P, 3, 2, ET], I32)
                key = ph.sb("key", [P, 3, 2, ET], I32)
                keyf = ph.sb("keyf", [P, 3, 2, ET])
                near = ph.sb("near", [P, 2, ET])
                column, row_base = ph.sb("column", [P, ET], I32), ph.sb("row_base", [P, 2], I32)
                columnf, row_basef = ph.sb("columnf", [P, ET]), ph.sb("row_basef", [P, 2])
                per_part = ph.sb("per_part", [P, 3, AUX])
                small = ph.sb("small", [P, 8])
                ones_aux = ph.sb("ones_aux", [P, AUX])
                first_key = ph.sb("first_key", [P, P])
                fill = ph.sb("fill", [P, NT, 2], I32)
                zeros = ph.sb("zeros", [P, RW])
                turned = ph.ps("turned", [P, 512])
                loaded, numbered, dve_steps = ph.sem("loaded"), ph.sem("numbered"), ph.sem("dve_steps")
                to_turn, turned_ok, filled, written = (ph.sem(n) for n in ("to_turn", "turned_ok", "filled", "written"))
                block = ph.block()

                @block.gpsimd
                def _(pool):
                    nc.gpsimd.iota(column[:, :], [[1, ET]], base=0, channel_multiplier=0).then_inc(numbered, 1)
                    nc.gpsimd.iota(row_base[:, 0:1], [[0, 1]], base=0, channel_multiplier=ET).then_inc(numbered, 1)
                    nc.gpsimd.iota(row_base[:, 1:2], [[0, 1]], base=SPARE_ROWS, channel_multiplier=1).then_inc(numbered, 1)

                @block.sync
                def _(sp):
                    for n, off in enumerate((1, 0, 2)):
                        for o in (DST, SRC):
                            sp.dma_start(raw[:, n, o, :], sorted_words[o, off:off + EP].rearrange("(p t) -> p t", p=P)).then_inc(loaded, 16)
                    sp.wait_ge(filled, 2)
                    for o in (DST, SRC):
                        sp.dma_start(node_tab[o].rearrange("(p t) c -> p t c", p=P), fill[:, :, :]).then_inc(written, 16)
                    for r in range(0, 2 * P, P):
                        sp.dma_start(sums[EP + r:EP + r + P, :], zeros[:, :]).then_inc(written, 16)
                    sp.wait_ge(written, 64)
                    sp.dma_start(sums[DEFAULT_ROW:DEFAULT_ROW + 1, D:RW], ones_aux[0:1, :]).then_inc(written, 16)
                    sp.wait_ge(written, 80)

                @block.tensor
                def _(pe):
                    for o in (DST, SRC):
                        for n in range(3):
                            pe.wait_ge(to_turn, 4 * o + n + 1)
                            nc.tensor.transpose(turned[0:AUX, n * P:(n + 1) * P], per_part[:, n, :], ident[:, :]).then_inc(turned_ok, 1)
                        pe.wait_ge(to_turn, 4 * o + 4)
                        nc.tensor.transpose(turned[:, 3 * P:4 * P], first_key[:, :], ident[:, :]).then_inc(turned_ok, 1)

                @block.vector
                def _(dve):
                    st = Steps(dve, dve_steps)
                    st.then(nc.vector.memset(ones_aux[:, :], 1.0))
                    st.then(nc.vector.memset(fill[:, :, 0], DEFAULT_ROW))
                    nc.vector.memset(fill[:, :, 1].bitcast(F32), 1.0).then_inc(filled, 1)
                    nc.vector.memset(zeros[:, :], 0.0).then_inc(filled, 1)
                    dve.wait_ge(loaded, 96)
                    dve.wait_ge(numbered, 3)
                    st.then(nc.vector.tensor_scalar(key[:, :, :, :], raw[:, :, :, :], KEY_SHIFT, None, ALU.logical_shift_right))
                    st.then(nc.vector.tensor_scalar(keyf[:, :, :, :], key[:, :, :, :], -float(KEY_BIAS), None, ALU.add))
                    st.then(nc.vector.tensor_copy(columnf[:, :], column[:, :]))
                    st.then(nc.vector.tensor_copy(row_basef[:, :], row_base[:, :]))
                    for o in (DST, SRC):
                        t = order[o]
                        own = keyf[:, 0, o, :]
                        st.then(nc.vector.tensor_scalar(t["edge_idx"][:, :], raw[:, 0, o, :], (1 << KEY_SHIFT) - 1, None, ALU.bitwise_and))
                        st.then(nc.vector.tensor_scalar(t["own_idx"][:, :], own, float(NP - 1), None, ALU.min))
                        st.then(nc.vector.tensor_tensor(t["not_first"][:, :], own, keyf[:, 1, o, :], ALU.is_equal))
                        st.then(nc.vector.tensor_tensor(t["not_last"][:, :], own, keyf[:, 2, o, :], ALU.is_equal))
                        st.then(nc.vector.tensor_scalar(t["is_last"][:, :], t["not_last"][:, :], -1.0, 1.0, ALU.mult, ALU.add))
                        st.then(nc.vector.tensor_scalar(t["restart"][:, :], t["not_first"][:, :], -1.0, BIG, ALU.add, ALU.mult))
                        st.then(nc.vector.scalar_tensor_tensor(t["scatter_idx"][:, :], t["not_last"][:, :], float(FAR), own, ALU.mult, ALU.add))
                        for n, m in ((0, "not_first"), (1, "restart"), (2, "not_last")):
                            st.then(nc.vector.tensor_reduce(small[:, n + 1:n + 2], t[m][:, :], AX_X, ALU.min))
                            nc.vector.tensor_copy(per_part[:, n, :], small[:, n + 1:n + 2].broadcast_to([P, AUX])).then_inc(to_turn, 1)
                            dve.wait_ge(turned_ok, 4 * o + n + 1)
                            st.then(nc.vector.tensor_copy(t["part_rows"][:, n, :], turned[0:AUX, n * P:(n + 1) * P]))
                        nc.vector.tensor_copy(first_key[:, :], keyf[:, 0, o, 0:1].broadcast_to([P, P])).then_inc(to_turn, 1)
                        dve.wait_ge(turned_ok, 4 * o + 4)
                        st.then(nc.vector.tensor_scalar(t["carry_mat"][:, :], turned[:, 3 * P:4 * P], keyf[:, 0, o, ET - 1:ET], None, ALU.is_equal))
                        st.then(nc.vector.tensor_tensor(t["carry_mat"][:, :], t["carry_mat"][:, :], before[:, :], ALU.mult))
                        st.then(nc.vector.scalar_tensor_tensor(near[:, o, :], t["not_last"][:, :], float(FAR), columnf[:, :], ALU.mult, ALU.add))
                        st.then(nc.vector.tensor_reduce(small[:, 4:5], near[:, o, :], AX_X, ALU.min))
                        st.then(nc.vector.tensor_scalar(small[:, 5:6], small[:, 4:5], float(ET), None, ALU.is_lt))
                        st.then(nc.vector.tensor_scalar(small[:, 6:7], small[:, 4:5], float(ET), row_basef[:, 0:1], ALU.min, ALU.add))
                        st.then(nc.vector.tensor_tensor(small[:, 6:7], small[:, 6:7], row_basef[:, 1:2], ALU.subtract))
                        st.then(nc.vector.scalar_tensor_tensor(t["lead_idx"][:, :], small[:, 6:7], small[:, 5:6], row_basef[:, 1:2], ALU.mult, ALU.add))
                        st.then(nc.vector.memset(t["aux"][:, :, :], 0.0))

        def fetch_small(name, jobs):
            with phase(name) as ph:
                width = max(w for _, w, _, _ in jobs)
                dt = jobs[0][3].dtype
                idx = ph.sb("idx", [P, 2, GE], I32)
                got = ph.sb("got", [P, 2, GE, width], dt)
                staged, pace = ph.sem("staged"), ph.sem("pace")
                landed = [[ph.gather_sem(f"landed{n}{s}") for s in range(2)] for n in range(len(jobs))]
                moved = [ph.sem(f"moved{n}") for n in range(len(jobs))]
                block = ph.block()

                @block.gpsimd
                def _(pool):
                    for n, (table, w, index, _) in enumerate(jobs):
                        with pool.Fori(0, EG // 2) as k:
                            for s in range(2):
                                pool.wait_ge(moved[n], 2 * k + s + 1)
                                pool.sem_inc(pace, 1)
                                nc.gpsimd.tensor_copy(idx[:, s, :], index[:, bass.ds((2 * k + s) * GE, GE)]).then_inc(staged, 1)
                                pool.wait_ge(staged, n * EG + 2 * k + s + 1)
                                pool.sem_inc(pace, 1)
                                for j in range(GE):
                                    nc.gpsimd.indirect_dma_start(
                                        out=got[:, s, j, 0:w], out_offset=None, in_=table,
                                        in_offset=bass.IndirectOffsetOnAxis(ap=idx[:, s, j:j + 1], axis=0)).then_inc(landed[n][s], 16)
                        pool.wait_ge(moved[n], EG + 2)

                @block.vector
                def _(dve):
                    for n, (_, w, _, dest) in enumerate(jobs):
                        dve.sem_inc(moved[n], 2)
                        with dve.Fori(0, EG // 2) as k:
                            for s in range(2):
                                dve.wait_ge(landed[n][s], 16 * GE * (k + 1))
                                nc.vector.tensor_copy(dest[:, bass.ds((2 * k + s) * GE, GE), 0:w], got[:, s, :, 0:w]).then_inc(moved[n], 1)

        class Totals:

            def __init__(self, ph, heads):
                self.heads = heads
                self.ends = ph.sb("ends", [P, AUX])
                self.rows = ph.sb("rows", [AUX, P + 2])
                self.init = ph.sb("init", [P, AUX])
                self.turned = ph.ps("ends_turned", [P, 512])
                self.back = ph.ps("ends_back", [P, 512])
                self.asked, self.done = ph.sem("turn_asked"), ph.sem("turn_done")
                self.n = 0

            def tensor_turns(self, pe, count):
                h = self.heads
                for n in range(0, 2 * count, 2):
                    pe.wait_ge(self.asked, n + 1)
                    nc.tensor.transpose(self.turned[0:h, 0:P], self.ends[:, 0:h], ident[:, :]).then_inc(self.done, 1)
                    pe.wait_ge(self.asked, n + 2)
                    lo = 0 if (n // 2) % 2 == 0 else 2
                    nc.tensor.transpose(self.back[:, 0:h], self.rows[0:h, lo:lo + P], ident[0:h, 0:h]).then_inc(self.done, 1)

            def carries(self, dve, st, flags, op0, op1, forward, start):
                h = self.heads
                dve.sem_inc(self.asked, 1)
                self.n += 1
                dve.wait_ge(self.done, self.n)
                row = self.rows[0:h, 1:P + 1]
                edge = self.rows[0:h, 0:1] if forward else self.rows[0:h, P + 1:P + 2]
                st.then(nc.vector.memset(edge, start))
                ends = self.turned[0:h, 0:P]
                if not forward:
                    row, flags, ends = row[:, ::-1], flags[:, ::-1], ends[:, ::-1]
                st.then(nc.vector.tensor_tensor_scan(row, flags, ends, start, op0, op1))
                dve.sem_inc(self.asked, 1)
                self.n += 1
                dve.wait_ge(self.done, self.n)
                st.then(nc.vector.tensor_copy(self.init[:, 0:h], self.back[:, 0:h]))

            def total(self, dve, st, v, t, is_max):
                h = self.heads
                marks_, op0, op1 = (t["restart"], ALU.add, ALU.max) if is_max else (t["not_first"], ALU.mult, ALU.add)
                start = -BIG if is_max else 0.0
                run = self.scratch
                for n in range(h):
                    st.mark(nc.vector.tensor_tensor_scan(run[:, n, :], marks_[:, :], v[:, n, :], start, op0, op1))
                st.ready()
                st.then(nc.vector.tensor_copy(self.ends[:, 0:h], run[:, :, ET - 1]))
                self.carries(dve, st, t["part_rows"][0:h, 1 if is_max else 0, :], op0, op1, True, start)
                for n in range(h):
                    st.mark(nc.vector.tensor_tensor_scan(run[:, n, :], marks_[:, :], v[:, n, :], self.init[:, n:n + 1], op0, op1))
                st.ready()
                st.then(nc.vector.tensor_tensor(run[:, :, :], run[:, :, :], t["is_last"][:, None, :].broadcast_to([P, h, ET]), ALU.mult))
                for n in range(h):
                    st.mark(nc.vector.tensor_tensor_scan(v[:, n, ::-1], t["not_last"][:, ::-1], run[:, n, ::-1], 0.0, ALU.mult, ALU.add))
                st.ready()
                st.then(nc.vector.tensor_copy(self.ends[:, 0:h], v[:, :, 0]))
                self.carries(dve, st, t["part_rows"][0:h, 2, :], ALU.mult, ALU.add, False, 0.0)
                for n in range(h):
                    st.mark(nc.vector.tensor_tensor_scan(v[:, n, ::-1], t["not_last"][:, ::-1], run[:, n, ::-1], self.init[:, n:n + 1], ALU.mult, ALU.add))
                st.ready()

        def degrees(o, fields_tab, node_col, weight_col):
            t = order[o]
            with phase(f"deg{o}") as ph:
                tot = Totals(ph, 1)
                tot.scratch = ph.sb("scratch", [P, 1, ET])
                deg = ph.sb("deg", [P, 1, ET])
                pos, root = ph.sb("pos", [P, ET]), ph.sb("root", [P, ET])
                dve_steps, deg_ready, root_ready = ph.sem("dve_steps"), ph.sem("deg_ready"), ph.sem("root_ready")
                block = ph.block()

                @block.tensor
                def _(pe):
                    tot.tensor_turns(pe, 2)

                @block.scalar
                def _(act):
                    act.wait_ge(deg_ready, 1)
                    nc.scalar.activation(root[:, :], deg[:, 0, :], ACT.Sqrt).then_inc(root_ready, 1)

                @block.vector
                def _(dve):
                    st = Steps(dve, dve_steps)
                    st.then(nc.vector.tensor_copy(t["weight"][:, :], fields_tab[:, :, weight_col].bitcast(F32)))
                    st.then(nc.vector.tensor_copy(t["gather_idx"][:, :], fields_tab[:, :, node_col]))
                    if o == DST:
                        st.then(nc.vector.tensor_copy(edge_term[:, :, :], fields_tab[:, :, 0:AUX].bitcast(F32)))
                    st.then(nc.vector.tensor_copy(deg[:, 0, :], t["weight"][:, :]))
                    tot.total(dve, st, deg, t, False)
                    st.then(nc.vector.tensor_scalar(deg[:, :, :], deg[:, :, :], 1.0, None, ALU.add))
                    st.then(nc.vector.tensor_scalar(pos[:, :], deg[:, 0, :], 0.0, None, ALU.is_gt))
                    st.then(nc.vector.scalar_tensor_tensor(deg[:, 0, :], deg[:, 0, :], -1.0, pos[:, :], ALU.add, ALU.mult))
                    nc.vector.tensor_scalar(deg[:, :, :], deg[:, :, :], 1.0, None, ALU.add).then_inc(deg_ready, 1)
                    dve.wait_ge(root_ready, 1)
                    st.then(nc.vector.reciprocal(root[:, :], root[:, :]))
                    st.then(nc.vector.tensor_tensor(t["aux"][:, :, 4], root[:, :], pos[:, :], ALU.mult))

        def scatter_nodes(o):
            t = order[o]
            with phase(f"ends{o}") as ph:
                val = ph.sb("val", [P, ET, 2], I32)
                idx = ph.sb("idx", [P, 2, GE], I32)
                put = ph.sb("put", [P, 2, GE, 2], I32)
                numbered, valued, staged, pace = (ph.sem(n) for n in ("numbered", "valued", "staged", "pace"))
                written = [ph.gather_sem("written0"), ph.gather_sem("written1")]
                tab_loaded = ph.gather_sem("tab_loaded")
                block = ph.block()

                @block.vector
                def _(dve):
                    nc.vector.tensor_copy(val[:, :, 1].bitcast(F32), t["aux"][:, :, 4]).then_inc(valued, 1)

                @block.gpsimd
                def _(pool):
                    nc.gpsimd.iota(val[:, :, 0], [[1, ET]], base=0, channel_multiplier=ET).then_inc(numbered, 1)
                    pool.wait_ge(numbered, 1)
                    pool.wait_ge(valued, 1)

                    def scatter(k, s):
                        if reused(k):
                            pool.wait_ge(written[s], 16 * GE * k)
                            pool.sem_inc(pace, 1)
                        nc.gpsimd.tensor_copy(idx[:, s, :], t["scatter_idx"][:, bass.ds((2 * k + s) * GE, GE)]).then_inc(staged, 1)
                        nc.gpsimd.tensor_copy(put[:, s, :, :], val[:, bass.ds((2 * k + s) * GE, GE), :]).then_inc(staged, 1)
                        pool.wait_ge(staged, 4 * k + 2 * s + 2)
                        pool.sem_inc(pace, 1)
                        for j in range(GE):
                            nc.gpsimd.indirect_dma_start(
                                out=node_tab[o][:, :], out_offset=bass.IndirectOffsetOnAxis(ap=idx[:, s, j:j + 1], axis=0),
                                in_=put[:, s, j, :], in_offset=None, bounds_check=NP - 1, oob_is_err=False).then_inc(written[s], 16)

                    in_slots(pool, EG, [(scatter, 0)])
                    for s in range(2):
                        pool.wait_ge(written[s], 16 * GE * (EG // 2))
                    pool.dma_start(t["node_rows"][:, :, :], node_tab[o].rearrange("(p t) c -> p t c", p=P)).then_inc(tab_loaded, 16)
                    pool.wait_ge(tab_loaded, 16)

        def sum_edges(name, o, source, by_gather, weights_of, heads, default):
            t = order[o]
            with phase(name) as ph:
                idx = ph.sb("idx", [P, 2, GE], I32)
                rows = ph.sb("rows", [P, 2, GE, D])
                run = ph.sb("run", [P, 2, GE, RW])
                lead, lead_out = ph.sb("lead", [P, RW]), ph.sb("lead_out", [P, RW])
                carry = ph.ps("carry", [P, 512])
                staged, pace, rows_free = ph.sem("staged"), ph.sem("pace"), ph.sem("rows_free")
                landed = [ph.gather_sem("landed0"), ph.gather_sem("landed1")] if by_gather else [ph.sem("landed0"), ph.sem("landed1")]
                scaled, chain, run_full, aux_full = (ph.sem(n) for n in ("scaled", "chain", "run_full", "aux_full"))
                stored = [ph.sem("stored0"), ph.sem("stored1")]
                carried, lead_sum, default_in = (ph.sem(n) for n in ("carried", "lead_sum", "default_in"))
                lead_in, lead_stored = ph.gather_sem("lead_in"), ph.gather_sem("lead_stored")
                sums_v = sums[0:EP, :].rearrange("(p t) c -> p t c", p=P)
                half = EG // 2
                block = ph.block()

                @block.gpsimd
                def _(pool):
                    if by_gather:
                        with pool.Fori(0, half) as k:
                            for s in range(2):
                                pool.wait_ge(rows_free, 2 * k + s + 1)
                                pool.sem_inc(pace, 1)
                                nc.gpsimd.tensor_copy(idx[:, s, :], t["gather_idx"][:, bass.ds((2 * k + s) * GE, GE)]).then_inc(staged, 1)
                                pool.wait_ge(staged, 2 * k + s + 1)
                                pool.sem_inc(pace, 1)
                                for j in range(GE):
                                    nc.gpsimd.indirect_dma_start(
                                        out=rows[:, s, j, :], out_offset=None, in_=source,
                                        in_offset=bass.IndirectOffsetOnAxis(ap=idx[:, s, j:j + 1], axis=0)).then_inc(landed[s], 16)
                    for s in range(2):
                        pool.wait_ge(stored[s], 16 * half)
                    nc.gpsimd.indirect_dma_start(
                        out=lead[:, :], out_offset=None, in_=sums[:, :],
                        in_offset=bass.IndirectOffsetOnAxis(ap=t["lead_idx"][:, :], axis=0)).then_inc(lead_in, 16)
                    pool.wait_ge(lead_sum, 2)
                    nc.gpsimd.indirect_dma_start(
                        out=sums[:, :], out_offset=bass.IndirectOffsetOnAxis(ap=t["lead_idx"][:, :], axis=0),
                        in_=lead_out[:, :], in_offset=None).then_inc(lead_stored, 16)
                    pool.wait_ge(lead_stored, 16)

                @block.sync
                def _(sp):
                    if default is not None:
                        sp.dma_start(sums[DEFAULT_ROW:DEFAULT_ROW + 1, 0:D], default).then_inc(default_in, 16)
                        sp.wait_ge(default_in, 16)

                    def load(k, s):
                        sp.wait_ge(rows_free, 2 * k + s + 1)
                        sp.dma_start(rows[:, s, :, :], source.rearrange("(p t) c -> p t c", p=P)[:, bass.ds((2 * k + s) * GE, GE), :]).then_inc(landed[s], 16)

                    def store(k, s):
                        sp.wait_ge(run_full, 2 * k + s + 1)
                        sp.wait_ge(aux_full, 2 * k + s + 1)
                        sp.dma_start(sums_v[:, bass.ds((2 * k + s) * GE, GE), :], run[:, s, :, :]).then_inc(stored[s], 16)

                    if by_gather:
                        in_slots(sp, EG, [(store, 0)])
                    else:
                        in_slots(sp, EG, [(load, 0), (store, 2)])
                    for s in range(2):
                        sp.wait_ge(stored[s], 16 * half)

                per_group = 16 * GE if by_gather else 16

                @block.scalar
                def _(act):
                    def extras(k, s):
                        if reused(k):
                            act.wait_ge(stored[s], 16 * k)
                            act.sem_inc(pace, 1)
                        nc.scalar.activation(run[:, s, :, D:RW], t["aux"][:, bass.ds((2 * k + s) * GE, GE), :], ACT.Copy).then_inc(aux_full, 1)

                    def scale(k, s):
                        act.wait_ge(landed[s], per_group * (k + 1))
                        act.sem_inc(pace, 1)
                        for j in range(GE):
                            last = nc.scalar.activation(rows[:, s, j, :], rows[:, s, j, :], ACT.Copy,
                                                        scale=weights_of[:, bass.ds((2 * k + s) * GE + j, 1)])
                            if j == GE - 1:
                                last.then_inc(scaled, 1)

                    in_slots(act, EG, [(extras, 0)] + ([(scale, 0)] if heads == 0 else []))

                @block.vector
                def _(dve):
                    dve.sem_inc(rows_free, 2)
                    first = Steps(dve, chain)
                    first.then(nc.vector.memset(run[:, 1, GE - 1, 0:D], 0.0))

                    def add_up(k, s):
                        st = Steps(dve, chain, 1 + (2 * k + s) * (GE + (1 if heads else 0)))
                        if heads:
                            dve.wait_ge(landed[s], per_group * (k + 1))
                            st.then(nc.vector.tensor_tensor(
                                rows[:, s, :, :].rearrange("p j (h c) -> p j h c", h=heads),
                                rows[:, s, :, :].rearrange("p j (h c) -> p j h c", h=heads),
                                weights_of[:, :, bass.ds((2 * k + s) * GE, GE)].rearrange("p h j -> p j h")[:, :, :, None].broadcast_to([P, GE, heads, D // heads]),
                                ALU.mult))
                        else:
                            dve.wait_ge(scaled, 2 * k + s + 1)
                        if reused(k):
                            dve.wait_ge(stored[s], 16 * k)
                        for j in range(GE):
                            prev = run[:, s, j - 1, 0:D] if j else run[:, 1 - s, GE - 1, 0:D]
                            st.then(nc.vector.scalar_tensor_tensor(
                                run[:, s, j, 0:D], prev, t["not_first"][:, bass.ds((2 * k + s) * GE + j, 1)],
                                rows[:, s, j, :], ALU.mult, ALU.add))
                        dve.sem_inc(run_full, 1)
                        dve.sem_inc(rows_free, 1)

                    in_slots(dve, EG, [(add_up, 0)])
                    dve.wait_ge(carried, 1)
                    dve.wait_ge(lead_in, 16)
                    nc.vector.tensor_tensor(lead_out[:, 0:D], lead[:, 0:D], carry[:, 0:D], ALU.add).then_inc(lead_sum, 1)
                    nc.vector.tensor_copy(lead_out[:, D:RW], lead[:, D:RW]).then_inc(lead_sum, 1)

                @block.tensor
                def _(pe):
                    pe.wait_ge(run_full, EG)
                    nc.tensor.matmul(carry[:, 0:D], t["carry_mat"][:, :], run[:, 1, GE - 1, 0:D], start=True, stop=True).then_inc(carried, 1)

        def scale_weights(extra):
            t = order[SRC]
            with phase("coef") as ph:
                dve_steps = ph.sem("dve_steps")
                block = ph.block()

                @block.vector
                def _(dve):
                    st = Steps(dve, dve_steps)
                    st.then(nc.vector.tensor_tensor(t["weight"][:, :], t["weight"][:, :], extra[:, :, 1].bitcast(F32), ALU.mult))
                    st.then(nc.vector.tensor_tensor(t["weight"][:, :], t["weight"][:, :], t["aux"][:, :, 4], ALU.mult))

        def attention(name, heads, w, terms, self_terms, clip):
            t = order[DST]
            with phase(name) as ph:
                tot = Totals(ph, heads)
                tot.scratch = ph.sb("scratch", [P, heads, ET])
                alpha = ph.sb("alpha", [P, heads, ET])
                own = ph.sb("own", [P, heads, ET])
                top = ph.sb("top", [P, heads, ET])
                dve_steps, to_exp, exps = ph.sem("dve_steps"), ph.sem("to_exp"), ph.sem("exps")
                block = ph.block()
                n_exp = 2 if self_terms else 1

                @block.tensor
                def _(pe):
                    tot.tensor_turns(pe, 4)

                @block.scalar
                def _(act):
                    act.wait_ge(to_exp, 1)
                    nc.scalar.activation(alpha[:, :, :], alpha[:, :, :], ACT.Exp).then_inc(exps, 1)
                    if self_terms:
                        act.wait_ge(to_exp, 2)
                        nc.scalar.activation(own[:, :, :], own[:, :, :], ACT.Exp).then_inc(exps, 1)

                @block.vector
                def _(dve):
                    st = Steps(dve, dve_steps)

                    def leaky_sum(dst, parts):
                        parts = [x.rearrange("p t h -> p h t") for x in parts]
                        st.then(nc.vector.tensor_tensor(dst[:, :, :], parts[0], parts[1], ALU.add))
                        for x in parts[2:]:
                            st.then(nc.vector.tensor_tensor(dst[:, :, :], dst[:, :, :], x, ALU.add))
                        st.then(nc.vector.scalar_tensor_tensor(dst[:, :, :], dst[:, :, :], SLOPE, dst[:, :, :], ALU.mult, ALU.max))

                    leaky_sum(alpha, terms)
                    st.then(nc.vector.tensor_copy(top[:, :, :], alpha[:, :, :]))
                    tot.total(dve, st, top, t, True)
                    if self_terms:
                        leaky_sum(own, self_terms)
                        st.then(nc.vector.tensor_tensor(top[:, :, :], top[:, :, :], own[:, :, :], ALU.max))
                    nc.vector.tensor_tensor(alpha[:, :, :], alpha[:, :, :], top[:, :, :], ALU.subtract).then_inc(to_exp, 1)
                    if self_terms:
                        nc.vector.tensor_tensor(own[:, :, :], own[:, :, :], top[:, :, :], ALU.subtract).then_inc(to_exp, 1)
                    dve.wait_ge(exps, n_exp)
                    st.then(nc.vector.tensor_copy(top[:, :, :], alpha[:, :, :]))
                    tot.total(dve, st, top, t, False)
                    if self_terms:
                        st.then(nc.vector.tensor_tensor(top[:, :, :], top[:, :, :], own[:, :, :], ALU.add))
                    if clip:
                        st.then(nc.vector.tensor_scalar(top[:, :, :], top[:, :, :], 1e-16, None, ALU.max))
                    st.then(nc.vector.reciprocal(top[:, :, :], top[:, :, :]))
                    st.then(nc.vector.tensor_tensor(w[:, :, :], alpha[:, :, :], top[:, :, :], ALU.mult))
                    if self_terms:
                        st.then(nc.vector.tensor_tensor(t["aux"][:, :, 0:heads].rearrange("p t h -> p h t"),
                                                        own[:, :, :], top[:, :, :], ALU.mult))

        def project_edges(eh):
            t = order[DST]
            with phase("proj") as ph:
                idx = ph.sb("idx", [P, 2, GE], I32)
                rows = ph.sb("rows", [P, 2, GE, D])
                rows_t = ph.sb("rows_t", [P, 2, D])
                ft = ph.sb("ft", [P, 2, GE, RW])
                ps_t = ph.ps("ps_t", [P, 2, 512])
                ps_f = ph.ps("ps_f", [P, 2, 512])
                staged, pace, rows_free = ph.sem("staged"), ph.sem("pace"), ph.sem("rows_free")
                landed = [ph.gather_sem("landed0"), ph.gather_sem("landed1")]
                stored = [ph.sem("stored0"), ph.sem("stored1")]
                turned, flat, made, eh_out, ft_out = (ph.sem(n) for n in ("turned", "flat", "made", "eh_out", "ft_out"))
                half = EG // 2
                block = ph.block()

                @block.gpsimd
                def _(pool):
                    with pool.Fori(0, half) as k:
                        for s in range(2):
                            pool.wait_ge(rows_free, 2 * k + s + 1)
                            pool.sem_inc(pace, 1)
                            nc.gpsimd.tensor_copy(idx[:, s, :], t["gather_idx"][:, bass.ds((2 * k + s) * GE, GE)]).then_inc(staged, 1)
                            pool.wait_ge(staged, 2 * k + s + 1)
                            pool.sem_inc(pace, 1)
                            for j in range(GE):
                                nc.gpsimd.indirect_dma_start(
                                    out=rows[:, s, j, :], out_offset=None, in_=x1[:, :],
                                    in_offset=bass.IndirectOffsetOnAxis(ap=idx[:, s, j:j + 1], axis=0)).then_inc(landed[s], 16)

                def tile_no(k, s, j):
                    return 2 * GE * k + GE * s + j

                @block.tensor
                def _(pe):
                    pe.sem_inc(rows_free, 2)
                    with pe.Fori(0, half) as k:
                        for s in range(2):
                            pe.wait_ge(landed[s], 16 * GE * (k + 1))
                            for j in range(GE + 1):
                                if j < GE:
                                    b = (GE * s + j) % 2
                                    pe.wait_ge(flat, tile_no(k, s, j) + 1)
                                    for c in range(2):
                                        last = nc.tensor.transpose(ps_t[:, b, c * P:(c + 1) * P], rows[:, s, j, c * P:(c + 1) * P], ident[:, :])
                                    last.then_inc(turned, 1)
                                if j >= 1:
                                    i, b = j - 1, (GE * s + j - 1) % 2
                                    pe.wait_ge(flat, tile_no(k, s, i) + 3)
                                    pe.wait_ge(ft_out, tile_no(k, s, i) + 1)
                                    nc.tensor.matmul(ps_f[:, b, 0:RW], ones3[:, :], bias3["fc"][:, :], start=True, stop=False)
                                    for c in range(2):
                                        last = nc.tensor.matmul(ps_f[:, b, 0:RW], rows_t[:, b, c * P:(c + 1) * P], wfc[:, c, :],
                                                                start=False, stop=c == 1)
                                    last.then_inc(made, 1)
                            pe.sem_inc(rows_free, 1)

                @block.vector
                def _(dve):
                    dve.sem_inc(flat, 2)
                    dve.sem_inc(eh_out, 2)
                    with dve.Fori(0, half) as k:
                        for s in range(2):
                            for j in range(GE):
                                b = (GE * s + j) % 2
                                dve.wait_ge(turned, tile_no(k, s, j) + 1)
                                dve.wait_ge(ft_out, tile_no(k, s, j) + 1)
                                nc.vector.tensor_copy(rows_t[:, b, :], ps_t[:, b, 0:D]).then_inc(flat, 1)
                            dve.wait_ge(ft_out, tile_no(k, s, GE) + 2)
                            nc.vector.tensor_copy(eh[:, bass.ds((2 * k + s) * GE, GE), :], ft[:, s, :, D:RW]).then_inc(eh_out, 1)

                @block.scalar
                def _(act):
                    act.sem_inc(ft_out, 2)

                    def take(k, s):
                        if reused(k):
                            act.wait_ge(stored[s], 16 * k)
                        act.wait_ge(eh_out, 2 * k + s + 1)
                        for j in range(GE):
                            b = (GE * s + j) % 2
                            act.wait_ge(made, tile_no(k, s, j) + 1)
                            nc.scalar.activation(ft[:, s, j, :], ps_f[:, b, 0:RW], ACT.Copy).then_inc(ft_out, 1)

                    in_slots(act, EG, [(take, 0)])

                @block.sync
                def _(sp):
                    with sp.Fori(0, half) as k:
                        for s in range(2):
                            sp.wait_ge(ft_out, 2 + tile_no(k, s, GE - 1) + 1)
                            sp.dma_start(ft_edges.rearrange("(p t) c -> p t c", p=P)[:, bass.ds((2 * k + s) * GE, GE), :], ft[:, s, :, 0:D]).then_inc(stored[s], 16)
                    for s in range(2):
                        sp.wait_ge(stored[s], 16 * half)

        class NodePass:

            U = 4

            def __init__(self, ph, o, loads, stores, wide=()):
                self.ph, self.t, self.loads, self.stores = ph, order[o], loads, stores
                self.idx = ph.sb("idx", [P, 2, GN], I32)
                self.got = ph.sb("got", [P, 2, GN, RW])
                self.staged, self.pace = ph.sem("staged"), ph.sem("pace")
                self.landed = [ph.gather_sem("landed0"), ph.gather_sem("landed1")]
                self.tile, self.in_landed = {}, {}
                for n, (_, depth, _) in loads.items():
                    self.tile[n] = ph.sb(f"in_{n}", [P, depth, GN, D])
                    self.in_landed[n] = [ph.sem(f"in_{n}{b}") for b in range(depth)]
                self.full, self.stored = {}, {}
                for n in stores:
                    self.tile[n] = ph.sb(f"out_{n}", [P, 2, GN, RW if n in wide else D])
                    self.stored[n] = [ph.sem(f"stored_{n}{b}") for b in range(2)]
                self.r = ph.sb("r", [P, 2, GN, D])

            def group(self, k, u):
                return self.U * k + u

            def turn(self, k, u, depth=2):
                return (self.U // depth) * k + u // depth

            def pool_gather(self, pool, got_used):
                def step(k, u):
                    g, s = self.group(k, u), u % 2
                    pool.wait_ge(got_used, g + 1)
                    pool.sem_inc(self.pace, 1)
                    nc.gpsimd.tensor_copy(self.idx[:, s, :], self.t["node_rows"][:, bass.ds(g * GN, GN), 0]).then_inc(self.staged, 1)
                    pool.wait_ge(self.staged, g + 1)
                    pool.sem_inc(self.pace, 1)
                    for j in range(GN):
                        nc.gpsimd.indirect_dma_start(
                            out=self.got[:, s, j, :], out_offset=None, in_=sums[:, :],
                            in_offset=bass.IndirectOffsetOnAxis(ap=self.idx[:, s, j:j + 1], axis=0)).then_inc(self.landed[s], 16)
                in_slots(pool, NG, [(step, 0)], self.U)

            def wait_got(self, dve, k, u):
                dve.wait_ge(self.landed[u % 2], 16 * GN * (self.turn(k, u) + 1))

            def sp_moves(self, sp, store_lag):
                def load(n):
                    array, depth, used = self.loads[n]

                    def step(k, u):
                        g, b = self.group(k, u), u % depth
                        sp.wait_ge(used, g + 1)
                        sp.dma_start(self.tile[n][:, b, :, :],
                                     array.rearrange("(p t) c -> p t c", p=P)[:, bass.ds(g * GN, GN), :]).then_inc(self.in_landed[n][b], 16)
                    return step

                def store(n):
                    def step(k, u):
                        g, b = self.group(k, u), u % 2
                        ready, start = self.full[n]
                        sp.wait_ge(ready, g + 1 + start)
                        sp.dma_start(self.stores[n].rearrange("(p t) c -> p t c", p=P)[:, bass.ds(g * GN, GN), :],
                                     self.tile[n][:, b, :, 0:D]).then_inc(self.stored[n][b], 16)
                    return step

                in_slots(sp, NG, [(load(n), 0) for n in self.loads] + [(store(n), store_lag[n]) for n in self.stores], self.U)
                for n in self.stores:
                    for b in range(2):
                        sp.wait_ge(self.stored[n][b], 16 * (NG // 2))

            def wait_in(self, eng, n, k, u):
                d = self.loads[n][1]
                eng.wait_ge(self.in_landed[n][u % d], 16 * (self.turn(k, u, d) + 1))

            def wait_stored(self, eng, n, k, u):
                if reused(self.turn(k, u)):
                    eng.wait_ge(self.stored[n][u % 2], 16 * self.turn(k, u))

            def norm(self, name, src, dst):
                ph, tag = self.ph, name
                n = {"src": src, "dst": dst,
                     "stats": ph.sb(f"{tag}_stats", [P, 2, GN, 6]), "mv": ph.sb(f"{tag}_mv", [P, 2, GN, 2]),
                     "sd": ph.sb(f"{tag}_sd", [P, 2, GN]), "rs": ph.sb(f"{tag}_rs", [P, 2, GN]), "nm": ph.sb(f"{tag}_nm", [P, 2, GN])}
                for x in ("stat_steps", "measured", "rooted", "factors", "factor_steps", "normed", "paced"):
                    n[x] = ph.sem(f"{tag}_{x}")
                return n

            def norm_stats(self, dve, n, k, u):
                g, s = self.group(k, u), u % 2
                st = Steps(dve, n["stat_steps"], GN * g)
                for j in range(GN):
                    st.mark(nc.vector.bn_stats(n["stats"][:, s, j, :], n["src"][:, s, j, :]))
                st.ready()
                dve.sem_inc(n["paced"], 1)
                for j in range(GN):
                    last = nc.vector.bn_aggr(n["mv"][:, s, j, :], n["stats"][:, s, j, :])
                    if j == GN - 1:
                        last.then_inc(n["measured"], 1)

            def norm_root(self, act, n, k, u):
                g, s = self.group(k, u), u % 2
                act.wait_ge(n["measured"], g + 1)
                nc.scalar.activation(n["sd"][:, s, :], n["mv"][:, s, :, 1], ACT.Sqrt, bias=eps[:, :]).then_inc(n["rooted"], 1)

            def norm_factors(self, dve, n, k, u):
                g, s = self.group(k, u), u % 2
                dve.wait_ge(n["rooted"], g + 1)
                st = Steps(dve, n["factor_steps"], g)
                st.then(nc.vector.reciprocal(n["rs"][:, s, :], n["sd"][:, s, :]))
                nc.vector.scalar_tensor_tensor(n["nm"][:, s, :], n["mv"][:, s, :, 0], -1.0, n["rs"][:, s, :],
                                               ALU.mult, ALU.mult).then_inc(n["factors"], 1)

            def norm_apply(self, act, n, k, u):
                g, s = self.group(k, u), u % 2
                act.wait_ge(n["factors"], g + 1)
                for j in range(GN):
                    last = nc.scalar.activation(n["dst"][:, s, j, :], n["src"][:, s, j, :], ACT.Identity,
                                                bias=n["nm"][:, s, j:j + 1], scale=n["rs"][:, s, j:j + 1])
                    if j == GN - 1:
                        last.then_inc(n["normed"], 1)

        def store_scores(sp, tab, ready, stored):
            sp.wait_ge(ready, NG)
            sp.dma_start(scores.rearrange("(p t) c -> p t c", p=P), tab[:, :, :]).then_inc(stored, 16)
            sp.wait_ge(stored, 16)

        def later(k, g):
            return not isinstance(k, int) or g >= 2

        def mlp_pass():
            with phase("mlp") as ph:
                (z_steps, z_full, z_turned, z_flat, made1, relu_done, made2, r_full,
                 x_turned, x_flat, score_made, scored, tab_stored) = (ph.sem(n) for n in (
                     "z_steps", "z_full", "z_turned", "z_flat", "made1", "relu_done", "made2", "r_full",
                     "x_turned", "x_flat", "score_made", "scored", "tab_stored"))
                np_ = NodePass(ph, SRC, {"x": (a["x"], 4, r_full)}, {"x1": x1})
                x, o1, r = np_.tile["x"], np_.tile["x1"], np_.r
                z = ph.sb("z", [P, 2, GN, D])
                zt, ht, xt = (ph.sb(n, [P, 2, 2, GN * P]) for n in ("zt", "ht", "xt"))
                dd = ph.sb("dd", [P, 2, GN])
                score_tab = ph.sb("score_tab", [P, NT, AUX])
                ps_z, ps_1, ps_2, ps_x = (ph.ps(n, [P, 2, GN * P]) for n in ("ps_z", "ps_1", "ps_2", "ps_x"))
                ln = np_.norm("ln", r, o1)
                np_.full["x1"] = (ln["normed"], 0)
                block = ph.block()

                @block.gpsimd
                def _(pool):
                    np_.pool_gather(pool, z_full)

                @block.sync
                def _(sp):
                    np_.sp_moves(sp, {"x1": 3})
                    store_scores(sp, score_tab, scored, tab_stored)

                @block.tensor
                def _(pe):
                    def turn_z(k, u):
                        g, s = np_.group(k, u), u % 2
                        pe.wait_ge(z_full, g + 3)
                        pe.wait_ge(z_flat, g + 1)
                        for j in range(GN):
                            for c in range(2):
                                last = nc.tensor.transpose(ps_z[:, c, j * P:(j + 1) * P], z[:, s, j, c * P:(c + 1) * P], ident[:, :])
                        last.then_inc(z_turned, 1)

                    def second(k, u):
                        g, s = np_.group(k, u), u % 2
                        pe.wait_ge(relu_done, g + 1)
                        pe.wait_ge(r_full, g + 4)
                        for j in range(GN):
                            dst = ps_2[:, j // 2, (j % 2) * D:(j % 2 + 1) * D]
                            nc.tensor.matmul(dst, ones3[:, :], bias3["b2"][:, 0:D], start=True, stop=False)
                            for c in range(2):
                                last = nc.tensor.matmul(dst, ht[:, s, c, j * P:(j + 1) * P], w2[:, c, :], start=False, stop=c == 1)
                        last.then_inc(made2, 1)

                    def first(k, u):
                        g, s = np_.group(k, u), u % 2
                        pe.wait_ge(z_flat, g + 2)
                        pe.wait_ge(relu_done, g)
                        for m in range(2):
                            for c in range(2):
                                last = nc.tensor.matmul(ps_1[:, m, :], ww1[:, c, m * P:(m + 1) * P], zt[:, s, c, :], start=c == 0, stop=c == 1)
                        last.then_inc(made1, 1)

                    def score(k, u):
                        g, s = np_.group(k, u), u % 2
                        pe.wait_ge(x_flat, g + 1)
                        for j in range(GN):
                            for c in range(2):
                                last = nc.tensor.matmul(ps_x[:, 0, j * AUX:(j + 1) * AUX], xt[:, s, c, j * P:(j + 1) * P], v_t[:, c, :],
                                                        start=c == 0, stop=c == 1)
                        last.then_inc(score_made, 1)

                    def turn_x(k, u):
                        g, s = np_.group(k, u), u % 2
                        pe.wait_ge(ln["normed"], g + 1)
                        pe.wait_ge(scored, g)
                        for j in range(GN):
                            for c in range(2):
                                last = nc.tensor.transpose(ps_x[:, c, j * P:(j + 1) * P], o1[:, s, j, c * P:(c + 1) * P], ident[:, :])
                        last.then_inc(x_turned, 1)

                    in_slots(pe, NG, [(turn_z, 1), (second, 2), (first, 1), (score, 4), (turn_x, 3)], np_.U)

                @block.scalar
                def _(act):
                    act.sem_inc(z_flat, 1)

                    def flat_z(k, u):
                        g, s = np_.group(k, u), u % 2
                        act.wait_ge(z_turned, g + 1)
                        if later(k, g):
                            act.wait_ge(made1, g - 1)
                        nc.scalar.activation(zt[:, s, :, :], ps_z[:, :, :], ACT.Copy).then_inc(z_flat, 1)

                    def flat_x(k, u):
                        g, s = np_.group(k, u), u % 2
                        act.wait_ge(x_turned, g + 1)
                        if later(k, g):
                            act.wait_ge(score_made, g - 1)
                        nc.scalar.activation(xt[:, s, :, :], ps_x[:, :, :], ACT.Copy).then_inc(x_flat, 1)

                    def relu(k, u):
                        g, s = np_.group(k, u), u % 2
                        act.wait_ge(made1, g + 1)
                        if later(k, g):
                            act.wait_ge(made2, g - 1)
                        for m in range(2):
                            last = nc.scalar.activation(ht[:, s, m, :], ps_1[:, m, :], ACT.Relu, bias=mlp_bias[:, m:m + 1])
                        last.then_inc(relu_done, 1)

                    def root(k, u):
                        np_.norm_root(act, ln, k, u)

                    def apply(k, u):
                        g = np_.group(k, u)
                        np_.wait_stored(act, "x1", k, u)
                        if later(k, g):
                            act.wait_ge(x_turned, g - 1)
                        np_.norm_apply(act, ln, k, u)

                    in_slots(act, NG, [(flat_z, 1), (flat_x, 4), (relu, 1), (root, 2), (apply, 2)], np_.U)

                @block.vector
                def _(dve):
                    dve.sem_inc(z_full, 2)
                    dve.sem_inc(r_full, 4)

                    def mix(k, u):
                        g, s = np_.group(k, u), u % 2
                        np_.wait_got(dve, k, u)
                        np_.wait_in(dve, "x", k, u)
                        if later(k, g):
                            dve.wait_ge(z_turned, g - 1)
                        st = Steps(dve, z_steps, g)
                        st.then(nc.vector.tensor_tensor(dd[:, s, :], np_.got[:, s, :, D + 4], np_.got[:, s, :, D + 4], ALU.mult))
                        for j in range(GN):
                            last = nc.vector.scalar_tensor_tensor(z[:, s, j, :], x[:, u % 4, j, :], dd[:, s, j:j + 1],
                                                                  np_.got[:, s, j, 0:D], ALU.mult, ALU.add)
                        last.then_inc(z_full, 1)

                    def residual(k, u):
                        g, s = np_.group(k, u), u % 2
                        dve.wait_ge(made2, g + 1)
                        if later(k, g):
                            dve.wait_ge(ln["normed"], g - 1)
                        nc.vector.tensor_tensor(r[:, s, :, :].rearrange("p (a b) c -> p a (b c)", a=2), ps_2[:, :, :],
                                                x[:, u % 4, :, :].rearrange("p (a b) c -> p a (b c)", a=2), ALU.add).then_inc(r_full, 1)
                        dve.wait_ge(r_full, g + 5)
                        np_.norm_stats(dve, ln, k, u)

                    def factors(k, u):
                        np_.norm_factors(dve, ln, k, u)

                    def take_scores(k, u):
                        g = np_.group(k, u)
                        dve.wait_ge(score_made, g + 1)
                        nc.vector.tensor_copy(score_tab[:, bass.ds(g * GN, GN), :],
                                              ps_x[:, 0, 0:GN * AUX].rearrange("p (j h) -> p j h", h=AUX)).then_inc(scored, 1)

                    in_slots(dve, NG, [(mix, 0), (residual, 2), (factors, 2), (take_scores, 4)], np_.U)

        def layer_pass(name, kind, loads, stores, weight, bias):
            with phase(name) as ph:
                (pre_steps, pre_done, turned, flat, made, taken, scored, sum_done, tab_stored) = (
                    ph.sem(n) for n in ("pre_steps", "pre_done", "turned", "flat", "made", "taken", "scored", "sum_done", "tab_stored"))
                gat, tail = kind in ("gat_in", "gat_mid"), kind == "gcn_out"
                gcn = kind in ("gcn_mid", "gcn_out")
                ins = {n: (array, 2, pre_done) for n, array in loads.items()}
                if tail:
                    ins["x3"] = (loads["x3"], 4, sum_done)
                h_name = next((n for n in stores if n.startswith("h")), None)
                np_ = NodePass(ph, DST, ins, stores, (h_name,) if gat else ())
                r, got, tile = np_.r, np_.got, np_.tile
                vt = ph.sb("vt", [P, 2, 2, GN * P])
                y = ph.sb("y", [P, 2, GN, D]) if kind in ("gat_out", "gcn_mid") else None
                score_tab = ph.sb("score_tab", [P, NT, AUX]) if gat else None
                dis_tab = ph.sb("dis_tab", [P, NT]) if not gat else None
                ps_t = [ph.ps(f"ps_t{b}", [P, 2, GN * P]) for b in range(2)]
                ps_h = ph.ps("ps_h", [P, 4, 512])
                width = RW if gat else D
                norms, lag = [], 0
                operand = r
                if kind == "gat_in":
                    norms = [(np_.norm("ln", r, tile["x2"]), 1)]
                elif kind == "gat_out":
                    norms = [(np_.norm("ln1", r, tile["x3"]), 1), (np_.norm("ln2", tile["x3"], y), 2)]
                elif kind == "gcn_mid":
                    norms = [(np_.norm("ln", tile["x4"], y), 1)]
                if norms:
                    operand, lag = norms[-1][0]["dst"], norms[-1][1]
                    np_.full = {"x2": (norms[0][0]["normed"], 0), "x3": (norms[0][0]["normed"], 0), "x4": (pre_done, 2)}
                if tail:
                    r2 = ph.sb("r2", [P, 2, GN, D])
                    out_norm = np_.norm("out_ln", r2, tile["out"])
                    np_.full["out"] = (out_norm["normed"], 0)
                h_full = ph.sem("h_full")
                np_.full[h_name] = (h_full, 0)
                turn_lag, product_lag = lag + 1, lag + 2
                block = ph.block()

                @block.gpsimd
                def _(pool):
                    np_.pool_gather(pool, pre_done)

                @block.sync
                def _(sp):
                    np_.sp_moves(sp, {n: product_lag + 1 if n == h_name else product_lag + 2 if n == "out" else 2 for n in stores})
                    if gat:
                        store_scores(sp, score_tab, scored, tab_stored)

                @block.tensor
                def _(pe):
                    def turn(k, u):
                        g, s = np_.group(k, u), u % 2
                        if norms:
                            pe.wait_ge(norms[-1][0]["normed"], g + 1)
                        else:
                            pe.wait_ge(pre_done, g + 3)
                        if later(k, g):
                            pe.wait_ge(flat, g - 1)
                        for j in range(GN):
                            for c in range(2):
                                last = nc.tensor.transpose(ps_t[s][:, c, j * P:(j + 1) * P], operand[:, s, j, c * P:(c + 1) * P], ident[:, :])
                        last.then_inc(turned, 1)

                    def product(k, u):
                        g, s = np_.group(k, u), u % 2
                        pe.wait_ge(flat, g + 1)
                        for j in range(GN):
                            pe.wait_ge(taken, g * GN + j + 1)
                            nc.tensor.matmul(ps_h[:, j, 0:width], ones3[:, :], bias3[bias][:, 0:width], start=True, stop=False)
                            for c in range(2):
                                last = nc.tensor.matmul(ps_h[:, j, 0:width], vt[:, s, c, j * P:(j + 1) * P], weight[:, c, 0:width],
                                                        start=False, stop=c == 1)
                            last.then_inc(made, 1)

                    in_slots(pe, NG, [(turn, turn_lag), (product, product_lag)], np_.U)

                @block.scalar
                def _(act):
                    if not tail:
                        act.sem_inc(taken, GN)

                    def flatten(k, u):
                        g, s = np_.group(k, u), u % 2
                        act.wait_ge(turned, g + 1)
                        if later(k, g):
                            act.wait_ge(made, GN * (g - 1))
                        nc.scalar.activation(vt[:, s, :, :], ps_t[s][:, :, :], ACT.Relu if kind == "gat_mid" else ACT.Copy).then_inc(flat, 1)

                    def root(n):
                        return lambda k, u: np_.norm_root(act, n, k, u)

                    def apply(n):
                        def step(k, u):
                            g = np_.group(k, u)
                            stored_name = next((x for x in stores if tile[x] is n["dst"]), None)
                            if stored_name:
                                np_.wait_stored(act, stored_name, k, u)
                            if later(k, g):
                                if n["dst"] is operand:
                                    act.wait_ge(turned, g - 1)
                                elif not tail:
                                    act.wait_ge(norms[1][0]["normed"], g - 1)
                            np_.norm_apply(act, n, k, u)
                        return step

                    def take(k, u):
                        g, s = np_.group(k, u), u % 2
                        np_.wait_stored(act, h_name, k, u)
                        if gat and later(k, g):
                            act.wait_ge(scored, g - 1)
                        for j in range(GN):
                            act.wait_ge(made, g * GN + j + 1)
                            if gat:
                                nc.scalar.activation(tile[h_name][:, s, j, :], ps_h[:, j, 0:RW], ACT.Copy).then_inc(taken, 1)
                            else:
                                nc.scalar.activation(tile[h_name][:, s, j, :], ps_h[:, j, 0:D], ACT.Copy,
                                                     scale=dis_tab[:, bass.ds(g * GN + j, 1)]).then_inc(taken, 1)
                        act.wait_ge(taken, GN * (g + 2))
                        act.sem_inc(h_full, 1)

                    steps = [(flatten, turn_lag)]
                    for n, l in reversed(norms):
                        steps += [(apply(n), l)]
                    for n, l in norms:
                        steps += [(root(n), l - 1)]
                    if tail:
                        steps += [(apply(out_norm), product_lag + 1), (root(out_norm), product_lag)]
                    else:
                        steps += [(take, product_lag)]
                    in_slots(act, NG, steps, np_.U)

                @block.vector
                def _(dve):
                    dve.sem_inc(pre_done, 2)
                    if tail:
                        dve.sem_inc(sum_done, 4)
                        dve.sem_inc(taken, GN)

                    def pre(k, u):
                        g, s = np_.group(k, u), u % 2
                        np_.wait_got(dve, k, u)
                        for n in loads:
                            if not (tail and n == "x3"):
                                np_.wait_in(dve, n, k, u)
                        dst = tile["x4"] if kind == "gcn_mid" else r
                        if kind == "gcn_mid":
                            np_.wait_stored(dve, "x4", k, u)
                        if later(k, g):
                            dve.wait_ge(norms[0][0]["normed"] if norms else turned, g - 1)
                        g_rows, extras = got[:, s, :, 0:D], got[:, s, :, D:RW]
                        if kind == "gat_in":
                            nc.vector.tensor_tensor(r[:, s, :, :], g_rows, tile["x1"][:, s, :, :], ALU.add).then_inc(pre_done, 1)
                        elif kind in ("gat_mid", "gat_out"):
                            count = 1 if kind == "gat_mid" else 3
                            st = Steps(dve, pre_steps, g * count)
                            st.then(nc.vector.tensor_tensor(r[:, s, :, :].rearrange("p j (h c) -> p j h c", h=4),
                                                            tile["h"][:, s, :, :].rearrange("p j (h c) -> p j h c", h=4),
                                                            extras[:, :, 0:4, None].broadcast_to([P, GN, 4, D // 4]), ALU.mult))
                            if kind == "gat_out":
                                st.then(nc.vector.tensor_tensor(r[:, s, :, :], r[:, s, :, :], tile["x2"][:, s, :, :], ALU.add))
                                st.mark(nc.vector.tensor_copy(dis_tab[:, bass.ds(g * GN, GN)], extras[:, :, 4]))
                            nc.vector.tensor_tensor(r[:, s, :, :], r[:, s, :, :], g_rows, ALU.add).then_inc(pre_done, 1)
                        else:
                            st = Steps(dve, pre_steps, g * (2 + GN))
                            b_all = b6_all if kind == "gcn_mid" else b7_all
                            st.mark(nc.vector.tensor_copy(dis_tab[:, bass.ds(g * GN, GN)], extras[:, :, 4]))
                            st.then(nc.vector.tensor_tensor(r[:, s, :, :], tile["h"][:, s, :, :], g_rows, ALU.add))
                            for j in range(GN):
                                st.mark(nc.vector.scalar_tensor_tensor(r[:, s, j, :], r[:, s, j, :], extras[:, j, 4:5], b_all[:, :], ALU.mult, ALU.add))
                            st.ready()
                            nc.vector.scalar_tensor_tensor(dst[:, s, :, :], r[:, s, :, :], 0.0, tile["x3" if kind == "gcn_mid" else "x4"][:, s, :, :],
                                                           ALU.max, ALU.add).then_inc(pre_done, 1)
                        if norms:
                            dve.wait_ge(pre_done, g + 3)
                            np_.norm_stats(dve, norms[0][0], k, u)

                    def factors(n):
                        return lambda k, u: np_.norm_factors(dve, n, k, u)

                    def stats2(k, u):
                        g = np_.group(k, u)
                        dve.wait_ge(norms[0][0]["normed"], g + 1)
                        np_.norm_stats(dve, norms[1][0], k, u)

                    def take_scores(k, u):
                        g, s = np_.group(k, u), u % 2
                        dve.wait_ge(taken, GN * (g + 2))
                        nc.vector.tensor_copy(score_tab[:, bass.ds(g * GN, GN), :], tile[h_name][:, s, :, D:RW]).then_inc(scored, 1)

                    def last_sum(k, u):
                        g, s = np_.group(k, u), u % 2
                        np_.wait_in(dve, "x3", k, u)
                        if later(k, g):
                            dve.wait_ge(out_norm["normed"], g - 1)
                        for j in range(GN):
                            dve.wait_ge(made, GN * g + j + 1)
                            nc.vector.tensor_tensor(r2[:, s, j, :], ps_h[:, j, 0:D], tile["x3"][:, u % 4, j, :], ALU.add).then_inc(taken, 1)
                        dve.wait_ge(taken, GN * (g + 2))
                        dve.sem_inc(sum_done, 1)
                        np_.norm_stats(dve, out_norm, k, u)

                    steps = [(factors(n), l) for n, l in norms]
                    if tail:
                        steps += [(factors(out_norm), product_lag + 1)]
                    steps += [(pre, 0)]
                    if len(norms) == 2:
                        steps += [(stats2, 1)]
                    if gat:
                        steps += [(take_scores, product_lag + 1)]
                    if tail:
                        steps += [(last_sum, product_lag)]
                    in_slots(dve, NG, steps, np_.U)

        weights()
        edge_table()
        sort()
        marks()
        dst, src = order
        with phase("s_fields") as ph:
            got = ph.sb("got", [P, ET, 4], I32)
            extra = ph.sb("extra", [P, ET, 2], I32)
            fetch_small("fetch_s", [(edge_pair[:, :], 4, src["edge_idx"], got)])
            degrees(SRC, got, 0, 1)
            scatter_nodes(SRC)
            fetch_small("fetch_deg", [(node_tab[SRC][:, :], 2, src["gather_idx"], extra)])
            scale_weights(extra)
        sum_edges("sum0", SRC, a["x"][:, :], True, src["weight"], 0, None)
        mlp_pass()
        with phase("d_fields") as ph:
            got = ph.sb("got", [P, ET, 16], I32)
            fetch_small("fetch_d", [(edge_fields[:, :], 16, dst["edge_idx"], got)])
            degrees(DST, got, 8, 9)
            scatter_nodes(DST)
        with phase("gat1") as ph:
            w = ph.sb("w", [P, 8, ET])
            eh, et = ph.sb("eh", [P, ET, AUX]), ph.sb("et", [P, ET, AUX])
            fetch_small("fetch_et", [(scores[:, :], AUX, dst["own_idx"], et)])
            project_edges(eh)
            attention("att1", 8, w, [eh, edge_term, et], None, False)
            sum_edges("sum1", DST, ft_edges, False, w, 8, a["L1_bias"].rearrange("(a n) -> a n", a=1))
        layer_pass("gat_in", "gat_in", {"x1": x1}, {"x2": x2, "h_out": h2a}, wa, "a")

        def self_loop_gat(name, h):
            with phase(name) as ph:
                w = ph.sb("w", [P, 4, ET])
                from_src, own = ph.sb("from_src", [P, ET, AUX]), ph.sb("own", [P, ET, AUX])
                fetch_small(f"{name}_f", [(scores[:, :], AUX, dst["gather_idx"], from_src),
                                          (scores[:, :], AUX, dst["own_idx"], own)])
                attention(f"{name}_a", 4, w, [from_src[:, :, 0:4], own[:, :, 4:8]], [own[:, :, 0:4], own[:, :, 4:8]], True)
                sum_edges(f"{name}_s", DST, h[:, :], True, w, 4, a["zero_row"])

        self_loop_gat("gat2", h2a)
        layer_pass("gat_mid", "gat_mid", {"h": h2a}, {"h_out": h2b}, wb, "b")
        self_loop_gat("gat3", h2b)
        layer_pass("gat_out", "gat_out", {"h": h2b, "x2": x2}, {"x3": x3, "h_out": h3a}, w6, "c6")
        sum_edges("sum4", DST, h3a[:, :], True, dst["weight"], 0, a["zero_row"])
        layer_pass("gcn_mid", "gcn_mid", {"h": h3a, "x3": x3}, {"x4": x4, "h_out": h3b}, w7, "c7")
        sum_edges("sum5", DST, h3b[:, :], True, dst["weight"], 0, a["zero_row"])
        layer_pass("gcn_out", "gcn_out", {"h": h3b, "x4": x4, "x3": x3}, {"out": out}, wp, "bp")


def sort_signs():
    i = np.arange(P)[:, None] * SW + np.arange(SW)[None, :]
    s = [1.0 - 2.0 * ((i >> k) & 1) for k in range(LOG + 1)]
    return np.stack([s[1]] + [s[k] * s[k + 1] for k in range(1, LOG)], axis=1).astype(np.float32)


def kernel(**inputs):
    import numpy as _np
    import concourse.bacc as _bacc
    from concourse.bass_utils import run_bass_kernel_spmd as _run

    def rows(x, n):
        x = _np.asarray(x)
        return _np.concatenate([x, _np.zeros((n - x.shape[0],) + x.shape[1:], x.dtype)])

    def column(x):
        return x.reshape(2, P).T

    g = {k: _np.ascontiguousarray(v) for k, v in inputs.items()}
    arrays = {
        "x": rows(g["x"], NP),
        "src": rows(g["src"], EP), "dst": rows(g["dst"], EP), "edge_weight": rows(g["edge_weight"], EP),
        "edge_attr_pairs": _np.ascontiguousarray(
            rows(g["edge_attr_64"], EP).reshape(P, ET // 2, 2, 64).transpose(2, 3, 1, 0).reshape(P, ET // 2, P)),
        "L0_Wt": g["L0_gnn_W"].T, "L0_W1": g["L0_gnn_W1"], "L0_W2": g["L0_gnn_W2"],
        "L0_b": column(g["L0_gnn_b"]), "L0_b1": column(g["L0_gnn_b1"]), "L0_b2": g["L0_gnn_b2"],
        "L1_W_fc": g["L1_gnn_W_fc"], "L1_W_e": g["L1_gnn_W_e"],
        "L1_attn_h": g["L1_gnn_attn_h"].reshape(-1), "L1_attn_e": g["L1_gnn_attn_e"].reshape(-1),
        "L1_attn_t": g["L1_gnn_attn_t"].reshape(-1), "L1_bias": g["L1_gnn_bias"].reshape(-1),
        "L2_W1": g["L2_gnn_W1"], "L2_att_src1": g["L2_gnn_att_src1"].reshape(-1), "L2_att_dst1": g["L2_gnn_att_dst1"].reshape(-1),
        "L2_b1": g["L2_gnn_b1"], "L2_W2": g["L2_gnn_W2"], "L2_att_src2": g["L2_gnn_att_src2"].reshape(-1),
        "L2_att_dst2": g["L2_gnn_att_dst2"].reshape(-1), "L2_b2": g["L2_gnn_b2"],
        "L3_ln6_g": column(g["L3_gnn_ln6_g"]), "L3_ln6_b": column(g["L3_gnn_ln6_b"]), "L3_W6t": g["L3_gnn_W6"].T, "L3_b6": g["L3_gnn_b6"],
        "L3_ln7_g": column(g["L3_gnn_ln7_g"]), "L3_ln7_b": column(g["L3_gnn_ln7_b"]), "L3_W7t": g["L3_gnn_W7"].T, "L3_b7": g["L3_gnn_b7"],
        "L3_Wpt": g["L3_gnn_Wp"].T, "L3_bp": g["L3_gnn_bp"],
        "ident": _np.eye(P, dtype=_np.float32),
        "before": _np.triu(_np.ones((P, P), _np.float32), 1),
        "zero_row": _np.zeros((1, D), _np.float32),
        "sort_signs": sort_signs(),
    }
    nc = _bacc.Bacc("TRN2", target_bir_lowering=False, num_devices=1)
    aps, data = {}, {}
    for name, v in arrays.items():
        data[f"in_{name}"] = _np.ascontiguousarray(v)
        aps[name] = nc.dram_tensor(f"in_{name}", v.shape, mybir.dt.from_np(v.dtype), kind="ExternalInput").ap()
    out = nc.dram_tensor("out_0", (NP, D), F32, kind="ExternalOutput").ap()
    build(nc, aps, out)
    r = _run(nc, [data], core_ids=[0])
    return r.results[0]["out_0"][:N_NODES]
```

```python
from contextlib import ExitStack

import numpy as np

import concourse.bass as bass
from concourse import mybir

F32 = mybir.dt.float32
I32 = mybir.dt.int32
BF16 = mybir.dt.bfloat16
F32R = mybir.dt.float32r
ALU = mybir.AluOpType
ACT = mybir.ActivationFunctionType
AX_X = mybir.AxisListType.X

P = 128
N_NODES, N_EDGES, D = 50000, 25000, 256
NT = 392
NP = P * NT
ET = 196
EP = P * ET
GN, GE = 4, 7
NG, EG = NT // GN, ET // GE
AUX = 8
RW = D + AUX
DEFAULT_ROW = EP
SPARE_ROWS = EP + P
SUM_ROWS = EP + 2 * P
SORT = 32768
SW = SORT // P
LOG = 15
KEY_SHIFT = 15
KEY_BIAS = 256
PAD_KEY = 65023
FAR = 1 << 20
BIG = 1e38
EPS = 1e-5
SLOPE = 0.2
DST, SRC = 0, 1


class Steps:

    def __init__(self, eng, sem, base=0):
        self.eng, self.sem, self.base, self.n = eng, sem, base, 0

    def mark(self, ins):
        ins.then_inc(self.sem, 1)
        self.n += 1

    def then(self, ins):
        self.mark(ins)
        self.ready()

    def ready(self):
        self.eng.wait_ge(self.sem, self.base + self.n)


def in_slots(eng, groups, steps, unroll=2):
    lags = [lag for _, lag in steps]
    first = -(-(max(lags) + 2) // unroll)
    rounds = (groups + min(lags)) // unroll - first

    def slot(k, u):
        for step, lag in steps:
            back, at = divmod(u - lag, unroll)
            if not isinstance(k, int) or 0 <= unroll * (k + back) + at < groups:
                step(k + back, at)

    for tau in range(unroll * first):
        slot(tau // unroll, tau % unroll)
    with eng.Fori(first, first + rounds) as k:
        for u in range(unroll):
            slot(k, u)
    for tau in range(unroll * (first + rounds), groups + max(lags)):
        slot(tau // unroll, tau % unroll)


def reused(turn):
    return not isinstance(turn, int) or turn >= 1


def build(nc, a, out):
    with ExitStack() as whole:
        def dram(name, shape, dt=F32):
            return nc.dram_tensor(name, shape, dt).ap()

        def keep(name, shape, dt=F32):
            return whole.enter_context(nc.sbuf_tensor(name, shape, dt))

        sorted_words = dram("sorted_words", (2, SORT + 2), I32)
        edge_fields = dram("edge_fields", (EP, 16), I32)
        edge_pair = dram("edge_pair", (EP, 4), I32)
        node_tab = [dram(f"node_tab_{o}", (NP, 2), I32) for o in ("d", "s")]
        scores = dram("scores", (NP, AUX))
        sums = dram("sums", (SUM_ROWS, RW))
        ft_edges = dram("ft_edges", (EP, D))
        x1, x2, x3, x4 = (dram(f"x{i}", (NP, D)) for i in (1, 2, 3, 4))
        h2a, h2b, h3a, h3b = (dram(n, (NP, D)) for n in ("h2a", "h2b", "h3a", "h3b"))

        ident = keep("ident", [P, P])
        before = keep("before", [P, P])
        ww1 = keep("ww1", [P, 2, D])
        w2 = keep("w2", [P, 2, D])
        wfc = keep("wfc", [P, 2, RW])
        v_t = keep("v_t", [P, 2, AUX])
        v_e = keep("v_e", [P, 2 * AUX])
        wa = keep("wa", [P, 2, RW])
        wb = keep("wb", [P, 2, RW])
        w6 = keep("w6", [P, 2, D])
        w7 = keep("w7", [P, 2, D])
        wp = keep("wp", [P, 2, D])
        mlp_bias = keep("mlp_bias", [P, 2])
        ones3 = keep("ones3", [3, P], BF16)
        bias3 = {n: keep(f"bias3_{n}", [3, RW], BF16) for n in ("b2", "fc", "a", "b", "c6", "c7", "bp")}
        b6_all = keep("b6_all", [P, D])
        b7_all = keep("b7_all", [P, D])
        eps = keep("eps", [P, 1])

        order = []
        for o in ("d", "s"):
            t = {n: keep(f"{n}_{o}", [P, ET]) for n in ("not_first", "restart", "not_last", "is_last", "weight")}
            t["gather_idx"] = keep(f"gather_idx_{o}", [P, ET], I32)
            t["own_idx"] = keep(f"own_idx_{o}", [P, ET], I32)
            t["edge_idx"] = keep(f"edge_idx_{o}", [P, ET], I32)
            t["scatter_idx"] = keep(f"scatter_idx_{o}", [P, ET], I32)
            t["part_rows"] = keep(f"part_rows_{o}", [AUX, 3, P])
            t["lead_idx"] = keep(f"lead_idx_{o}", [P, 1], I32)
            t["carry_mat"] = keep(f"carry_mat_{o}", [P, P])
            t["aux"] = keep(f"aux_{o}", [P, ET, AUX])
            t["node_rows"] = keep(f"node_rows_{o}", [P, NT, 2], I32)
            order.append(t)
        edge_term = keep("edge_term", [P, ET, AUX])

        def phase(name):
            st = ExitStack()
            st.sb = lambda n, shape, dt=F32: st.enter_context(nc.sbuf_tensor(f"{name}_{n}", shape, dt))
            st.ps = lambda n, shape, dt=F32: st.enter_context(nc.psum_tensor(f"{name}_{n}", shape, dt))
            sems = []

            def gather_sem(n):
                return whole.enter_context(nc.semaphore(f"{name}_{n}"))

            def sem(n):
                sems.append(st.enter_context(nc.semaphore(f"{name}_{n}")))
                return sems[-1]

            def clear():
                if sems:
                    with nc.Block() as block:
                        @block.sync
                        def _(sp):
                            for x in sems:
                                sp.sem_clear(x)

            def blocks():
                st.callback(clear)
                return st.enter_context(nc.Block())

            st.clear_at_end = lambda: st.callback(clear)
            st.sem, st.gather_sem, st.block = sem, gather_sem, blocks
            return st

        def weights(ph, made):
            w0t, w1 = ph.sb("w0t", [P, 2, D]), ph.sb("w1", [P, 2, D])
            we = ph.sb("we", [P, D])
            rows = {n: ph.sb(f"row_{n}", [P, D]) for n in
                    ("attn_h", "attn_t", "attn_e", "as1", "ad1", "as2", "ad2")}
            prod = ph.sb("prod", [P, D])
            red = ph.sb("red", [P, AUX])
            b_col = ph.sb("b_col", [P, 2])
            b1_col = ph.sb("b1_col", [P, 2])
            g_col = ph.sb("g_col", [P, 2, 2])
            ln_col = ph.sb("ln_col", [P, 2, 2])
            ln_col3 = ph.sb("ln_col3", [P, 2, 2, 3])
            raw3 = {n: ph.sb(f"raw3_{n}", [3, D]) for n in ("b2", "fc", "a", "b", "bp")}
            w6t, w7t = ph.sb("w6t", [P, 2, D]), ph.sb("w7t", [P, 2, D])
            c67 = ph.sb("c67", [3, 2, D])
            part = ph.sb("part", [3, 3, D])
            part_b = ph.sb("part_b", [3, 2, D], BF16)
            ps_ww = ph.ps("ww", [P, 2, 512])
            ps_c = ph.ps("c", [P, 512])
            ps_r = ph.ps("r", [P, 2, 512])
            loaded = ph.sem("loaded")
            dve_steps = ph.sem("dve_steps")
            cols_ready = ph.sem("cols_ready")
            products = ph.sem("products")

            def chunks(w):
                return w.rearrange("(k p) n -> p k n", p=P)

            def spread(v, parts):
                return v.rearrange("(a n) -> a n", a=1).broadcast_to([parts, v.shape[0]])

            loads = [
                (w0t[:, :, :], chunks(a["L0_Wt"])), (w1[:, :, :], chunks(a["L0_W1"])),
                (w2[:, :, :], chunks(a["L0_W2"])),
                (wfc[:, :, 0:D], chunks(a["L1_W_fc"])),
                (we[0:64, :], a["L1_W_e"]), (we[64:128, :], a["L1_W_e"]),
                (wa[:, :, 0:D], chunks(a["L2_W1"])), (wb[:, :, 0:D], chunks(a["L2_W2"])),
                (w6t[:, :, :], chunks(a["L3_W6t"])), (w7t[:, :, :], chunks(a["L3_W7t"])),
                (wp[:, :, :], chunks(a["L3_Wpt"])),
                (rows["attn_h"][:, :], spread(a["L1_attn_h"], P)), (rows["attn_t"][:, :], spread(a["L1_attn_t"], P)),
                (rows["attn_e"][:, :], spread(a["L1_attn_e"], P)),
                (rows["as1"][:, :], spread(a["L2_att_src1"], P)), (rows["ad1"][:, :], spread(a["L2_att_dst1"], P)),
                (rows["as2"][:, :], spread(a["L2_att_src2"], P)), (rows["ad2"][:, :], spread(a["L2_att_dst2"], P)),
                (b_col[:, :], a["L0_b"]),
                (b1_col[:, :], a["L0_b1"]),
                (g_col[:, 0, :], a["L3_ln6_g"]),
                (g_col[:, 1, :], a["L3_ln7_g"]),
                (ln_col[:, 0, :], a["L3_ln6_b"]),
                (ln_col[:, 1, :], a["L3_ln7_b"]),
                (raw3["b2"][:, :], spread(a["L0_b2"], 3)), (raw3["fc"][:, :], spread(a["L1_bias"], 3)),
                (raw3["a"][:, :], spread(a["L2_b1"], 3)), (raw3["b"][:, :], spread(a["L2_b2"], 3)),
                (raw3["bp"][:, :], spread(a["L3_bp"], 3)),
                (b6_all[:, :], spread(a["L3_b6"], P)), (b7_all[:, :], spread(a["L3_b7"], P)),
            ]
            def sp_part(sp):
                for dst, src in loads:
                    sp.dma_start(dst, src).then_inc(loaded, 16)
                sp.wait_ge(loaded, 16 * len(loads))

            def pe_part(pe):
                pe.wait_ge(loaded, 16 * len(loads))
                for m in range(2):
                    for k in range(2):
                        last = nc.tensor.matmul(ps_ww[:, m, 0:D], w0t[:, k, m * P:(m + 1) * P], w1[:, k, :],
                                                start=k == 0, stop=k == 1)
                last.then_inc(products, 1)
                for m in range(2):
                    for k in range(2):
                        last = nc.tensor.matmul(ps_c[:, m:m + 1], w1[:, k, m * P:(m + 1) * P], b_col[:, k:k + 1],
                                                start=k == 0, stop=k == 1)
                last.then_inc(products, 1)
                pe.wait_ge(cols_ready, 1)
                for l, w in enumerate((w6t, w7t)):
                    for k in range(2):
                        last = nc.tensor.matmul(ps_r[0:3, l, 0:D], ln_col3[:, l, k, :], w[:, k, :],
                                                start=k == 0, stop=k == 1)
                last.then_inc(products, 1)

            def dve_part(dve):
                st = Steps(dve, dve_steps)
                dve.wait_ge(loaded, 16 * len(loads))
                for l in range(2):
                    for k in range(2):
                        last = nc.vector.tensor_copy(ln_col3[:, l, k, :], ln_col[:, l, k:k + 1].broadcast_to([P, 3]))
                        if (l, k) == (1, 1):
                            last.then_inc(cols_ready, 1)
                st.then(nc.vector.memset(ones3[:, :], 1.0))
                st.then(nc.vector.memset(eps[:, :], EPS))
                st.then(nc.vector.memset(v_e[:, :], 0.0))

                def attend(dst, w, row, heads, parts=slice(0, P)):
                    st.then(nc.vector.tensor_tensor(prod[parts, :], w, row[parts, :], ALU.mult))
                    st.then(nc.vector.tensor_reduce(dst, prod[parts, :].rearrange("p (h c) -> p h c", h=heads),
                                                    AX_X, ALU.add))

                for k in range(2):
                    attend(wfc[:, k, D:RW], wfc[:, k, 0:D], rows["attn_h"], 8)
                    attend(v_t[:, k, :], wfc[:, k, 0:D], rows["attn_t"], 8)
                    for w, s, d in ((wa, "as1", "ad1"), (wb, "as2", "ad2")):
                        attend(w[:, k, D:D + 4], w[:, k, 0:D], rows[s], 4)
                        attend(w[:, k, D + 4:RW], w[:, k, 0:D], rows[d], 4)
                    for l, (dst, src) in enumerate(((w6, w6t), (w7, w7t))):
                        st.then(nc.vector.tensor_scalar(dst[:, k, :], src[:, k, :], g_col[:, l, k:k + 1], None, ALU.mult))
                attend(v_e[0:64, 0:AUX], we[0:64, :], rows["attn_e"], 8, slice(0, 64))
                attend(v_e[64:128, AUX:2 * AUX], we[64:128, :], rows["attn_e"], 8, slice(64, 128))
                dve.wait_ge(products, 1)
                st.then(nc.vector.tensor_copy(ww1[:, :, :], ps_ww[:, :, 0:D]))
                dve.wait_ge(products, 2)
                st.then(nc.vector.tensor_tensor(mlp_bias[:, :], ps_c[:, 0:2], b1_col[:, :], ALU.add))
                dve.wait_ge(products, 3)
                st.then(nc.vector.tensor_copy(c67[:, :, :], ps_r[0:3, :, 0:D]))

                def in_three(name, src):
                    dst = bias3[name]
                    st.then(nc.vector.memset(dst[:, D:RW], 0.0))
                    st.then(nc.vector.tensor_copy(part_b[:, 0, :], src))
                    st.then(nc.vector.tensor_tensor(part[:, 0, :], src, part_b[:, 0, :], ALU.subtract))
                    st.then(nc.vector.tensor_copy(part_b[:, 1, :], part[:, 0, :]))
                    st.then(nc.vector.tensor_tensor(part[:, 1, :], part[:, 0, :], part_b[:, 1, :], ALU.subtract))
                    st.then(nc.vector.tensor_scalar(part[:, 2, :], part[:, 1, :], ident[0:3, 2:3], None, ALU.mult))
                    st.then(nc.vector.scalar_tensor_tensor(part[:, 0, :], part_b[:, 1, :], ident[0:3, 1:2],
                                                           part[:, 2, :], ALU.mult, ALU.add))
                    st.then(nc.vector.scalar_tensor_tensor(dst[:, 0:D], part_b[:, 0, :], ident[0:3, 0:1],
                                                           part[:, 0, :], ALU.mult, ALU.add))

                for n in ("b2", "fc", "a", "b", "bp"):
                    in_three(n, raw3[n][:, :])
                in_three("c6", c67[:, 0, :])
                in_three("c7", c67[:, 1, :])
                dve.sem_inc(made, 1)

            return sp_part, pe_part, dve_part

        def edge_table(ph, made):
            src_i = ph.sb("src", [P, ET], I32)
            ew = ph.sb("ew", [P, ET])
            at = ph.sb("at", [P, 2, GE, P])
            fields = ph.sb("fields", [P, ET, 16], I32)
            ps = ph.ps("ps", [P, 2, 512])
            loaded, at_landed, at_used = ph.sem("loaded"), [ph.sem("at0"), ph.sem("at1")], ph.sem("at_used")
            terms, taken, cleared, filled, written = (ph.sem(n) for n in
                                                      ("terms", "taken", "cleared", "filled", "written"))
            attr = a["edge_attr_pairs"]
            groups = ET // 2 // GE
            def sp_part(sp):
                for dst, src in ((src_i, "src"), (ew, "edge_weight")):
                    sp.dma_start(dst[:, :], a[src].rearrange("(p t) -> p t", p=P)).then_inc(loaded, 16)
                with sp.Fori(0, groups // 2) as k:
                    for s in range(2):
                        sp.wait_ge(at_used, 2 * k + s + 1)
                        sp.dma_start(at[:, s, :, :], attr[:, bass.ds((2 * k + s) * GE, GE), :]).then_inc(at_landed[s], 16)
                sp.wait_ge(filled, 2)
                sp.wait_ge(taken, groups + 1)
                sp.dma_start(edge_fields.rearrange("(p t) c -> p t c", p=P), fields[:, :, :]).then_inc(written, 16)
                sp.wait_ge(written, 16)

            def pe_part(pe):
                pe.sem_inc(at_used, 2)
                pe.wait_ge(made, 1)
                with pe.Fori(0, groups // 2) as k:
                    for s in range(2):
                        pe.wait_ge(at_landed[s], 16 * (k + 1))
                        pe.wait_ge(taken, 2 * k + s)
                        for j in range(GE):
                            last = nc.tensor.matmul(ps[:, s, j * 16:j * 16 + 16], at[:, s, j, :], v_e[:, :],
                                                    start=True, stop=True)
                            if j == GE - 1:
                                last.then_inc(terms, 1)
                        pe.wait_ge(terms, 2 * k + s + 1)
                        pe.sem_inc(at_used, 1)

            def dve_part(dve):
                nc.vector.memset(fields[:, :, :], 0).then_inc(cleared, 1)
                dve.wait_ge(cleared, 1)
                dve.wait_ge(loaded, 32)
                nc.vector.tensor_copy(fields[:, :, 8], src_i[:, :]).then_inc(filled, 1)
                nc.vector.tensor_copy(fields[:, :, 9].bitcast(F32), ew[:, :]).then_inc(filled, 1)
                dve.sem_inc(taken, 1)
                with dve.Fori(0, groups // 2) as k:
                    for s in range(2):
                        dve.wait_ge(terms, 2 * k + s + 1)
                        nc.vector.tensor_copy(
                            fields[:, bass.ds((2 * k + s) * 2 * GE, 2 * GE), 0:AUX].bitcast(F32),
                            ps[:, s, 0:GE * 16].rearrange("p (t h) -> p t h", h=AUX)).then_inc(taken, 1)

            return sp_part, pe_part, dve_part

        def sort():
            with phase("sort") as ph:
                keys = ph.sb("keys", [P, 2, SW], I32)
                edge_no = ph.sb("edge_no", [P, SW], I32)
                words = [ph.sb("words0", [P, 2 * SW]), ph.sb("words1", [P, 2 * SW])]
                signs = ph.sb("signs", [P, LOG, SW])
                fence = ph.sb("fence", [1, 1], I32)
                dst_i, ew, pair = ph.sb("dst", [P, ET], I32), ph.sb("ew", [P, ET]), ph.sb("pair", [P, ET, 4], I32)
                pair_loaded, paired, pair_stored = ph.sem("pair_loaded"), ph.sem("paired"), ph.sem("pair_stored")
                turned = ph.ps("turned", [P, 2 * SW])
                filled, numbered, loaded = ph.sem("filled"), ph.sem("numbered"), ph.sem("loaded")
                dve_steps, turn_ready, turn_done = ph.sem("dve_steps"), ph.sem("turn_ready"), ph.sem("turn_done")
                ready, stored = ph.sem("ready"), ph.sem("stored")
                last_part = N_EDGES - (P - 1) * ET
                turns = []

                plan = [("sign", 0)]
                for k in range(1, LOG + 1):
                    if k > 8:
                        plan.append(("turn",))
                        plan += [("cmp", 1 << (b - 8)) for b in range(k - 1, 7, -1)]
                        plan.append(("turn",))
                    plan += [("cmp", 1 << b) for b in range(min(k, 8) - 1, -1, -1)]
                    if k < LOG:
                        plan.append(("sign", k))
                cur = 0
                for step in plan:
                    if step[0] == "turn":
                        turns.append(cur)
                    cur ^= 1
                final = words[cur][:, :].bitcast(I32)

                block = ph.block()

                @block.gpsimd
                def _(pool):
                    nc.gpsimd.iota(edge_no[:, 0:ET], [[1, ET]], base=0, channel_multiplier=ET).then_inc(numbered, 1)
                    nc.gpsimd.iota(edge_no[:, ET:SW], [[1, SW - ET]], base=EP, channel_multiplier=SW - ET).then_inc(numbered, 1)
                    nc.gpsimd.memset(pair[:, :, :], 0).then_inc(paired, 1)
                    pool.wait_ge(paired, 1)
                    pool.wait_ge(pair_loaded, 32)
                    nc.gpsimd.tensor_copy(pair[:, :, 0], dst_i[:, :]).then_inc(paired, 1)
                    nc.gpsimd.tensor_copy(pair[:, :, 1].bitcast(F32), ew[:, :]).then_inc(paired, 1)

                @block.sync
                def _(sp):
                    sp.dma_start(signs[:, :, :], a["sort_signs"]).then_inc(loaded, 16)
                    sp.wait_ge(filled, 1)
                    for o, n in ((DST, "dst"), (SRC, "src")):
                        sp.dma_start(keys[0:P - 1, o, 0:ET],
                                     a[n][0:(P - 1) * ET].rearrange("(p t) -> p t", t=ET)).then_inc(loaded, 16)
                        sp.dma_start(keys[P - 1:P, o, 0:last_part],
                                     a[n][(P - 1) * ET:N_EDGES].rearrange("(p t) -> p t", p=1)).then_inc(loaded, 16)
                    for dst, n in ((ident, "ident"), (before, "before")):
                        sp.dma_start(dst[:, :], a[n]).then_inc(loaded, 16)
                    for dst, n in ((dst_i, "dst"), (ew, "edge_weight")):
                        sp.dma_start(dst[:, :], a[n].rearrange("(p t) -> p t", p=P)).then_inc(pair_loaded, 16)
                    sp.wait_ge(paired, 3)
                    sp.dma_start(edge_pair.rearrange("(p t) c -> p t c", p=P), pair[:, :, :]).then_inc(pair_stored, 16)
                    sp.wait_ge(pair_stored, 16)
                    sp.wait_ge(ready, 1)
                    for o in (DST, SRC):
                        sp.dma_start(sorted_words[o, 1:1 + SORT].rearrange("(p f) -> p f", p=P),
                                     final[:, o * SW:(o + 1) * SW]).then_inc(stored, 16)
                        sp.dma_start(sorted_words[o:o + 1, 0:1], fence[:, :]).then_inc(stored, 16)
                    sp.wait_ge(stored, 64)
                    for o in (DST, SRC):
                        sp.dma_start(sorted_words[o:o + 1, 1 + EP:2 + EP], fence[:, :]).then_inc(stored, 16)
                    sp.wait_ge(stored, 96)

                @block.tensor
                def _(pe):
                    for n, buf in enumerate(turns):
                        pe.wait_ge(turn_ready, n + 1)
                        for b in range(4):
                            last = nc.tensor.transpose(turned[:, b * P:(b + 1) * P], words[buf][:, b * P:(b + 1) * P], ident[:, :])
                        last.then_inc(turn_done, 1)

                @block.vector
                def _(dve):
                    st = Steps(dve, dve_steps)
                    nc.vector.memset(keys[:, :, :], PAD_KEY).then_inc(filled, 1)
                    st.then(nc.vector.memset(fence[:, :], -1))
                    dve.wait_ge(loaded, 16 * 7)
                    dve.wait_ge(numbered, 2)
                    st.then(nc.vector.tensor_scalar(keys[:, :, :], keys[:, :, :], float(KEY_BIAS), None, ALU.add))
                    st.then(nc.vector.tensor_scalar(keys[:, :, :], keys[:, :, :], KEY_SHIFT, None, ALU.logical_shift_left))
                    st.then(nc.vector.tensor_tensor(words[0][:, :].bitcast(I32).rearrange("p (o f) -> p o f", o=2), keys[:, :, :],
                                                    edge_no[:, None, :].broadcast_to([P, 2, SW]), ALU.bitwise_or))
                    cur, turn = 0, 0
                    for step in plan:
                        src, dst = words[cur], words[cur ^ 1]
                        if step[0] == "sign":
                            st.then(nc.vector.tensor_tensor(dst[:, :].rearrange("p (o f) -> p o f", o=2),
                                                            src[:, :].rearrange("p (o f) -> p o f", o=2),
                                                            signs[:, step[1]:step[1] + 1, :].broadcast_to([P, 2, SW]), ALU.mult))
                        elif step[0] == "turn":
                            dve.sem_inc(turn_ready, 1)
                            turn += 1
                            dve.wait_ge(turn_done, turn)
                            st.then(nc.vector.tensor_copy(dst[:, :], turned[:, :]))
                        else:
                            s4 = src[:, :].rearrange("p (m two d) -> p m two d", two=2, d=step[1])
                            d4 = dst[:, :].rearrange("p (m two d) -> p m two d", two=2, d=step[1])
                            st.mark(nc.vector.tensor_tensor(d4[:, :, 0, :], s4[:, :, 0, :], s4[:, :, 1, :], ALU.min))
                            st.then(nc.vector.tensor_tensor(d4[:, :, 1, :], s4[:, :, 0, :], s4[:, :, 1, :], ALU.max))
                        cur ^= 1
                    dve.sem_inc(ready, 1)

        def marks():
            with phase("marks") as ph:
                raw = ph.sb("raw", [P, 3, 2, ET], I32)
                key = ph.sb("key", [P, 3, 2, ET], I32)
                keyf = ph.sb("keyf", [P, 3, 2, ET])
                near = ph.sb("near", [P, 2, ET])
                column, row_base = ph.sb("column", [P, ET], I32), ph.sb("row_base", [P, 2], I32)
                columnf, row_basef = ph.sb("columnf", [P, ET]), ph.sb("row_basef", [P, 2])
                per_part = ph.sb("per_part", [P, 3, AUX])
                small = ph.sb("small", [P, 8])
                ones_aux = ph.sb("ones_aux", [P, AUX])
                first_key = ph.sb("first_key", [P, P])
                fill = ph.sb("fill", [P, NT, 2], I32)
                zeros = ph.sb("zeros", [P, RW])
                turned = ph.ps("turned", [P, 512])
                loaded, numbered, dve_steps = ph.sem("loaded"), ph.sem("numbered"), ph.sem("dve_steps")
                to_turn, turned_ok, filled, written = (ph.sem(n) for n in ("to_turn", "turned_ok", "filled", "written"))
                block = ph.block()

                @block.gpsimd
                def _(pool):
                    nc.gpsimd.iota(column[:, :], [[1, ET]], base=0, channel_multiplier=0).then_inc(numbered, 1)
                    nc.gpsimd.iota(row_base[:, 0:1], [[0, 1]], base=0, channel_multiplier=ET).then_inc(numbered, 1)
                    nc.gpsimd.iota(row_base[:, 1:2], [[0, 1]], base=SPARE_ROWS, channel_multiplier=1).then_inc(numbered, 1)

                @block.sync
                def _(sp):
                    for n, off in enumerate((1, 0, 2)):
                        for o in (DST, SRC):
                            sp.dma_start(raw[:, n, o, :], sorted_words[o, off:off + EP].rearrange("(p t) -> p t", p=P)).then_inc(loaded, 16)
                    sp.wait_ge(filled, 2)
                    for o in (DST, SRC):
                        sp.dma_start(node_tab[o].rearrange("(p t) c -> p t c", p=P), fill[:, :, :]).then_inc(written, 16)
                    for r in range(0, 2 * P, P):
                        sp.dma_start(sums[EP + r:EP + r + P, :], zeros[:, :]).then_inc(written, 16)
                    sp.wait_ge(written, 64)
                    sp.dma_start(sums[DEFAULT_ROW:DEFAULT_ROW + 1, D:RW], ones_aux[0:1, :]).then_inc(written, 16)
                    sp.wait_ge(written, 80)

                @block.tensor
                def _(pe):
                    for o in (DST, SRC):
                        for n in range(3):
                            pe.wait_ge(to_turn, 4 * o + n + 1)
                            nc.tensor.transpose(turned[0:AUX, n * P:(n + 1) * P], per_part[:, n, :], ident[:, :]).then_inc(turned_ok, 1)
                        pe.wait_ge(to_turn, 4 * o + 4)
                        nc.tensor.transpose(turned[:, 3 * P:4 * P], first_key[:, :], ident[:, :]).then_inc(turned_ok, 1)

                @block.vector
                def _(dve):
                    st = Steps(dve, dve_steps)
                    st.then(nc.vector.memset(ones_aux[:, :], 1.0))
                    st.then(nc.vector.memset(fill[:, :, 0], DEFAULT_ROW))
                    nc.vector.memset(fill[:, :, 1].bitcast(F32), 1.0).then_inc(filled, 1)
                    nc.vector.memset(zeros[:, :], 0.0).then_inc(filled, 1)
                    dve.wait_ge(loaded, 96)
                    dve.wait_ge(numbered, 3)
                    st.then(nc.vector.tensor_scalar(key[:, :, :, :], raw[:, :, :, :], KEY_SHIFT, None, ALU.logical_shift_right))
                    st.then(nc.vector.tensor_scalar(keyf[:, :, :, :], key[:, :, :, :], -float(KEY_BIAS), None, ALU.add))
                    st.then(nc.vector.tensor_copy(columnf[:, :], column[:, :]))
                    st.then(nc.vector.tensor_copy(row_basef[:, :], row_base[:, :]))
                    for o in (DST, SRC):
                        t = order[o]
                        own = keyf[:, 0, o, :]
                        st.then(nc.vector.tensor_scalar(t["edge_idx"][:, :], raw[:, 0, o, :], (1 << KEY_SHIFT) - 1, None, ALU.bitwise_and))
                        st.then(nc.vector.tensor_scalar(t["own_idx"][:, :], own, float(NP - 1), None, ALU.min))
                        st.then(nc.vector.tensor_tensor(t["not_first"][:, :], own, keyf[:, 1, o, :], ALU.is_equal))
                        st.then(nc.vector.tensor_tensor(t["not_last"][:, :], own, keyf[:, 2, o, :], ALU.is_equal))
                        st.then(nc.vector.tensor_scalar(t["is_last"][:, :], t["not_last"][:, :], -1.0, 1.0, ALU.mult, ALU.add))
                        st.then(nc.vector.tensor_scalar(t["restart"][:, :], t["not_first"][:, :], -1.0, BIG, ALU.add, ALU.mult))
                        st.then(nc.vector.scalar_tensor_tensor(t["scatter_idx"][:, :], t["not_last"][:, :], float(FAR), own, ALU.mult, ALU.add))
                        for n, m in ((0, "not_first"), (1, "restart"), (2, "not_last")):
                            st.then(nc.vector.tensor_reduce(small[:, n + 1:n + 2], t[m][:, :], AX_X, ALU.min))
                            nc.vector.tensor_copy(per_part[:, n, :], small[:, n + 1:n + 2].broadcast_to([P, AUX])).then_inc(to_turn, 1)
                            dve.wait_ge(turned_ok, 4 * o + n + 1)
                            st.then(nc.vector.tensor_copy(t["part_rows"][:, n, :], turned[0:AUX, n * P:(n + 1) * P]))
                        nc.vector.tensor_copy(first_key[:, :], keyf[:, 0, o, 0:1].broadcast_to([P, P])).then_inc(to_turn, 1)
                        dve.wait_ge(turned_ok, 4 * o + 4)
                        st.then(nc.vector.tensor_scalar(t["carry_mat"][:, :], turned[:, 3 * P:4 * P], keyf[:, 0, o, ET - 1:ET], None, ALU.is_equal))
                        st.then(nc.vector.tensor_tensor(t["carry_mat"][:, :], t["carry_mat"][:, :], before[:, :], ALU.mult))
                        st.then(nc.vector.scalar_tensor_tensor(near[:, o, :], t["not_last"][:, :], float(FAR), columnf[:, :], ALU.mult, ALU.add))
                        st.then(nc.vector.tensor_reduce(small[:, 4:5], near[:, o, :], AX_X, ALU.min))
                        st.then(nc.vector.tensor_scalar(small[:, 5:6], small[:, 4:5], float(ET), None, ALU.is_lt))
                        st.then(nc.vector.tensor_scalar(small[:, 6:7], small[:, 4:5], float(ET), row_basef[:, 0:1], ALU.min, ALU.add))
                        st.then(nc.vector.tensor_tensor(small[:, 6:7], small[:, 6:7], row_basef[:, 1:2], ALU.subtract))
                        st.then(nc.vector.scalar_tensor_tensor(t["lead_idx"][:, :], small[:, 6:7], small[:, 5:6], row_basef[:, 1:2], ALU.mult, ALU.add))
                        st.then(nc.vector.memset(t["aux"][:, :, :], 0.0))

        def side_fetch(ph, tag, table, w, index, dest, cols, groups, unroll):
            idx = ph.sb(f"{tag}_idx", [P, 2, cols], I32)
            got = ph.sb(f"{tag}_got", [P, 2, cols, w], dest.dtype)
            staged, moved, pace = ph.sem(f"{tag}_staged"), ph.sem(f"{tag}_moved"), ph.sem(f"{tag}_pace")
            landed = [ph.gather_sem(f"{tag}_landed{s}") for s in range(2)]

            def move(pool, g, s, turn):
                pool.wait_ge(landed[s], 16 * cols * turn)
                pool.sem_inc(pace, 1)
                nc.gpsimd.tensor_copy(dest[:, bass.ds(g * cols, cols), :], got[:, s, :, :]).then_inc(moved, 1)

            def step(pool, k, u):
                g, s, turn = unroll * k + u, u % 2, (unroll // 2) * k + u // 2
                if reused(turn):
                    move(pool, g - 2, s, turn)
                nc.gpsimd.tensor_copy(idx[:, s, :], index[:, bass.ds(g * cols, cols)]).then_inc(staged, 1)
                pool.wait_ge(staged, g + 1)
                if reused(turn):
                    pool.wait_ge(moved, g - 1)
                pool.sem_inc(pace, 1)
                for j in range(cols):
                    nc.gpsimd.indirect_dma_start(
                        out=got[:, s, j, :], out_offset=None, in_=table,
                        in_offset=bass.IndirectOffsetOnAxis(ap=idx[:, s, j:j + 1], axis=0)).then_inc(landed[s], 16)

            def end(pool):
                for s in range(2):
                    move(pool, groups - 2 + s, s, groups // 2)

            return step, end

        def tabulate(ph, o, cols, groups, unroll):
            t = order[o]
            idx, put = ph.sb("tab_idx", [P, 2, cols], I32), ph.sb("tab_put", [P, 2, cols, 2], I32)
            edge_row = ph.sb("edge_row", [P, ET], I32)
            numbered, staged, pace = ph.sem("tab_numbered"), ph.sem("tab_staged"), ph.sem("tab_pace")
            written = [ph.gather_sem(f"tab_written{s}") for s in range(2)]
            tab_loaded = ph.gather_sem("tab_loaded")

            def begin(pool):
                nc.gpsimd.iota(edge_row[:, :], [[1, ET]], base=0, channel_multiplier=ET).then_inc(numbered, 1)
                nc.gpsimd.memset(put[:, :, :, :], 0).then_inc(numbered, 1)
                pool.wait_ge(numbered, 2)

            def step(pool, k, u):
                g, s, turn = unroll * k + u, u % 2, (unroll // 2) * k + u // 2
                if reused(turn):
                    pool.wait_ge(written[s], 16 * cols * turn)
                    pool.sem_inc(pace, 1)
                nc.gpsimd.tensor_copy(idx[:, s, :], t["scatter_idx"][:, bass.ds(g * cols, cols)]).then_inc(staged, 1)
                nc.gpsimd.tensor_copy(put[:, s, :, 0], edge_row[:, bass.ds(g * cols, cols)]).then_inc(staged, 1)
                pool.wait_ge(staged, 2 * g + 2)
                pool.sem_inc(pace, 1)
                for j in range(cols):
                    nc.gpsimd.indirect_dma_start(
                        out=node_tab[o][:, :], out_offset=bass.IndirectOffsetOnAxis(ap=idx[:, s, j:j + 1], axis=0),
                        in_=put[:, s, j, :], in_offset=None, bounds_check=NP - 1, oob_is_err=False).then_inc(written[s], 16)

            def end(pool):
                for s in range(2):
                    pool.wait_ge(written[s], 16 * cols * (groups // 2))
                pool.dma_start(t["node_rows"][:, :, :], node_tab[o].rearrange("(p t) c -> p t c", p=P)).then_inc(tab_loaded, 16)
                pool.wait_ge(tab_loaded, 16)

            return begin, step, end

        def fetch_small(name, jobs):
            with phase(name) as ph:
                width = max(w for _, w, _, _ in jobs)
                dt = jobs[0][3].dtype
                idx = ph.sb("idx", [P, 2, GE], I32)
                got = ph.sb("got", [P, 2, GE, width], dt)
                staged, pace = ph.sem("staged"), ph.sem("pace")
                landed = [[ph.gather_sem(f"landed{n}{s}") for s in range(2)] for n in range(len(jobs))]
                moved = [ph.sem(f"moved{n}") for n in range(len(jobs))]
                block = ph.block()

                @block.gpsimd
                def _(pool):
                    for n, (table, w, index, _) in enumerate(jobs):
                        with pool.Fori(0, EG // 2) as k:
                            for s in range(2):
                                pool.wait_ge(moved[n], 2 * k + s + 1)
                                pool.sem_inc(pace, 1)
                                nc.gpsimd.tensor_copy(idx[:, s, :], index[:, bass.ds((2 * k + s) * GE, GE)]).then_inc(staged, 1)
                                pool.wait_ge(staged, n * EG + 2 * k + s + 1)
                                pool.sem_inc(pace, 1)
                                for j in range(GE):
                                    nc.gpsimd.indirect_dma_start(
                                        out=got[:, s, j, 0:w], out_offset=None, in_=table,
                                        in_offset=bass.IndirectOffsetOnAxis(ap=idx[:, s, j:j + 1], axis=0)).then_inc(landed[n][s], 16)
                        pool.wait_ge(moved[n], EG + 2)

                @block.vector
                def _(dve):
                    for n, (_, w, _, dest) in enumerate(jobs):
                        dve.sem_inc(moved[n], 2)
                        with dve.Fori(0, EG // 2) as k:
                            for s in range(2):
                                dve.wait_ge(landed[n][s], 16 * GE * (k + 1))
                                nc.vector.tensor_copy(dest[:, bass.ds((2 * k + s) * GE, GE), 0:w], got[:, s, :, 0:w]).then_inc(moved[n], 1)

        def prepare(pairs):
            with phase("weights") as ph_w, phase("fields") as ph_e:
                made = ph_w.sem("made")
                fetch_step, fetch_end = side_fetch(ph_w, "pairs", edge_pair[:, :], 4, order[SRC]["edge_idx"], pairs, GE, EG, 2)
                w_sp, w_pe, w_dve = weights(ph_w, made)
                e_sp, e_pe, e_dve = edge_table(ph_e, made)
                ph_w.clear_at_end()
                block = ph_e.block()

                @block.gpsimd
                def _(pool):
                    in_slots(pool, EG, [(lambda k, u: fetch_step(pool, k, u), 0)])
                    fetch_end(pool)

                @block.sync
                def _(sp):
                    w_sp(sp)
                    e_sp(sp)

                @block.tensor
                def _(pe):
                    w_pe(pe)
                    e_pe(pe)

                @block.vector
                def _(dve):
                    w_dve(dve)
                    e_dve(dve)

        class Totals:

            def __init__(self, ph, heads):
                self.heads = heads
                self.ends = ph.sb("ends", [P, AUX])
                self.rows = ph.sb("rows", [AUX, P + 2])
                self.init = ph.sb("init", [P, AUX])
                self.turned = ph.ps("ends_turned", [P, 512])
                self.back = ph.ps("ends_back", [P, 512])
                self.asked, self.done = ph.sem("turn_asked"), ph.sem("turn_done")
                self.n = 0

            def tensor_turns(self, pe, count):
                h = self.heads
                for n in range(0, 2 * count, 2):
                    pe.wait_ge(self.asked, n + 1)
                    nc.tensor.transpose(self.turned[0:h, 0:P], self.ends[:, 0:h], ident[:, :]).then_inc(self.done, 1)
                    pe.wait_ge(self.asked, n + 2)
                    lo = 0 if (n // 2) % 2 == 0 else 2
                    nc.tensor.transpose(self.back[:, 0:h], self.rows[0:h, lo:lo + P], ident[0:h, 0:h]).then_inc(self.done, 1)

            def carries(self, dve, st, flags, op0, op1, forward, start):
                h = self.heads
                dve.sem_inc(self.asked, 1)
                self.n += 1
                dve.wait_ge(self.done, self.n)
                row = self.rows[0:h, 1:P + 1]
                edge = self.rows[0:h, 0:1] if forward else self.rows[0:h, P + 1:P + 2]
                st.then(nc.vector.memset(edge, start))
                ends = self.turned[0:h, 0:P]
                if not forward:
                    row, flags, ends = row[:, ::-1], flags[:, ::-1], ends[:, ::-1]
                st.then(nc.vector.tensor_tensor_scan(row, flags, ends, start, op0, op1))
                dve.sem_inc(self.asked, 1)
                self.n += 1
                dve.wait_ge(self.done, self.n)
                st.then(nc.vector.tensor_copy(self.init[:, 0:h], self.back[:, 0:h]))

            def total(self, dve, st, v, t, is_max):
                h = self.heads
                marks_, op0, op1 = (t["restart"], ALU.add, ALU.max) if is_max else (t["not_first"], ALU.mult, ALU.add)
                start = -BIG if is_max else 0.0
                run = self.scratch
                for n in range(h):
                    st.mark(nc.vector.tensor_tensor_scan(run[:, n, :], marks_[:, :], v[:, n, :], start, op0, op1))
                st.ready()
                st.then(nc.vector.tensor_copy(self.ends[:, 0:h], run[:, :, ET - 1]))
                self.carries(dve, st, t["part_rows"][0:h, 1 if is_max else 0, :], op0, op1, True, start)
                for n in range(h):
                    st.mark(nc.vector.tensor_tensor_scan(run[:, n, :], marks_[:, :], v[:, n, :], self.init[:, n:n + 1], op0, op1))
                st.ready()
                st.then(nc.vector.tensor_tensor(run[:, :, :], run[:, :, :], t["is_last"][:, None, :].broadcast_to([P, h, ET]), ALU.mult))
                for n in range(h):
                    st.mark(nc.vector.tensor_tensor_scan(v[:, n, ::-1], t["not_last"][:, ::-1], run[:, n, ::-1], 0.0, ALU.mult, ALU.add))
                st.ready()
                st.then(nc.vector.tensor_copy(self.ends[:, 0:h], v[:, :, 0]))
                self.carries(dve, st, t["part_rows"][0:h, 2, :], ALU.mult, ALU.add, False, 0.0)
                for n in range(h):
                    st.mark(nc.vector.tensor_tensor_scan(v[:, n, ::-1], t["not_last"][:, ::-1], run[:, n, ::-1], self.init[:, n:n + 1], ALU.mult, ALU.add))
                st.ready()

        def degrees(o, fields_tab, node_col, weight_col):
            t = order[o]
            with phase(f"deg{o}") as ph:
                tot = Totals(ph, 1)
                tot.scratch = ph.sb("scratch", [P, 1, ET])
                deg = ph.sb("deg", [P, 1, ET])
                pos, root = ph.sb("pos", [P, ET]), ph.sb("root", [P, ET])
                dve_steps, deg_ready, root_ready = ph.sem("dve_steps"), ph.sem("deg_ready"), ph.sem("root_ready")
                block = ph.block()

                @block.tensor
                def _(pe):
                    tot.tensor_turns(pe, 2)

                @block.scalar
                def _(act):
                    act.wait_ge(deg_ready, 1)
                    nc.scalar.activation(root[:, :], deg[:, 0, :], ACT.Sqrt).then_inc(root_ready, 1)

                @block.vector
                def _(dve):
                    st = Steps(dve, dve_steps)
                    st.then(nc.vector.tensor_copy(t["weight"][:, :], fields_tab[:, :, weight_col].bitcast(F32)))
                    st.then(nc.vector.tensor_copy(t["gather_idx"][:, :], fields_tab[:, :, node_col]))
                    if o == DST:
                        st.then(nc.vector.tensor_copy(edge_term[:, :, :], fields_tab[:, :, 0:AUX].bitcast(F32)))
                    st.then(nc.vector.tensor_copy(deg[:, 0, :], t["weight"][:, :]))
                    tot.total(dve, st, deg, t, False)
                    st.then(nc.vector.tensor_scalar(deg[:, :, :], deg[:, :, :], 1.0, None, ALU.add))
                    st.then(nc.vector.tensor_scalar(pos[:, :], deg[:, 0, :], 0.0, None, ALU.is_gt))
                    st.then(nc.vector.scalar_tensor_tensor(deg[:, 0, :], deg[:, 0, :], -1.0, pos[:, :], ALU.add, ALU.mult))
                    nc.vector.tensor_scalar(deg[:, :, :], deg[:, :, :], 1.0, None, ALU.add).then_inc(deg_ready, 1)
                    dve.wait_ge(root_ready, 1)
                    st.then(nc.vector.reciprocal(root[:, :], root[:, :]))
                    st.then(nc.vector.tensor_tensor(t["aux"][:, :, 4], root[:, :], pos[:, :], ALU.mult))

        def scatter_nodes(o):
            t = order[o]
            with phase(f"ends{o}") as ph:
                val = ph.sb("val", [P, ET, 2], I32)
                idx = ph.sb("idx", [P, 2, GE], I32)
                put = ph.sb("put", [P, 2, GE, 2], I32)
                numbered, valued, staged, pace = (ph.sem(n) for n in ("numbered", "valued", "staged", "pace"))
                written = [ph.gather_sem("written0"), ph.gather_sem("written1")]
                tab_loaded = ph.gather_sem("tab_loaded")
                block = ph.block()

                @block.vector
                def _(dve):
                    nc.vector.tensor_copy(val[:, :, 1].bitcast(F32), t["aux"][:, :, 4]).then_inc(valued, 1)

                @block.gpsimd
                def _(pool):
                    nc.gpsimd.iota(val[:, :, 0], [[1, ET]], base=0, channel_multiplier=ET).then_inc(numbered, 1)
                    pool.wait_ge(numbered, 1)
                    pool.wait_ge(valued, 1)

                    def scatter(k, s):
                        if reused(k):
                            pool.wait_ge(written[s], 16 * GE * k)
                            pool.sem_inc(pace, 1)
                        nc.gpsimd.tensor_copy(idx[:, s, :], t["scatter_idx"][:, bass.ds((2 * k + s) * GE, GE)]).then_inc(staged, 1)
                        nc.gpsimd.tensor_copy(put[:, s, :, :], val[:, bass.ds((2 * k + s) * GE, GE), :]).then_inc(staged, 1)
                        pool.wait_ge(staged, 4 * k + 2 * s + 2)
                        pool.sem_inc(pace, 1)
                        for j in range(GE):
                            nc.gpsimd.indirect_dma_start(
                                out=node_tab[o][:, :], out_offset=bass.IndirectOffsetOnAxis(ap=idx[:, s, j:j + 1], axis=0),
                                in_=put[:, s, j, :], in_offset=None, bounds_check=NP - 1, oob_is_err=False).then_inc(written[s], 16)

                    in_slots(pool, EG, [(scatter, 0)])
                    for s in range(2):
                        pool.wait_ge(written[s], 16 * GE * (EG // 2))
                    pool.dma_start(t["node_rows"][:, :, :], node_tab[o].rearrange("(p t) c -> p t c", p=P)).then_inc(tab_loaded, 16)
                    pool.wait_ge(tab_loaded, 16)

        def sum_edges(name, o, source, by_gather, weights_of, heads, default):
            t = order[o]
            with phase(name) as ph:
                ahead = 4
                idx = ph.sb("idx", [P, ahead, GE], I32)
                rows = ph.sb("rows", [P, ahead, GE, D])
                run = ph.sb("run", [P, 2, GE, RW])
                lead, lead_out = ph.sb("lead", [P, RW]), ph.sb("lead_out", [P, RW])
                carry = ph.ps("carry", [P, 512])
                staged, pace, rows_free = ph.sem("staged"), ph.sem("pace"), ph.sem("rows_free")
                landed = [(ph.gather_sem if by_gather else ph.sem)(f"landed{u}") for u in range(ahead)]
                scaled, chain, run_full, aux_full = (ph.sem(n) for n in ("scaled", "chain", "run_full", "aux_full"))
                stored = [ph.sem("stored0"), ph.sem("stored1")]
                carried, lead_sum, default_in = (ph.sem(n) for n in ("carried", "lead_sum", "default_in"))
                lead_in, lead_stored = ph.gather_sem("lead_in"), ph.gather_sem("lead_stored")
                sums_v = sums[0:EP, :].rearrange("(p t) c -> p t c", p=P)
                half = EG // 2

                def turn(k, u):
                    return 2 * k + u // 2

                block = ph.block()

                @block.gpsimd
                def _(pool):
                    if by_gather:
                        with pool.Fori(0, EG // ahead) as k:
                            for u in range(ahead):
                                pool.wait_ge(rows_free, ahead * k + u + 1)
                                pool.sem_inc(pace, 1)
                                nc.gpsimd.tensor_copy(idx[:, u, :], t["gather_idx"][:, bass.ds((ahead * k + u) * GE, GE)]).then_inc(staged, 1)
                                pool.wait_ge(staged, ahead * k + u + 1)
                                pool.sem_inc(pace, 1)
                                for j in range(GE):
                                    nc.gpsimd.indirect_dma_start(
                                        out=rows[:, u, j, :], out_offset=None, in_=source,
                                        in_offset=bass.IndirectOffsetOnAxis(ap=idx[:, u, j:j + 1], axis=0)).then_inc(landed[u], 16)
                    for s in range(2):
                        pool.wait_ge(stored[s], 16 * half)
                    nc.gpsimd.indirect_dma_start(
                        out=lead[:, :], out_offset=None, in_=sums[:, :],
                        in_offset=bass.IndirectOffsetOnAxis(ap=t["lead_idx"][:, :], axis=0)).then_inc(lead_in, 16)
                    pool.wait_ge(lead_sum, 2)
                    nc.gpsimd.indirect_dma_start(
                        out=sums[:, :], out_offset=bass.IndirectOffsetOnAxis(ap=t["lead_idx"][:, :], axis=0),
                        in_=lead_out[:, :], in_offset=None).then_inc(lead_stored, 16)
                    pool.wait_ge(lead_stored, 16)

                @block.sync
                def _(sp):
                    if default is not None:
                        sp.dma_start(sums[DEFAULT_ROW:DEFAULT_ROW + 1, 0:D], default).then_inc(default_in, 16)
                        sp.wait_ge(default_in, 16)

                    def load(k, u):
                        g = ahead * k + u
                        sp.wait_ge(rows_free, g + 1)
                        sp.dma_start(rows[:, u, :, :], source.rearrange("(p t) c -> p t c", p=P)[:, bass.ds(g * GE, GE), :]).then_inc(landed[u], 16)

                    def store(k, u):
                        g, s = ahead * k + u, u % 2
                        sp.wait_ge(run_full, g + 1)
                        sp.wait_ge(aux_full, g + 1)
                        sp.dma_start(sums_v[:, bass.ds(g * GE, GE), :], run[:, s, :, :]).then_inc(stored[s], 16)

                    if by_gather:
                        in_slots(sp, EG, [(store, 0)], ahead)
                    else:
                        in_slots(sp, EG, [(load, 0), (store, 4)], ahead)
                    for s in range(2):
                        sp.wait_ge(stored[s], 16 * half)

                per_group = 16 * GE if by_gather else 16

                @block.scalar
                def _(act):
                    def extras(k, u):
                        g, s = ahead * k + u, u % 2
                        if reused(turn(k, u)):
                            act.wait_ge(stored[s], 16 * turn(k, u))
                            act.sem_inc(pace, 1)
                        nc.scalar.activation(run[:, s, :, D:RW], t["aux"][:, bass.ds(g * GE, GE), :], ACT.Copy).then_inc(aux_full, 1)

                    def scale(k, u):
                        g = ahead * k + u
                        act.wait_ge(landed[u], per_group * (k + 1))
                        act.sem_inc(pace, 1)
                        for j in range(GE):
                            last = nc.scalar.activation(rows[:, u, j, :], rows[:, u, j, :], ACT.Copy,
                                                        scale=weights_of[:, bass.ds(g * GE + j, 1)])
                            if j == GE - 1:
                                last.then_inc(scaled, 1)

                    in_slots(act, EG, [(extras, 0)] + ([(scale, 0)] if heads == 0 else []), ahead)

                @block.vector
                def _(dve):
                    dve.sem_inc(rows_free, ahead)
                    first = Steps(dve, chain)
                    first.then(nc.vector.memset(run[:, 1, GE - 1, 0:D], 0.0))

                    def add_up(k, u):
                        g, s = ahead * k + u, u % 2
                        st = Steps(dve, chain, 1 + g * (GE + (1 if heads else 0)))
                        if heads:
                            dve.wait_ge(landed[u], per_group * (k + 1))
                            st.then(nc.vector.tensor_tensor(
                                rows[:, u, :, :].rearrange("p j (h c) -> p j h c", h=heads),
                                rows[:, u, :, :].rearrange("p j (h c) -> p j h c", h=heads),
                                weights_of[:, :, bass.ds(g * GE, GE)].rearrange("p h j -> p j h")[:, :, :, None].broadcast_to([P, GE, heads, D // heads]),
                                ALU.mult))
                        else:
                            dve.wait_ge(scaled, g + 1)
                        if reused(turn(k, u)):
                            dve.wait_ge(stored[s], 16 * turn(k, u))
                        for j in range(GE):
                            prev = run[:, s, j - 1, 0:D] if j else run[:, 1 - s, GE - 1, 0:D]
                            st.then(nc.vector.scalar_tensor_tensor(
                                run[:, s, j, 0:D], prev, t["not_first"][:, bass.ds(g * GE + j, 1)],
                                rows[:, u, j, :], ALU.mult, ALU.add))
                        dve.sem_inc(run_full, 1)
                        dve.sem_inc(rows_free, 1)

                    in_slots(dve, EG, [(add_up, 0)], ahead)
                    dve.wait_ge(carried, 1)
                    dve.wait_ge(lead_in, 16)
                    nc.vector.tensor_tensor(lead_out[:, 0:D], lead[:, 0:D], carry[:, 0:D], ALU.add).then_inc(lead_sum, 1)
                    nc.vector.tensor_copy(lead_out[:, D:RW], lead[:, D:RW]).then_inc(lead_sum, 1)

                @block.tensor
                def _(pe):
                    pe.wait_ge(run_full, EG)
                    nc.tensor.matmul(carry[:, 0:D], t["carry_mat"][:, :], run[:, 1, GE - 1, 0:D], start=True, stop=True).then_inc(carried, 1)

        def scale_weights(extra):
            t = order[SRC]
            with phase("coef") as ph:
                dve_steps = ph.sem("dve_steps")
                block = ph.block()

                @block.vector
                def _(dve):
                    st = Steps(dve, dve_steps)
                    st.then(nc.vector.tensor_tensor(t["weight"][:, :], t["weight"][:, :], extra[:, :, 1].bitcast(F32), ALU.mult))
                    st.then(nc.vector.tensor_tensor(t["weight"][:, :], t["weight"][:, :], t["aux"][:, :, 4], ALU.mult))

        def attention(name, heads, w, terms, self_terms, clip):
            t = order[DST]
            with phase(name) as ph:
                tot = Totals(ph, heads)
                tot.scratch = ph.sb("scratch", [P, heads, ET])
                alpha = ph.sb("alpha", [P, heads, ET])
                own = ph.sb("own", [P, heads, ET])
                top = ph.sb("top", [P, heads, ET])
                dve_steps, to_exp, exps = ph.sem("dve_steps"), ph.sem("to_exp"), ph.sem("exps")
                block = ph.block()
                n_exp = 2 if self_terms else 1

                @block.tensor
                def _(pe):
                    tot.tensor_turns(pe, 4)

                @block.scalar
                def _(act):
                    act.wait_ge(to_exp, 1)
                    nc.scalar.activation(alpha[:, :, :], alpha[:, :, :], ACT.Exp).then_inc(exps, 1)
                    if self_terms:
                        act.wait_ge(to_exp, 2)
                        nc.scalar.activation(own[:, :, :], own[:, :, :], ACT.Exp).then_inc(exps, 1)

                @block.vector
                def _(dve):
                    st = Steps(dve, dve_steps)

                    def leaky_sum(dst, parts):
                        parts = [x.rearrange("p t h -> p h t") for x in parts]
                        st.then(nc.vector.tensor_tensor(dst[:, :, :], parts[0], parts[1], ALU.add))
                        for x in parts[2:]:
                            st.then(nc.vector.tensor_tensor(dst[:, :, :], dst[:, :, :], x, ALU.add))
                        st.then(nc.vector.scalar_tensor_tensor(dst[:, :, :], dst[:, :, :], SLOPE, dst[:, :, :], ALU.mult, ALU.max))

                    leaky_sum(alpha, terms)
                    st.then(nc.vector.tensor_copy(top[:, :, :], alpha[:, :, :]))
                    tot.total(dve, st, top, t, True)
                    if self_terms:
                        leaky_sum(own, self_terms)
                        st.then(nc.vector.tensor_tensor(top[:, :, :], top[:, :, :], own[:, :, :], ALU.max))
                    nc.vector.tensor_tensor(alpha[:, :, :], alpha[:, :, :], top[:, :, :], ALU.subtract).then_inc(to_exp, 1)
                    if self_terms:
                        nc.vector.tensor_tensor(own[:, :, :], own[:, :, :], top[:, :, :], ALU.subtract).then_inc(to_exp, 1)
                    dve.wait_ge(exps, n_exp)
                    st.then(nc.vector.tensor_copy(top[:, :, :], alpha[:, :, :]))
                    tot.total(dve, st, top, t, False)
                    if self_terms:
                        st.then(nc.vector.tensor_tensor(top[:, :, :], top[:, :, :], own[:, :, :], ALU.add))
                    if clip:
                        st.then(nc.vector.tensor_scalar(top[:, :, :], top[:, :, :], 1e-16, None, ALU.max))
                    st.then(nc.vector.reciprocal(top[:, :, :], top[:, :, :]))
                    st.then(nc.vector.tensor_tensor(w[:, :, :], alpha[:, :, :], top[:, :, :], ALU.mult))
                    if self_terms:
                        st.then(nc.vector.tensor_tensor(t["aux"][:, :, 0:heads].rearrange("p t h -> p h t"),
                                                        own[:, :, :], top[:, :, :], ALU.mult))

        def project_edges(eh, et):
            t = order[DST]
            with phase("proj") as ph:
                idx = ph.sb("idx", [P, 2, GE], I32)
                rows = ph.sb("rows", [P, 2, GE, D])
                rows_t = ph.sb("rows_t", [P, 2, D])
                ft = ph.sb("ft", [P, 2, GE, RW])
                ps_t = ph.ps("ps_t", [P, 2, 512])
                ps_f = ph.ps("ps_f", [P, 2, 512])
                staged, pace, rows_free = ph.sem("staged"), ph.sem("pace"), ph.sem("rows_free")
                landed = [ph.gather_sem("landed0"), ph.gather_sem("landed1")]
                stored = [ph.sem("stored0"), ph.sem("stored1")]
                turned, flat, made, eh_out, ft_out = (ph.sem(n) for n in ("turned", "flat", "made", "eh_out", "ft_out"))
                half = EG // 2
                fetch_step, fetch_end = side_fetch(ph, "et", scores[:, :], AUX, t["own_idx"], et, GE, EG, 2)
                block = ph.block()

                @block.gpsimd
                def _(pool):
                    def fetch_rows(k, s):
                        pool.wait_ge(rows_free, 2 * k + s + 1)
                        pool.sem_inc(pace, 1)
                        nc.gpsimd.tensor_copy(idx[:, s, :], t["gather_idx"][:, bass.ds((2 * k + s) * GE, GE)]).then_inc(staged, 1)
                        pool.wait_ge(staged, 2 * k + s + 1)
                        pool.sem_inc(pace, 1)
                        for j in range(GE):
                            nc.gpsimd.indirect_dma_start(
                                out=rows[:, s, j, :], out_offset=None, in_=x1[:, :],
                                in_offset=bass.IndirectOffsetOnAxis(ap=idx[:, s, j:j + 1], axis=0)).then_inc(landed[s], 16)

                    in_slots(pool, EG, [(fetch_rows, 0), (lambda k, u: fetch_step(pool, k, u), 0)])
                    fetch_end(pool)

                def tile_no(k, s, j):
                    return 2 * GE * k + GE * s + j

                @block.tensor
                def _(pe):
                    pe.sem_inc(rows_free, 2)
                    with pe.Fori(0, half) as k:
                        for s in range(2):
                            pe.wait_ge(landed[s], 16 * GE * (k + 1))
                            for j in range(GE + 1):
                                if j < GE:
                                    b = (GE * s + j) % 2
                                    pe.wait_ge(flat, tile_no(k, s, j) + 1)
                                    for c in range(2):
                                        last = nc.tensor.transpose(ps_t[:, b, c * P:(c + 1) * P], rows[:, s, j, c * P:(c + 1) * P], ident[:, :])
                                    last.then_inc(turned, 1)
                                if j >= 1:
                                    i, b = j - 1, (GE * s + j - 1) % 2
                                    pe.wait_ge(flat, tile_no(k, s, i) + 3)
                                    pe.wait_ge(ft_out, tile_no(k, s, i) + 1)
                                    nc.tensor.matmul(ps_f[:, b, 0:RW], ones3[:, :], bias3["fc"][:, :], start=True, stop=False)
                                    for c in range(2):
                                        last = nc.tensor.matmul(ps_f[:, b, 0:RW], rows_t[:, b, c * P:(c + 1) * P], wfc[:, c, :],
                                                                start=False, stop=c == 1)
                                    last.then_inc(made, 1)
                            pe.sem_inc(rows_free, 1)

                @block.vector
                def _(dve):
                    dve.sem_inc(flat, 2)
                    dve.sem_inc(eh_out, 2)
                    with dve.Fori(0, half) as k:
                        for s in range(2):
                            for j in range(GE):
                                b = (GE * s + j) % 2
                                dve.wait_ge(turned, tile_no(k, s, j) + 1)
                                dve.wait_ge(ft_out, tile_no(k, s, j) + 1)
                                nc.vector.tensor_copy(rows_t[:, b, :], ps_t[:, b, 0:D]).then_inc(flat, 1)
                            dve.wait_ge(ft_out, tile_no(k, s, GE) + 2)
                            nc.vector.tensor_copy(eh[:, bass.ds((2 * k + s) * GE, GE), :], ft[:, s, :, D:RW]).then_inc(eh_out, 1)

                @block.scalar
                def _(act):
                    act.sem_inc(ft_out, 2)

                    def take(k, s):
                        if reused(k):
                            act.wait_ge(stored[s], 16 * k)
                        act.wait_ge(eh_out, 2 * k + s + 1)
                        for j in range(GE):
                            b = (GE * s + j) % 2
                            act.wait_ge(made, tile_no(k, s, j) + 1)
                            nc.scalar.activation(ft[:, s, j, :], ps_f[:, b, 0:RW], ACT.Copy).then_inc(ft_out, 1)

                    in_slots(act, EG, [(take, 0)])

                @block.sync
                def _(sp):
                    with sp.Fori(0, half) as k:
                        for s in range(2):
                            sp.wait_ge(ft_out, 2 + tile_no(k, s, GE - 1) + 1)
                            sp.dma_start(ft_edges.rearrange("(p t) c -> p t c", p=P)[:, bass.ds((2 * k + s) * GE, GE), :], ft[:, s, :, 0:D]).then_inc(stored[s], 16)
                    for s in range(2):
                        sp.wait_ge(stored[s], 16 * half)

        class NodePass:

            U = 4
            AHEAD = 4

            def __init__(self, ph, o, loads, stores, wide=()):
                self.ph, self.t, self.loads, self.stores = ph, order[o], loads, stores
                self.idx = ph.sb("idx", [P, self.AHEAD, GN], I32)
                self.got = ph.sb("got", [P, self.AHEAD, GN, RW])
                self.staged, self.pace = ph.sem("staged"), ph.sem("pace")
                self.landed = [ph.gather_sem(f"landed{b}") for b in range(self.AHEAD)]
                self.tile, self.in_landed = {}, {}
                for n, (_, depth, _) in loads.items():
                    self.tile[n] = ph.sb(f"in_{n}", [P, depth, GN, D])
                    self.in_landed[n] = [ph.sem(f"in_{n}{b}") for b in range(depth)]
                self.full, self.stored = {}, {}
                for n in stores:
                    self.tile[n] = ph.sb(f"out_{n}", [P, 2, GN, RW if n in wide else D])
                    self.stored[n] = [ph.sem(f"stored_{n}{b}") for b in range(2)]
                self.r = ph.sb("r", [P, 2, GN, D])

            def group(self, k, u):
                return self.U * k + u

            def turn(self, k, u, depth=2):
                return (self.U // depth) * k + u // depth

            def pool_gather(self, pool, got_used, company=None):
                def step(k, u):
                    g, s = self.group(k, u), u % self.AHEAD
                    pool.wait_ge(got_used, g + 1)
                    pool.sem_inc(self.pace, 1)
                    nc.gpsimd.tensor_copy(self.idx[:, s, :], self.t["node_rows"][:, bass.ds(g * GN, GN), 0]).then_inc(self.staged, 1)
                    pool.wait_ge(self.staged, g + 1)
                    pool.sem_inc(self.pace, 1)
                    for j in range(GN):
                        nc.gpsimd.indirect_dma_start(
                            out=self.got[:, s, j, :], out_offset=None, in_=sums[:, :],
                            in_offset=bass.IndirectOffsetOnAxis(ap=self.idx[:, s, j:j + 1], axis=0)).then_inc(self.landed[s], 16)
                in_slots(pool, NG, [(step, 0)] + ([company] if company else []), self.U)

            def wait_got(self, dve, k, u):
                dve.wait_ge(self.landed[u % self.AHEAD], 16 * GN * (self.turn(k, u, self.AHEAD) + 1))

            def sp_moves(self, sp, load_lag, store_lag):
                def load(n):
                    array, depth, used = self.loads[n]

                    def step(k, u):
                        g, b = self.group(k, u), u % depth
                        sp.wait_ge(used, g + 1)
                        sp.dma_start(self.tile[n][:, b, :, :],
                                     array.rearrange("(p t) c -> p t c", p=P)[:, bass.ds(g * GN, GN), :]).then_inc(self.in_landed[n][b], 16)
                    return step

                def store(n):
                    def step(k, u):
                        g, b = self.group(k, u), u % 2
                        ready, start = self.full[n]
                        sp.wait_ge(ready, g + 1 + start)
                        sp.dma_start(self.stores[n].rearrange("(p t) c -> p t c", p=P)[:, bass.ds(g * GN, GN), :],
                                     self.tile[n][:, b, :, 0:D]).then_inc(self.stored[n][b], 16)
                    return step

                in_slots(sp, NG, [(load(n), load_lag.get(n, 0)) for n in self.loads] + [(store(n), store_lag[n]) for n in self.stores], self.U)
                for n in self.stores:
                    for b in range(2):
                        sp.wait_ge(self.stored[n][b], 16 * (NG // 2))

            def wait_in(self, eng, n, k, u):
                d = self.loads[n][1]
                eng.wait_ge(self.in_landed[n][u % d], 16 * (self.turn(k, u, d) + 1))

            def wait_stored(self, eng, n, k, u):
                if reused(self.turn(k, u)):
                    eng.wait_ge(self.stored[n][u % 2], 16 * self.turn(k, u))

            def norm(self, name, src, dst):
                ph, tag = self.ph, name
                n = {"src": src, "dst": dst,
                     "stats": ph.sb(f"{tag}_stats", [P, 2, GN, 6]), "mv": ph.sb(f"{tag}_mv", [P, 2, GN, 2]),
                     "sd": ph.sb(f"{tag}_sd", [P, 2, GN]), "rs": ph.sb(f"{tag}_rs", [P, 2, GN]), "nm": ph.sb(f"{tag}_nm", [P, 2, GN])}
                for x in ("stat_steps", "measured", "rooted", "factors", "factor_steps", "normed", "paced"):
                    n[x] = ph.sem(f"{tag}_{x}")
                return n

            def norm_stats(self, dve, n, k, u):
                g, s = self.group(k, u), u % 2
                st = Steps(dve, n["stat_steps"], GN * g)
                for j in range(GN):
                    st.mark(nc.vector.bn_stats(n["stats"][:, s, j, :], n["src"][:, s, j, :]))
                st.ready()
                dve.sem_inc(n["paced"], 1)
                for j in range(GN):
                    last = nc.vector.bn_aggr(n["mv"][:, s, j, :], n["stats"][:, s, j, :])
                    if j == GN - 1:
                        last.then_inc(n["measured"], 1)

            def norm_root(self, act, n, k, u):
                g, s = self.group(k, u), u % 2
                act.wait_ge(n["measured"], g + 1)
                nc.scalar.activation(n["sd"][:, s, :], n["mv"][:, s, :, 1], ACT.Sqrt, bias=eps[:, :]).then_inc(n["rooted"], 1)

            def norm_factors(self, dve, n, k, u):
                g, s = self.group(k, u), u % 2
                dve.wait_ge(n["rooted"], g + 1)
                st = Steps(dve, n["factor_steps"], g)
                st.then(nc.vector.reciprocal(n["rs"][:, s, :], n["sd"][:, s, :]))
                nc.vector.scalar_tensor_tensor(n["nm"][:, s, :], n["mv"][:, s, :, 0], -1.0, n["rs"][:, s, :],
                                               ALU.mult, ALU.mult).then_inc(n["factors"], 1)

            def norm_apply(self, act, n, k, u):
                g, s = self.group(k, u), u % 2
                act.wait_ge(n["factors"], g + 1)
                for j in range(GN):
                    last = nc.scalar.activation(n["dst"][:, s, j, :], n["src"][:, s, j, :], ACT.Identity,
                                                bias=n["nm"][:, s, j:j + 1], scale=n["rs"][:, s, j:j + 1])
                    if j == GN - 1:
                        last.then_inc(n["normed"], 1)

        def store_scores(sp, tab, ready, stored):
            sp.wait_ge(ready, NG)
            sp.dma_start(scores.rearrange("(p t) c -> p t c", p=P), tab[:, :, :]).then_inc(stored, 16)
            sp.wait_ge(stored, 16)

        def later(k, g):
            return not isinstance(k, int) or g >= 2

        def mlp_pass(fields):
            with phase("mlp") as ph:
                (z_steps, z_full, z_turned, z_hi, z_flat, made1, relu_done, h_hi, h_flat, made2, r_full, split, half_made,
                 act_pace,
                 x_turned, x_flat, score_made, scored, tab_stored) = (ph.sem(n) for n in (
                     "z_steps", "z_full", "z_turned", "z_hi", "z_flat", "made1", "relu_done", "h_hi", "h_flat", "made2", "r_full", "split", "half_made",
                     "act_pace",
                     "x_turned", "x_flat", "score_made", "scored", "tab_stored"))
                np_ = NodePass(ph, SRC, {"x": (a["x"], 4, r_full)}, {"x1": x1})
                x, o1, r = np_.tile["x"], np_.tile["x1"], np_.r
                z = ph.sb("z", [P, 2, GN, D])
                zt_hi, zt_lo, ht_hi, ht_lo = (ph.sb(n, [P, 2, GN * P], F32R) for n in ("zt_hi", "zt_lo", "ht_hi", "ht_lo"))
                ht, xt = ph.sb("ht", [P, 2, GN * P]), ph.sb("xt", [P, 2, GN * P])
                parts = {n: ph.sb(n, [P, 2, D], F32R) for n in ("ww1_hi", "ww1_lo", "w2_hi", "w2_lo")}
                dd = ph.sb("dd", [P, 2, GN])
                score_tab = ph.sb("score_tab", [P, NT, AUX])
                ps_z, ps_1, ps_2, ps_x = (ph.ps(n, [P, 2, GN * P]) for n in ("ps_z", "ps_1", "ps_2", "ps_x"))
                ln = np_.norm("ln", r, o1)
                np_.full["x1"] = (ln["normed"], 0)
                cols = ET // NG
                fetch_step, fetch_end = side_fetch(ph, "fields", edge_fields[:, :], 16, order[DST]["edge_idx"], fields, cols, NG, np_.U)
                tabulate_begin, tabulate_step, tabulate_end = tabulate(ph, DST, cols, NG, np_.U)
                block = ph.block()

                @block.gpsimd
                def _(pool):
                    def company(k, u):
                        fetch_step(pool, k, u)
                        tabulate_step(pool, k, u)

                    tabulate_begin(pool)
                    np_.pool_gather(pool, z_full, (company, 0))
                    fetch_end(pool)
                    tabulate_end(pool)

                @block.sync
                def _(sp):
                    np_.sp_moves(sp, {}, {"x1": 6})
                    store_scores(sp, score_tab, scored, tab_stored)

                @block.tensor
                def _(pe):
                    def turn_z(k, u):
                        g, s = np_.group(k, u), u % 2
                        pe.wait_ge(z_full, g + 5)
                        pe.wait_ge(z_flat, g + 1)
                        for j in range(GN):
                            for c in range(2):
                                last = nc.tensor.transpose(ps_z[:, c, j * P:(j + 1) * P], z[:, s, j, c * P:(c + 1) * P], ident[:, :])
                        last.then_inc(z_turned, 1)

                    def second(k, u):
                        g = np_.group(k, u)
                        pe.wait_ge(h_flat, g + 1)
                        pe.wait_ge(r_full, g + 4)
                        for j in range(GN):
                            dst = ps_2[:, j // 2, (j % 2) * D:(j % 2 + 1) * D]
                            nc.tensor.matmul(dst, ones3[:, :], bias3["b2"][:, 0:D], start=True, stop=False)
                            for h, w in ((ht_lo, "w2_hi"), (ht_hi, "w2_lo"), (ht_hi, "w2_hi")):
                                for c in range(2):
                                    last = nc.tensor.matmul(dst, h[:, c, j * P:(j + 1) * P], parts[w][:, c, :],
                                                            start=False, stop=(c == 1 and h is ht_hi and w == "w2_hi"))
                        last.then_inc(made2, 1)

                    def first(k, u):
                        g = np_.group(k, u)
                        pe.wait_ge(z_flat, g + 2)
                        pe.wait_ge(relu_done, g)
                        for m in range(2):
                            for x, w in ((zt_lo, "ww1_hi"), (zt_hi, "ww1_lo"), (zt_hi, "ww1_hi")):
                                for c in range(2):
                                    last = nc.tensor.matmul(ps_1[:, m, :], parts[w][:, c, m * P:(m + 1) * P], x[:, c, :],
                                                            start=(c == 0 and x is zt_lo), stop=(c == 1 and x is zt_hi and w == "ww1_hi"))
                            if m == 0:
                                last.then_inc(half_made, 1)
                        last.then_inc(made1, 1)

                    def score(k, u):
                        g = np_.group(k, u)
                        pe.wait_ge(x_flat, g + 1)
                        for j in range(GN):
                            for c in range(2):
                                last = nc.tensor.matmul(ps_x[:, 0, j * AUX:(j + 1) * AUX], xt[:, c, j * P:(j + 1) * P], v_t[:, c, :],
                                                        start=c == 0, stop=c == 1)
                        last.then_inc(score_made, 1)

                    def turn_x(k, u):
                        g, s = np_.group(k, u), u % 2
                        pe.wait_ge(ln["normed"], g + 1)
                        pe.wait_ge(scored, g)
                        for j in range(GN):
                            for c in range(2):
                                last = nc.tensor.transpose(ps_x[:, c, j * P:(j + 1) * P], o1[:, s, j, c * P:(c + 1) * P], ident[:, :])
                        last.then_inc(x_turned, 1)

                    pe.wait_ge(split, 4)
                    in_slots(pe, NG, [(score, 5), (turn_z, 1), (turn_x, 4), (second, 2), (first, 1)], np_.U)

                @block.scalar
                def _(act):
                    def round_z(k, u):
                        g = np_.group(k, u)
                        act.wait_ge(z_turned, g + 1)
                        if later(k, g + 1):
                            act.wait_ge(made1, g)
                        nc.scalar.activation(zt_hi[:, :, :], ps_z[:, :, :], ACT.Copy).then_inc(z_hi, 1)

                    def flat_x(k, u):
                        g = np_.group(k, u)
                        act.wait_ge(x_turned, g + 1)
                        if later(k, g + 1):
                            act.wait_ge(score_made, g)
                        nc.scalar.activation(xt[:, :, :], ps_x[:, :, :], ACT.Copy).then_inc(x_flat, 1)

                    def relu(k, u):
                        g = np_.group(k, u)
                        if later(k, g + 1):
                            act.wait_ge(made2, g)
                            act.wait_ge(h_flat, g)
                        for m in range(2):
                            act.wait_ge((half_made, made1)[m], g + 1)
                            last = nc.scalar.activation(ht[:, m, :], ps_1[:, m, :], ACT.Relu, bias=mlp_bias[:, m:m + 1])
                        last.then_inc(relu_done, 1)
                        act.wait_ge(relu_done, g + 1)
                        act.sem_inc(act_pace, 1)
                        nc.scalar.activation(ht_hi[:, :, :], ht[:, :, :], ACT.Copy).then_inc(h_hi, 1)

                    def root(k, u):
                        np_.norm_root(act, ln, k, u)

                    def apply(k, u):
                        g = np_.group(k, u)
                        np_.wait_stored(act, "x1", k, u)
                        if later(k, g):
                            act.wait_ge(x_turned, g - 1)
                        np_.norm_apply(act, ln, k, u)

                    in_slots(act, NG, [(root, 3), (round_z, 1), (flat_x, 4), (apply, 3), (relu, 1)], np_.U)

                @block.vector
                def _(dve):
                    dve.sem_inc(z_full, np_.AHEAD)
                    dve.sem_inc(r_full, 4)
                    dve.sem_inc(z_flat, 1)
                    for n, w in (("ww1", ww1), ("w2", w2)):
                        nc.vector.tensor_copy(parts[n + "_hi"][:, :, :], w[:, :, :]).then_inc(split, 1)
                    dve.wait_ge(split, 2)
                    for n, w in (("ww1", ww1), ("w2", w2)):
                        nc.vector.tensor_tensor(parts[n + "_lo"][:, :, :], w[:, :, :], parts[n + "_hi"][:, :, :].bitcast(F32),
                                                ALU.subtract).then_inc(split, 1)

                    def mix(k, u):
                        g, s = np_.group(k, u), u % 2
                        np_.wait_got(dve, k, u)
                        np_.wait_in(dve, "x", k, u)
                        if later(k, g):
                            dve.wait_ge(z_turned, g - 1)
                        st = Steps(dve, z_steps, g)
                        st.then(nc.vector.tensor_tensor(dd[:, s, :], np_.got[:, u % 4, :, D + 4], np_.got[:, u % 4, :, D + 4], ALU.mult))
                        for j in range(GN):
                            last = nc.vector.scalar_tensor_tensor(z[:, s, j, :], x[:, u % 4, j, :], dd[:, s, j:j + 1],
                                                                  np_.got[:, u % 4, j, 0:D], ALU.mult, ALU.add)
                        last.then_inc(z_full, 1)

                    def residual(k, u):
                        g, s = np_.group(k, u), u % 2
                        dve.wait_ge(made2, g + 1)
                        if later(k, g):
                            dve.wait_ge(ln["normed"], g - 1)
                        nc.vector.tensor_tensor(r[:, s, :, :].rearrange("p (a b) c -> p a (b c)", a=2), ps_2[:, :, :],
                                                x[:, u % 4, :, :].rearrange("p (a b) c -> p a (b c)", a=2), ALU.add).then_inc(r_full, 1)
                        dve.wait_ge(r_full, g + 5)
                        np_.norm_stats(dve, ln, k, u)

                    def rest_of_z(k, u):
                        g = np_.group(k, u)
                        dve.wait_ge(z_hi, g + 1)
                        nc.vector.tensor_tensor(zt_lo[:, :, :], ps_z[:, :, :], zt_hi[:, :, :].bitcast(F32), ALU.subtract).then_inc(z_flat, 1)

                    def rest_of_h(k, u):
                        g = np_.group(k, u)
                        dve.wait_ge(h_hi, g + 1)
                        nc.vector.tensor_tensor(ht_lo[:, :, :], ht[:, :, :], ht_hi[:, :, :].bitcast(F32), ALU.subtract).then_inc(h_flat, 1)

                    def factors(k, u):
                        np_.norm_factors(dve, ln, k, u)

                    def take_scores(k, u):
                        g = np_.group(k, u)
                        dve.wait_ge(score_made, g + 1)
                        nc.vector.tensor_copy(score_tab[:, bass.ds(g * GN, GN), :],
                                              ps_x[:, 0, 0:GN * AUX].rearrange("p (j h) -> p j h", h=AUX)).then_inc(scored, 1)

                    in_slots(dve, NG, [(rest_of_z, 1), (factors, 3), (mix, 0), (residual, 2), (take_scores, 4), (rest_of_h, 1)], np_.U)

        def layer_pass(name, kind, loads, stores, weight, bias):
            with phase(name) as ph:
                (pre_steps, pre_done, turned, flat, made, taken, scored, sum_done, tab_stored) = (
                    ph.sem(n) for n in ("pre_steps", "pre_done", "turned", "flat", "made", "taken", "scored", "sum_done", "tab_stored"))
                gat, tail = kind in ("gat_in", "gat_mid"), kind == "gcn_out"
                gcn = kind in ("gcn_mid", "gcn_out")
                ins = {n: (array, NodePass.AHEAD, pre_done) for n, array in loads.items()}
                if tail:
                    ins["x3"] = (loads["x3"], 4, sum_done)
                h_name = next((n for n in stores if n.startswith("h")), None)
                np_ = NodePass(ph, DST, ins, stores, (h_name,) if gat else ())
                r, got, tile = np_.r, np_.got, np_.tile
                vt = ph.sb("vt", [P, 2, 2, GN * P])
                in_parts = kind == "gat_mid"
                if in_parts:
                    v_hi, v_lo = ph.sb("v_hi", [P, 2, 2, GN * P], F32R), ph.sb("v_lo", [P, 2, 2, GN * P], F32R)
                    w_hi, w_lo = ph.sb("w_hi", [P, 2, RW], F32R), ph.sb("w_lo", [P, 2, RW], F32R)
                    rounded, v_split, w_split = ph.sem("rounded"), ph.sem("v_split"), ph.sem("w_split")
                y = ph.sb("y", [P, 2, GN, D]) if kind in ("gat_out", "gcn_mid") else None
                score_tab = ph.sb("score_tab", [P, NT, AUX]) if gat else None
                dis_tab = ph.sb("dis_tab", [P, NT]) if not gat else None
                ps_t = [ph.ps(f"ps_t{b}", [P, 2, GN * P]) for b in range(2)]
                ps_h = ph.ps("ps_h", [P, 4, 512])
                width = RW if gat else D
                norms, lag = [], 0
                operand = r
                if kind == "gat_in":
                    norms = [(np_.norm("ln", r, tile["x2"]), 1)]
                elif kind == "gat_out":
                    norms = [(np_.norm("ln1", r, tile["x3"]), 1), (np_.norm("ln2", tile["x3"], y), 3)]
                elif kind == "gcn_mid":
                    norms = [(np_.norm("ln", tile["x4"], y), 1)]
                if norms:
                    operand, lag = norms[-1][0]["dst"], norms[-1][1]
                    np_.full = {"x2": (norms[0][0]["normed"], 0), "x3": (norms[0][0]["normed"], 0), "x4": (pre_done, NodePass.AHEAD)}
                if tail:
                    r2 = ph.sb("r2", [P, 2, GN, D])
                    out_norm = np_.norm("out_ln", r2, tile["out"])
                    np_.full["out"] = (out_norm["normed"], 0)
                h_full = ph.sem("h_full")
                helped = {"gat_out": "x2", "gcn_out": "h"}.get(kind)
                helped_done = ph.sem("helped_done")
                np_.full[h_name] = (h_full, 0)
                turn_lag, flat_lag, product_lag = lag + 1, lag + 2, lag + 3
                block = ph.block()

                @block.gpsimd
                def _(pool):
                    def add_rows(k, u):
                        g, b = np_.group(k, u), u % np_.AHEAD
                        np_.wait_got(pool, k, u)
                        np_.wait_in(pool, helped, k, u)
                        pool.sem_inc(np_.pace, 1)
                        nc.gpsimd.tensor_tensor(got[:, b, :, 0:D], got[:, b, :, 0:D], tile[helped][:, b, :, :], ALU.add).then_inc(helped_done, 1)

                    np_.pool_gather(pool, pre_done, (add_rows, 1) if helped else None)

                @block.sync
                def _(sp):
                    np_.sp_moves(sp, {"x3": 2} if tail else {}, {n: product_lag + 3 if n == h_name else product_lag + 4 if n == "out" else 4 for n in stores})
                    if gat:
                        store_scores(sp, score_tab, scored, tab_stored)

                @block.tensor
                def _(pe):
                    def turn(k, u):
                        g, s = np_.group(k, u), u % 2
                        if norms:
                            pe.wait_ge(norms[-1][0]["normed"], g + 1)
                        else:
                            pe.wait_ge(pre_done, g + 1 + np_.AHEAD)
                        if later(k, g):
                            pe.wait_ge(flat, g - 1)
                        for j in range(GN):
                            for c in range(2):
                                last = nc.tensor.transpose(ps_t[s][:, c, j * P:(j + 1) * P], operand[:, s, j, c * P:(c + 1) * P], ident[:, :])
                        last.then_inc(turned, 1)

                    def product(k, u):
                        g, s = np_.group(k, u), u % 2
                        pe.wait_ge(v_split if in_parts else flat, g + 1)
                        for j in range(GN):
                            pe.wait_ge(taken, g * GN + j + 1)
                            nc.tensor.matmul(ps_h[:, j, 0:width], ones3[:, :], bias3[bias][:, 0:width], start=True, stop=False)
                            pairs = [(v_lo, w_hi), (v_hi, w_lo), (v_hi, w_hi)] if in_parts else [(vt, weight)]
                            for n, (v, w) in enumerate(pairs):
                                for c in range(2):
                                    last = nc.tensor.matmul(ps_h[:, j, 0:width], v[:, s, c, j * P:(j + 1) * P], w[:, c, 0:width],
                                                            start=False, stop=c == 1 and n == len(pairs) - 1)
                            last.then_inc(made, 1)

                    if in_parts:
                        pe.wait_ge(w_split, 2)
                    in_slots(pe, NG, [(product, product_lag), (turn, turn_lag)], np_.U)

                @block.scalar
                def _(act):
                    if not tail:
                        act.sem_inc(taken, GN)

                    def flatten(k, u):
                        g, s = np_.group(k, u), u % 2
                        act.wait_ge(turned, g + 1)
                        if later(k, g):
                            act.wait_ge(made, GN * (g - 1))
                            if in_parts:
                                act.wait_ge(v_split, g - 1)
                        nc.scalar.activation(vt[:, s, :, :], ps_t[s][:, :, :], ACT.Relu if kind == "gat_mid" else ACT.Copy).then_inc(flat, 1)
                        if in_parts:
                            act.wait_ge(flat, g + 1)
                            act.sem_inc(np_.pace, 1)
                            nc.scalar.activation(v_hi[:, s, :, :], vt[:, s, :, :], ACT.Copy).then_inc(rounded, 1)

                    def root(n):
                        return lambda k, u: np_.norm_root(act, n, k, u)

                    def apply(n):
                        def step(k, u):
                            g = np_.group(k, u)
                            stored_name = next((x for x in stores if tile[x] is n["dst"]), None)
                            if stored_name:
                                np_.wait_stored(act, stored_name, k, u)
                            if later(k, g):
                                if n["dst"] is operand:
                                    act.wait_ge(turned, g - 1)
                                elif not tail:
                                    act.wait_ge(norms[1][0]["normed"], g - 1)
                            np_.norm_apply(act, n, k, u)
                        return step

                    def take(k, u):
                        g, s = np_.group(k, u), u % 2
                        np_.wait_stored(act, h_name, k, u)
                        if gat and later(k, g):
                            act.wait_ge(scored, g - 1)
                        for j in range(GN):
                            act.wait_ge(made, g * GN + j + 1)
                            if gat:
                                nc.scalar.activation(tile[h_name][:, s, j, :], ps_h[:, j, 0:RW], ACT.Copy).then_inc(taken, 1)
                            else:
                                nc.scalar.activation(tile[h_name][:, s, j, :], ps_h[:, j, 0:D], ACT.Copy,
                                                     scale=dis_tab[:, bass.ds(g * GN + j, 1)]).then_inc(taken, 1)
                        act.wait_ge(taken, GN * (g + 2))
                        act.sem_inc(h_full, 1)

                    steps = [(root(n), l) for n, l in norms] + [(flatten, flat_lag)]
                    if tail:
                        steps += [(root(out_norm), product_lag + 1), (apply(out_norm), product_lag + 1)]
                    for n, l in reversed(norms):
                        steps += [(apply(n), l)]
                    if not tail:
                        steps += [(take, product_lag)]
                    in_slots(act, NG, steps, np_.U)

                @block.vector
                def _(dve):
                    dve.sem_inc(pre_done, np_.AHEAD)
                    if in_parts:
                        nc.vector.tensor_copy(w_hi[:, :, :], weight[:, :, :]).then_inc(w_split, 1)
                        dve.wait_ge(w_split, 1)
                        nc.vector.tensor_tensor(w_lo[:, :, :], weight[:, :, :], w_hi[:, :, :].bitcast(F32), ALU.subtract).then_inc(w_split, 1)
                    if tail:
                        dve.sem_inc(sum_done, 4)
                        dve.sem_inc(taken, GN)

                    def pre(k, u):
                        g, s, b = np_.group(k, u), u % 2, u % np_.AHEAD
                        if helped:
                            dve.wait_ge(helped_done, g + 1)
                        else:
                            np_.wait_got(dve, k, u)
                        for n in loads:
                            if n != helped and not (tail and n == "x3"):
                                np_.wait_in(dve, n, k, u)
                        dst = tile["x4"] if kind == "gcn_mid" else r
                        if kind == "gcn_mid":
                            np_.wait_stored(dve, "x4", k, u)
                        if later(k, g):
                            dve.wait_ge(norms[0][0]["normed"] if norms else turned, g - 1)
                        g_rows, extras = got[:, b, :, 0:D], got[:, b, :, D:RW]
                        if kind == "gat_in":
                            nc.vector.tensor_tensor(r[:, s, :, :], g_rows, tile["x1"][:, b, :, :], ALU.add).then_inc(pre_done, 1)
                        elif kind in ("gat_mid", "gat_out"):
                            count = 1 if kind == "gat_mid" else 2
                            st = Steps(dve, pre_steps, g * count)
                            st.then(nc.vector.tensor_tensor(r[:, s, :, :].rearrange("p j (h c) -> p j h c", h=4),
                                                            tile["h"][:, b, :, :].rearrange("p j (h c) -> p j h c", h=4),
                                                            extras[:, :, 0:4, None].broadcast_to([P, GN, 4, D // 4]), ALU.mult))
                            if kind == "gat_out":
                                st.mark(nc.vector.tensor_copy(dis_tab[:, bass.ds(g * GN, GN)], extras[:, :, 4]))
                            nc.vector.tensor_tensor(r[:, s, :, :], r[:, s, :, :], g_rows, ALU.add).then_inc(pre_done, 1)
                        else:
                            st = Steps(dve, pre_steps, g * ((1 if tail else 2) + GN))
                            b_all = b6_all if kind == "gcn_mid" else b7_all
                            st.mark(nc.vector.tensor_copy(dis_tab[:, bass.ds(g * GN, GN)], extras[:, :, 4]))
                            total = g_rows
                            if not tail:
                                st.then(nc.vector.tensor_tensor(r[:, s, :, :], tile["h"][:, b, :, :], g_rows, ALU.add))
                                total = r[:, s, :, :]
                            for j in range(GN):
                                st.mark(nc.vector.scalar_tensor_tensor(r[:, s, j, :], total[:, j, :], extras[:, j, 4:5], b_all[:, :], ALU.mult, ALU.add))
                            st.ready()
                            nc.vector.scalar_tensor_tensor(dst[:, s, :, :], r[:, s, :, :], 0.0, tile["x3" if kind == "gcn_mid" else "x4"][:, b, :, :],
                                                           ALU.max, ALU.add).then_inc(pre_done, 1)
                        if norms:
                            dve.wait_ge(pre_done, g + 1 + np_.AHEAD)
                            np_.norm_stats(dve, norms[0][0], k, u)

                    def factors(n):
                        return lambda k, u: np_.norm_factors(dve, n, k, u)

                    def stats2(k, u):
                        g = np_.group(k, u)
                        dve.wait_ge(norms[0][0]["normed"], g + 1)
                        np_.norm_stats(dve, norms[1][0], k, u)

                    def take_scores(k, u):
                        g, s = np_.group(k, u), u % 2
                        dve.wait_ge(taken, GN * (g + 2))
                        nc.vector.tensor_copy(score_tab[:, bass.ds(g * GN, GN), :], tile[h_name][:, s, :, D:RW]).then_inc(scored, 1)

                    def rest(k, u):
                        g, s = np_.group(k, u), u % 2
                        dve.wait_ge(rounded, g + 1)
                        nc.vector.tensor_tensor(v_lo[:, s, :, :], vt[:, s, :, :], v_hi[:, s, :, :].bitcast(F32), ALU.subtract).then_inc(v_split, 1)

                    def last_sum(k, u):
                        g, s = np_.group(k, u), u % 2
                        np_.wait_in(dve, "x3", k, u)
                        if later(k, g):
                            dve.wait_ge(out_norm["normed"], g - 1)
                        for j in range(GN):
                            dve.wait_ge(made, GN * g + j + 1)
                            nc.vector.tensor_tensor(r2[:, s, j, :], ps_h[:, j, 0:D], tile["x3"][:, u % 4, j, :], ALU.add).then_inc(taken, 1)
                        dve.wait_ge(taken, GN * (g + 2))
                        dve.sem_inc(sum_done, 1)
                        np_.norm_stats(dve, out_norm, k, u)

                    steps = [(stats2, 2)] if len(norms) == 2 else []
                    steps += [(factors(n), l) for n, l in norms]
                    steps += [(pre, 0)]
                    if in_parts:
                        steps += [(rest, flat_lag)]
                    if tail:
                        steps += [(factors(out_norm), product_lag + 1)]
                    if gat:
                        steps += [(take_scores, product_lag + 1)]
                    if tail:
                        steps += [(last_sum, product_lag)]
                    in_slots(dve, NG, steps, np_.U)

        sort()
        marks()
        dst, src = order
        with phase("s_fields") as ph:
            got = ph.sb("got", [P, ET, 4], I32)
            extra = ph.sb("extra", [P, ET, 2], I32)
            prepare(got)
            degrees(SRC, got, 0, 1)
            scatter_nodes(SRC)
            fetch_small("fetch_deg", [(node_tab[SRC][:, :], 2, src["gather_idx"], extra)])
            scale_weights(extra)
        sum_edges("sum0", SRC, a["x"][:, :], True, src["weight"], 0, None)
        with phase("d_fields") as ph:
            got = ph.sb("got", [P, ET, 16], I32)
            mlp_pass(got)
            degrees(DST, got, 8, 9)
        with phase("gat1") as ph:
            w = ph.sb("w", [P, 8, ET])
            eh, et = ph.sb("eh", [P, ET, AUX]), ph.sb("et", [P, ET, AUX])
            project_edges(eh, et)
            attention("att1", 8, w, [eh, edge_term, et], None, False)
            sum_edges("sum1", DST, ft_edges, False, w, 8, a["L1_bias"].rearrange("(a n) -> a n", a=1))
        layer_pass("gat_in", "gat_in", {"x1": x1}, {"x2": x2, "h_out": h2a}, wa, "a")

        def self_loop_gat(name, h):
            with phase(name) as ph:
                w = ph.sb("w", [P, 4, ET])
                from_src, own = ph.sb("from_src", [P, ET, AUX]), ph.sb("own", [P, ET, AUX])
                fetch_small(f"{name}_f", [(scores[:, :], AUX, dst["gather_idx"], from_src),
                                          (scores[:, :], AUX, dst["own_idx"], own)])
                attention(f"{name}_a", 4, w, [from_src[:, :, 0:4], own[:, :, 4:8]], [own[:, :, 0:4], own[:, :, 4:8]], True)
                sum_edges(f"{name}_s", DST, h[:, :], True, w, 4, a["zero_row"])

        self_loop_gat("gat2", h2a)
        layer_pass("gat_mid", "gat_mid", {"h": h2a}, {"h_out": h2b}, wb, "b")
        self_loop_gat("gat3", h2b)
        layer_pass("gat_out", "gat_out", {"h": h2b, "x2": x2}, {"x3": x3, "h_out": h3a}, w6, "c6")
        sum_edges("sum4", DST, h3a[:, :], True, dst["weight"], 0, a["zero_row"])
        layer_pass("gcn_mid", "gcn_mid", {"h": h3a, "x3": x3}, {"x4": x4, "h_out": h3b}, w7, "c7")
        sum_edges("sum5", DST, h3b[:, :], True, dst["weight"], 0, a["zero_row"])
        layer_pass("gcn_out", "gcn_out", {"h": h3b, "x4": x4, "x3": x3}, {"out": out}, wp, "bp")


def sort_signs():
    i = np.arange(P)[:, None] * SW + np.arange(SW)[None, :]
    s = [1.0 - 2.0 * ((i >> k) & 1) for k in range(LOG + 1)]
    return np.stack([s[1]] + [s[k] * s[k + 1] for k in range(1, LOG)], axis=1).astype(np.float32)


def kernel(**inputs):
    import numpy as _np
    import concourse.bacc as _bacc
    from concourse.bass_utils import run_bass_kernel_spmd as _run

    def rows(x, n):
        x = _np.asarray(x)
        return _np.concatenate([x, _np.zeros((n - x.shape[0],) + x.shape[1:], x.dtype)])

    def column(x):
        return x.reshape(2, P).T

    g = {k: _np.ascontiguousarray(v) for k, v in inputs.items()}
    arrays = {
        "x": rows(g["x"], NP),
        "src": rows(g["src"], EP), "dst": rows(g["dst"], EP), "edge_weight": rows(g["edge_weight"], EP),
        "edge_attr_pairs": _np.ascontiguousarray(
            rows(g["edge_attr_64"], EP).reshape(P, ET // 2, 2, 64).transpose(2, 3, 1, 0).reshape(P, ET // 2, P)),
        "L0_Wt": g["L0_gnn_W"].T, "L0_W1": g["L0_gnn_W1"], "L0_W2": g["L0_gnn_W2"],
        "L0_b": column(g["L0_gnn_b"]), "L0_b1": column(g["L0_gnn_b1"]), "L0_b2": g["L0_gnn_b2"],
        "L1_W_fc": g["L1_gnn_W_fc"], "L1_W_e": g["L1_gnn_W_e"],
        "L1_attn_h": g["L1_gnn_attn_h"].reshape(-1), "L1_attn_e": g["L1_gnn_attn_e"].reshape(-1),
        "L1_attn_t": g["L1_gnn_attn_t"].reshape(-1), "L1_bias": g["L1_gnn_bias"].reshape(-1),
        "L2_W1": g["L2_gnn_W1"], "L2_att_src1": g["L2_gnn_att_src1"].reshape(-1), "L2_att_dst1": g["L2_gnn_att_dst1"].reshape(-1),
        "L2_b1": g["L2_gnn_b1"], "L2_W2": g["L2_gnn_W2"], "L2_att_src2": g["L2_gnn_att_src2"].reshape(-1),
        "L2_att_dst2": g["L2_gnn_att_dst2"].reshape(-1), "L2_b2": g["L2_gnn_b2"],
        "L3_ln6_g": column(g["L3_gnn_ln6_g"]), "L3_ln6_b": column(g["L3_gnn_ln6_b"]), "L3_W6t": g["L3_gnn_W6"].T, "L3_b6": g["L3_gnn_b6"],
        "L3_ln7_g": column(g["L3_gnn_ln7_g"]), "L3_ln7_b": column(g["L3_gnn_ln7_b"]), "L3_W7t": g["L3_gnn_W7"].T, "L3_b7": g["L3_gnn_b7"],
        "L3_Wpt": g["L3_gnn_Wp"].T, "L3_bp": g["L3_gnn_bp"],
        "ident": _np.eye(P, dtype=_np.float32),
        "before": _np.triu(_np.ones((P, P), _np.float32), 1),
        "zero_row": _np.zeros((1, D), _np.float32),
        "sort_signs": sort_signs(),
    }
    nc = _bacc.Bacc("TRN2", target_bir_lowering=False, num_devices=1)
    aps, data = {}, {}
    for name, v in arrays.items():
        data[f"in_{name}"] = _np.ascontiguousarray(v)
        aps[name] = nc.dram_tensor(f"in_{name}", v.shape, mybir.dt.from_np(v.dtype), kind="ExternalInput").ap()
    out = nc.dram_tensor("out_0", (NP, D), F32, kind="ExternalOutput").ap()
    build(nc, aps, out)
    r = _run(nc, [data], core_ids=[0])
    return r.results[0]["out_0"][:N_NODES]
```
